# Optimizing a Trainium2 kernel written in Bass

```python
import numpy as np
import jax
import jax.numpy as jnp

def _softmax(x, axis=-1):
    return jax.nn.softmax(x, axis=axis)

def _gelu(x):
    return jax.nn.gelu(x, approximate=True)

def _silu(x):
    return jax.nn.silu(x)

def _sigmoid(x):
    return jax.nn.sigmoid(x)

def _layernorm(x, axis=-1, eps=1e-05):
    m = jnp.mean(x, axis=axis, keepdims=True)
    v = jnp.var(x, axis=axis, keepdims=True)
    return (x - m) / jnp.sqrt(v + eps)

def _scatter_add(tgt, idx, src, axis=0):
    return tgt.at[idx].add(src)

def _segment_sum(src, seg, n):
    return jax.ops.segment_sum(src, seg, n)
kernel_name = 'mk_decoder_preln_d2_seqx_r8_3ff1eb'

def setup_inputs(seed: int=0):
    np.random.seed(seed)
    _w = jnp.asarray

    def _rec_inputs():
        import jax
        import jax.numpy as jnp
        _rk = jax.random.key(seed)
        x = -0.0002928 + 1 * jax.random.normal(jax.random.fold_in(_rk, 1), (8, 128, 128), jnp.float32)
        _lenS = 128 - jax.random.randint(jax.random.fold_in(_rk, 7), (8,), 0, max(1, 128 // 4) + 1, jnp.int32)
        _lenS2 = 128 - jax.random.randint(jax.random.fold_in(_rk, 8), (8,), 0, max(1, 128 // 4) + 1, jnp.int32)
        _ctx_1024P = jax.random.normal(jax.random.fold_in(_rk, 11), (8, 16, 128), jnp.float32)
        _ctx_1024c = jax.random.dirichlet(jax.random.fold_in(_rk, 511), 0.3 * jnp.ones((16,), jnp.float32), (8, 128))
        _ctx_1024t = jnp.einsum('bsk,bkd->bsd', _ctx_1024c, _ctx_1024P)
        _ctx_1024t = _ctx_1024t * jax.lax.rsqrt(jnp.mean(jnp.square(_ctx_1024t)) + 1e-12) * 0.953939
        ctx_1024 = -1.39393e-06 + 0.999914 * (_ctx_1024t + 0.3 * jax.random.normal(jax.random.fold_in(_rk, 611), (8, 128, 128), jnp.float32))
        return (x, ctx_1024)
    x, ctx_1024 = _rec_inputs()

    def _L0_attn_setup():
        import jax, jax.numpy as jnp
        import numpy as np
        D_MODEL = 128
        N_HEADS = 16
        FEAT_DIM = 16
        V_DIM = 64
        EPS = 1e-12

        def taylor_exp(x):
            d = x.shape[-1]
            rd = jnp.sqrt(jnp.float32(d))
            rrd = jnp.sqrt(rd)
            r2 = jnp.sqrt(jnp.float32(2.0))
            x2 = (x[..., :, None] * x[..., None, :]).reshape(*x.shape[:-1], d * d) / r2
            ones = jnp.ones(x.shape[:-1] + (1,), dtype=x.dtype)
            return jnp.concatenate([ones, x / rrd, x2 / rd], axis=-1)
        key = jax.random.key(seed)
        k0, k1, k2, k3, k4 = jax.random.split(key, 5)
        b, l = (2, 256)
        scale = 1.0 / np.sqrt(D_MODEL)
        return {'hidden_states': jax.random.normal(k0, (b, l, D_MODEL), dtype=jnp.float32), 'Wq': jax.random.normal(k1, (D_MODEL, N_HEADS * FEAT_DIM), dtype=jnp.float32) * scale, 'Wk': jax.random.normal(k2, (D_MODEL, N_HEADS * FEAT_DIM), dtype=jnp.float32) * scale, 'Wv': jax.random.normal(k3, (D_MODEL, N_HEADS * V_DIM), dtype=jnp.float32) * scale, 'Wo': jax.random.normal(k4, (N_HEADS * V_DIM, D_MODEL), dtype=jnp.float32) * scale}
    _L0_attn_all = _L0_attn_setup()
    _L0_attn_in = {k: v for k, v in _L0_attn_all.items() if k in ('Wq', 'Wk', 'Wv', 'Wo')}
    del _L0_attn_all

    def _L0_xattn_setup():
        import jax, jax.numpy as jnp
        import numpy as np
        DIM = 128
        H = 16
        HD = DIM // H
        EPS = 1e-05
        key = jax.random.key(seed)
        ks = jax.random.split(key, 10)
        B, S = (2, 256)
        lim_h = 1.0 / np.sqrt(HD)
        lim_d = 1.0 / np.sqrt(DIM)
        u = lambda k, shape, lim: jax.random.uniform(k, shape, jnp.float32, -lim, lim)
        return {'q': jax.random.normal(ks[0], (B, S, DIM), jnp.float32), 'k': jax.random.normal(ks[1], (B, S, DIM), jnp.float32), 'v': jax.random.normal(ks[2], (B, S, DIM), jnp.float32), 'wq1': u(ks[3], (H, HD, HD), lim_h), 'wk1': u(ks[4], (H, HD, HD), lim_h), 'wq2': u(ks[5], (H, HD, HD), lim_h), 'wk2': u(ks[6], (H, HD, HD), lim_h), 'wv': u(ks[7], (H, HD, HD), lim_h), 'wo': u(ks[8], (DIM, DIM), lim_d), 'gain': jnp.float32(0.3)}
    _L0_xattn_all = _L0_xattn_setup()
    _L0_xattn_in = {k: v for k, v in _L0_xattn_all.items() if k in ('wq1', 'wk1', 'wq2', 'wk2', 'wv', 'wo', 'gain')}
    del _L0_xattn_all

    def _L0_ffn_setup():
        import jax, jax.numpy as jnp
        import numpy as np
        SL, BS, HS, FF, E, TOPK = (256, 2, 128, 512, 8, 2)
        key = jax.random.key(seed)
        ks = jax.random.split(key, 6)
        T = SL * BS
        x = jax.random.normal(ks[0], (SL, BS, HS), jnp.float32)
        scores = jax.random.uniform(ks[1], (T, E), jnp.float32)
        expert_weights = jax.random.uniform(ks[2], (T, TOPK), jnp.float32)
        expert_indices = jax.random.randint(ks[3], (T, TOPK), 0, E, jnp.int32)
        w1 = jax.random.normal(ks[4], (E, HS, FF), jnp.float32) * (1.0 / np.sqrt(HS))
        w2 = jax.random.normal(ks[5], (E, FF, HS), jnp.float32) * (1.0 / np.sqrt(FF))
        bias = jnp.zeros((HS,), jnp.float32)
        return dict(x=x, scores=scores, expert_weights=expert_weights, expert_indices=expert_indices, w1=w1, w2=w2, bias=bias)
    _L0_ffn_all = _L0_ffn_setup()
    _L0_ffn_in = {k: v for k, v in _L0_ffn_all.items() if k in ('scores', 'expert_weights', 'expert_indices', 'w1', 'w2', 'bias')}
    del _L0_ffn_all

    def _L1_attn_setup():
        import jax, jax.numpy as jnp
        import numpy as np
        NUM_HEADS = 16

        def _rope_tables(seq_len, head_dim):
            inv_freq = 1.0 / 10000.0 ** (jnp.arange(0, head_dim, 2, dtype=jnp.float32) / head_dim)
            t = jnp.arange(seq_len, dtype=jnp.float32)
            freqs = t[:, None] * inv_freq[None, :]
            return (jnp.cos(freqs), jnp.sin(freqs))

        def _apply_rope(x, cos, sin):
            hd = x.shape[-1]
            x1, x2 = (x[..., :hd // 2], x[..., hd // 2:])
            c = cos[None, None]
            s = sin[None, None]
            return jnp.concatenate([x1 * c - x2 * s, x2 * c + x1 * s], axis=-1)
        key = jax.random.key(seed)
        k1, k2, k3 = jax.random.split(key, 3)
        B, S, D = (2, 256, 128)
        x = jax.random.normal(k1, (B, S, D), dtype=jnp.float32)
        w_qkv = jax.random.normal(k2, (3 * D, D), dtype=jnp.float32) * (2.0 / D) ** 0.5
        w_out = jax.random.normal(k3, (D, D), dtype=jnp.float32) * (2.0 / D) ** 0.5
        b_out = jnp.zeros((D,), dtype=jnp.float32)
        return {'x': x, 'w_qkv': w_qkv, 'w_out': w_out, 'b_out': b_out}
    _L1_attn_all = _L1_attn_setup()
    _L1_attn_in = {k: v for k, v in _L1_attn_all.items() if k in ('w_qkv', 'w_out', 'b_out')}
    del _L1_attn_all

    def _L1_xattn_setup():
        import jax, jax.numpy as jnp
        import numpy as np
        H = 128
        B = 8
        L_CHAR = 256
        L_SUB = 128

        def _linear(x, W, b):
            return jnp.einsum('blh,oh->blo', x, W) + b

        def _interp_linear(x, out_len):
            L_in = x.shape[1]
            pos = (jnp.arange(out_len, dtype=x.dtype) + 0.5) * (L_in / out_len) - 0.5
            pos = jnp.clip(pos, 0.0, L_in - 1)
            lo = jnp.floor(pos).astype(jnp.int32)
            hi = jnp.minimum(lo + 1, L_in - 1)
            w = (pos - lo.astype(x.dtype))[None, :, None]
            return x[:, lo] * (1 - w) + x[:, hi] * w
        key = jax.random.key(seed)
        ks = jax.random.split(key, 18)
        s = 0.02
        inp = {'char_emb': jax.random.normal(ks[0], (B, L_CHAR, H), jnp.float32), 'subword_emb': jax.random.normal(ks[1], (B, L_SUB, H), jnp.float32)}
        names = ['Wq_c', 'Wk_s', 'Wv_s', 'Wq_s', 'Wk_c', 'Wv_c']
        for i, n in enumerate(names):
            inp[n] = jax.random.normal(ks[2 + 2 * i], (H, H), jnp.float32) * s
            inp['b' + n[1:]] = jax.random.normal(ks[3 + 2 * i], (H,), jnp.float32) * s
        inp['Wg'] = jax.random.normal(ks[14], (H, 2 * H), jnp.float32) * s
        inp['bg'] = jax.random.normal(ks[15], (H,), jnp.float32) * s
        return inp
    _L1_xattn_all = _L1_xattn_setup()
    _L1_xattn_in = {k: v for k, v in _L1_xattn_all.items() if k in ('Wq_c', 'bq_c', 'Wk_s', 'bk_s', 'Wv_s', 'bv_s', 'Wq_s', 'bq_s', 'Wk_c', 'bk_c', 'Wv_c', 'bv_c', 'Wg', 'bg')}
    del _L1_xattn_all

    def _L1_ffn_setup():
        import jax, jax.numpy as jnp
        import numpy as np
        DIM = 128
        DEPTH = 6
        HEADS = 16
        DIM_HEAD = 64
        WINDOW = 32
        INNER = HEADS * DIM_HEAD
        DIM_INNER = int(DIM * 4 * 2 / 3)
        QK_SCALE = 8.0

        def shift_tokens(t):
            a, s = jnp.split(t, 2, -1)
            s = jnp.pad(s, ((0, 0), (1, 0), (0, 0)))[:, :-1]
            return jnp.concatenate([a, s], -1)

        def l2norm(t):
            return t / jnp.maximum(jnp.linalg.norm(t, axis=-1, keepdims=True), 1e-12)

        def rotate_half(x):
            x1, x2 = jnp.split(x, 2, -1)
            return jnp.concatenate([-x2, x1], -1)

        def rotary_tables(n):
            half = jnp.arange(0, DIM_HEAD, 2, dtype=jnp.float32)
            inv_freq = 1.0 / 10000.0 ** (half / DIM_HEAD)
            t = jnp.arange(n, dtype=jnp.float32)
            freqs = t[:, None] * inv_freq[None, :]
            freqs = jnp.concatenate([freqs, freqs], -1)
            base_scale = (half + 0.4 * DIM_HEAD) / (1.4 * DIM_HEAD)
            power = (t - n // 2) / (WINDOW // 2)
            scale = base_scale[None, :] ** power[:, None]
            scale = jnp.concatenate([scale, scale], -1)
            return (freqs, scale)

        def local_attention(q, k, v):
            b, h, n, d = q.shape
            w = WINDOW
            nw = n // w
            bq = q.reshape(b, h, nw, w, d)
            bk = k.reshape(b, h, nw, w, d)
            bv = v.reshape(b, h, nw, w, d)

            def look(t):
                p = jnp.pad(t, ((0, 0), (0, 0), (1, 0), (0, 0), (0, 0)))
                return jnp.concatenate([p[:, :, :nw], p[:, :, 1:]], axis=3)
            bk2, bv2 = (look(bk), look(bv))
            seq = jnp.arange(n).reshape(nw, w)
            seq_p = jnp.pad(seq, ((1, 0), (0, 0)), constant_values=-1)
            jt = jnp.concatenate([seq_p[:nw], seq_p[1:]], axis=1)
            it = seq[:, :, None]
            jb = jt[:, None, :]
            mask = (it < jb) | (it > jb + w) | (jb == -1)
            sim = jnp.einsum('bhwie,bhwje->bhwij', bq, bk2) * QK_SCALE
            sim = jnp.where(mask, -jnp.finfo(sim.dtype).max, sim)
            attn = jax.nn.softmax(sim, -1)
            out = jnp.einsum('bhwij,bhwje->bhwie', attn, bv2)
            return out.reshape(b, h, n, d)

        def attn_layer(x, Wqkv, qs, ksc, Wo):
            b, n, _ = x.shape
            qkv = x @ Wqkv
            q, k, v = jnp.split(qkv, 3, -1)
            sh = lambda t: t.reshape(b, n, HEADS, DIM_HEAD).transpose(0, 2, 1, 3)
            q, k, v = (sh(q), sh(k), sh(v))
            q = l2norm(q) * qs
            k = l2norm(k) * ksc
            freqs, scale = rotary_tables(n)
            cos, sin = (jnp.cos(freqs), jnp.sin(freqs))
            q = q * cos * scale + rotate_half(q) * sin * scale
            inv = 1.0 / scale
            k = k * cos * inv + rotate_half(k) * sin * inv
            out = local_attention(q, k, v)
            out = out.transpose(0, 2, 1, 3).reshape(b, n, INNER)
            return out @ Wo

        def ffn_layer(x, g, bln, W1, b1, W2, b2):
            mu = x.mean(-1, keepdims=True)
            var = ((x - mu) ** 2).mean(-1, keepdims=True)
            xn = (x - mu) / jnp.sqrt(var + 1e-05) * g + bln
            hg = xn @ W1 + b1
            a, gate = jnp.split(hg, 2, -1)
            return a * jax.nn.gelu(gate, approximate=False) @ W2 + b2
        key = jax.random.key(seed)
        ks = jax.random.split(key, 8)
        B, N = (2, 256)
        init = lambda k, shape: jax.random.normal(k, shape, jnp.float32) * 0.02
        return {'x': jax.random.normal(ks[0], (B, N, DIM), jnp.float32), 'Wqkv': init(ks[1], (DEPTH, DIM, 3 * INNER)), 'q_scale': jnp.ones((DEPTH, DIM_HEAD), jnp.float32), 'k_scale': jnp.ones((DEPTH, DIM_HEAD), jnp.float32), 'Wo': init(ks[2], (DEPTH, INNER, DIM)), 'ln_g': jnp.ones((DEPTH, DIM), jnp.float32), 'ln_b': jnp.zeros((DEPTH, DIM), jnp.float32), 'W1': init(ks[3], (DEPTH, DIM, 2 * DIM_INNER)), 'b1': jnp.zeros((DEPTH, 2 * DIM_INNER), jnp.float32), 'W2': init(ks[4], (DEPTH, DIM_INNER, DIM)), 'b2': jnp.zeros((DEPTH, DIM), jnp.float32)}
    _L1_ffn_all = _L1_ffn_setup()
    _L1_ffn_in = {k: v for k, v in _L1_ffn_all.items() if k in ('Wqkv', 'q_scale', 'k_scale', 'Wo', 'ln_g', 'ln_b', 'W1', 'b1', 'W2', 'b2')}
    del _L1_ffn_all
    return {'x': x, 'ctx_1024': ctx_1024, 'L0_attn_Wq': _L0_attn_in['Wq'], 'L0_attn_Wk': _L0_attn_in['Wk'], 'L0_attn_Wv': _L0_attn_in['Wv'], 'L0_attn_Wo': _L0_attn_in['Wo'], 'L0_xattn_wq1': _L0_xattn_in['wq1'], 'L0_xattn_wk1': _L0_xattn_in['wk1'], 'L0_xattn_wq2': _L0_xattn_in['wq2'], 'L0_xattn_wk2': _L0_xattn_in['wk2'], 'L0_xattn_wv': _L0_xattn_in['wv'], 'L0_xattn_wo': _L0_xattn_in['wo'], 'L0_xattn_gain': _L0_xattn_in['gain'], 'L0_ffn_scores': _L0_ffn_in['scores'], 'L0_ffn_expert_weights': _L0_ffn_in['expert_weights'], 'L0_ffn_expert_indices': _L0_ffn_in['expert_indices'], 'L0_ffn_w1': _L0_ffn_in['w1'], 'L0_ffn_w2': _L0_ffn_in['w2'], 'L0_ffn_bias': _L0_ffn_in['bias'], 'L1_attn_w_qkv': _L1_attn_in['w_qkv'], 'L1_attn_w_out': _L1_attn_in['w_out'], 'L1_attn_b_out': _L1_attn_in['b_out'], 'L1_xattn_Wq_c': _L1_xattn_in['Wq_c'], 'L1_xattn_bq_c': _L1_xattn_in['bq_c'], 'L1_xattn_Wk_s': _L1_xattn_in['Wk_s'], 'L1_xattn_bk_s': _L1_xattn_in['bk_s'], 'L1_xattn_Wv_s': _L1_xattn_in['Wv_s'], 'L1_xattn_bv_s': _L1_xattn_in['bv_s'], 'L1_xattn_Wq_s': _L1_xattn_in['Wq_s'], 'L1_xattn_bq_s': _L1_xattn_in['bq_s'], 'L1_xattn_Wk_c': _L1_xattn_in['Wk_c'], 'L1_xattn_bk_c': _L1_xattn_in['bk_c'], 'L1_xattn_Wv_c': _L1_xattn_in['Wv_c'], 'L1_xattn_bv_c': _L1_xattn_in['bv_c'], 'L1_xattn_Wg': _L1_xattn_in['Wg'], 'L1_xattn_bg': _L1_xattn_in['bg'], 'L1_ffn_Wqkv': _L1_ffn_in['Wqkv'], 'L1_ffn_q_scale': _L1_ffn_in['q_scale'], 'L1_ffn_k_scale': _L1_ffn_in['k_scale'], 'L1_ffn_Wo': _L1_ffn_in['Wo'], 'L1_ffn_ln_g': _L1_ffn_in['ln_g'], 'L1_ffn_ln_b': _L1_ffn_in['ln_b'], 'L1_ffn_W1': _L1_ffn_in['W1'], 'L1_ffn_b1': _L1_ffn_in['b1'], 'L1_ffn_W2': _L1_ffn_in['W2'], 'L1_ffn_b2': _L1_ffn_in['b2']}

def reference(x, ctx_1024, L0_attn_Wq, L0_attn_Wk, L0_attn_Wv, L0_attn_Wo, L0_xattn_wq1, L0_xattn_wk1, L0_xattn_wq2, L0_xattn_wk2, L0_xattn_wv, L0_xattn_wo, L0_xattn_gain, L0_ffn_scores, L0_ffn_expert_weights, L0_ffn_expert_indices, L0_ffn_w1, L0_ffn_w2, L0_ffn_bias, L1_attn_w_qkv, L1_attn_w_out, L1_attn_b_out, L1_xattn_Wq_c, L1_xattn_bq_c, L1_xattn_Wk_s, L1_xattn_bk_s, L1_xattn_Wv_s, L1_xattn_bv_s, L1_xattn_Wq_s, L1_xattn_bq_s, L1_xattn_Wk_c, L1_xattn_bk_c, L1_xattn_Wv_c, L1_xattn_bv_c, L1_xattn_Wg, L1_xattn_bg, L1_ffn_Wqkv, L1_ffn_q_scale, L1_ffn_k_scale, L1_ffn_Wo, L1_ffn_ln_g, L1_ffn_ln_b, L1_ffn_W1, L1_ffn_b1, L1_ffn_W2, L1_ffn_b2):
    import jax
    import jax.numpy as jnp

    def _L0_attn_ref(hidden_states, Wq, Wk, Wv, Wo):
        import jax, jax.numpy as jnp
        import numpy as np
        D_MODEL = 128
        N_HEADS = 16
        FEAT_DIM = 16
        V_DIM = 64
        EPS = 1e-12

        def taylor_exp(x):
            d = x.shape[-1]
            rd = jnp.sqrt(jnp.float32(d))
            rrd = jnp.sqrt(rd)
            r2 = jnp.sqrt(jnp.float32(2.0))
            x2 = (x[..., :, None] * x[..., None, :]).reshape(*x.shape[:-1], d * d) / r2
            ones = jnp.ones(x.shape[:-1] + (1,), dtype=x.dtype)
            return jnp.concatenate([ones, x / rrd, x2 / rd], axis=-1)
        b, l, _ = hidden_states.shape
        q = (hidden_states @ Wq).reshape(b, l, N_HEADS, FEAT_DIM).transpose(0, 2, 1, 3)
        k = (hidden_states @ Wk).reshape(b, l, N_HEADS, FEAT_DIM).transpose(0, 2, 1, 3)
        v = (hidden_states @ Wv).reshape(b, l, N_HEADS, V_DIM).transpose(0, 2, 1, 3)
        qf = taylor_exp(q)
        kf = taylor_exp(k)
        A = jnp.einsum('bhnf,bhmf->bhnm', qf, kf)
        A = jnp.tril(A)
        y = jnp.einsum('bhnm,bhme->bhne', A, v)
        z = 1.0 / (jnp.einsum('bhlf,bhlf->bhl', qf, jnp.cumsum(kf, axis=2)) + EPS)
        y = y * z[..., None]
        out = y.transpose(0, 2, 1, 3).reshape(b, l, N_HEADS * V_DIM) @ Wo
        return out

    def _L0_xattn_ref(q, k, v, wq1, wk1, wq2, wk2, wv, wo, gain):
        import jax, jax.numpy as jnp
        import numpy as np
        DIM = 128
        H = 16
        HD = DIM // H
        EPS = 1e-05
        B, S, D = q.shape
        h, hd = (wq1.shape[0], wq1.shape[1])
        scale = jnp.sqrt(jnp.asarray(hd, jnp.float32))
        qh = q.reshape(B, S, h, hd)
        kh = k.reshape(B, S, h, hd)
        vh = v.reshape(B, S, h, hd)
        q1 = jnp.einsum('bshd,hed->bshe', qh, wq1)
        k1 = jnp.einsum('bshd,hed->bshe', kh, wk1)
        q2 = jnp.einsum('bshd,hed->bshe', qh, wq2)
        k2 = jnp.einsum('bshd,hed->bshe', kh, wk2)
        vp = jnp.einsum('bshd,hed->bshe', vh, wv)
        s1 = jnp.einsum('bshe,bthe->bhst', q1, k1) / scale
        s2 = jnp.einsum('bshe,bthe->bhst', q2, k2) / scale
        attn = jax.nn.softmax(s1, axis=-1) - gain * jax.nn.softmax(s2, axis=-1)
        o = jnp.einsum('bhst,bthe->bshe', attn, vp)
        mean = jnp.mean(o, axis=-1, keepdims=True)
        var = jnp.mean(jnp.square(o - mean), axis=-1, keepdims=True)
        o = (o - mean) / jnp.sqrt(var + EPS)
        out = o.reshape(B, S, D) @ wo.T
        return out

    def _L0_ffn_ref(x, scores, expert_weights, expert_indices, w1, w2, bias):
        import jax, jax.numpy as jnp
        import numpy as np
        SL, BS, HS, FF, E, TOPK = (256, 2, 128, 512, 8, 2)
        sl, bs, hs = x.shape
        n_exp = w1.shape[0]
        top_k = expert_indices.shape[-1]
        xf = x.reshape(-1, hs)
        flat_idx = expert_indices.reshape(-1)
        flat_w = expert_weights.reshape(-1)
        order = jnp.argsort(flat_idx)
        tok = order // top_k
        tokens_per_expert = jnp.bincount(flat_idx, length=n_exp).astype(jnp.int32)
        xs = xf[tok]
        h = jax.nn.gelu(jax.lax.ragged_dot(xs, w1, tokens_per_expert), approximate=False)
        ys = jax.lax.ragged_dot(h, w2, tokens_per_expert)
        ys = ys * flat_w[order][:, None]
        out = jnp.zeros_like(xf).at[tok].add(ys)
        return out.reshape(sl, bs, hs) + bias

    def _L1_attn_ref(x, w_qkv, w_out, b_out):
        import jax, jax.numpy as jnp
        import numpy as np
        NUM_HEADS = 16

        def _rope_tables(seq_len, head_dim):
            inv_freq = 1.0 / 10000.0 ** (jnp.arange(0, head_dim, 2, dtype=jnp.float32) / head_dim)
            t = jnp.arange(seq_len, dtype=jnp.float32)
            freqs = t[:, None] * inv_freq[None, :]
            return (jnp.cos(freqs), jnp.sin(freqs))

        def _apply_rope(x, cos, sin):
            hd = x.shape[-1]
            x1, x2 = (x[..., :hd // 2], x[..., hd // 2:])
            c = cos[None, None]
            s = sin[None, None]
            return jnp.concatenate([x1 * c - x2 * s, x2 * c + x1 * s], axis=-1)
        B, S, D = x.shape
        H = NUM_HEADS
        hd = D // H
        scale = hd ** (-0.5)
        qkv = jnp.einsum('bsd,ed->bse', x, w_qkv)
        qkv = qkv.reshape(B, S, 3, H, hd).transpose(2, 0, 3, 1, 4)
        q, k, v = (qkv[0], qkv[1], qkv[2])
        cos, sin = _rope_tables(S, hd)
        q = _apply_rope(q, cos, sin)
        k = _apply_rope(k, cos, sin)
        scores = jnp.einsum('bhqd,bhkd->bhqk', q, k) * scale
        attn = jax.nn.softmax(scores, axis=-1)
        out = jnp.einsum('bhqk,bhkd->bhqd', attn, v)
        out = out.transpose(0, 2, 1, 3).reshape(B, S, D)
        return jnp.einsum('bsd,ed->bse', out, w_out) + b_out

    def _L1_xattn_ref(char_emb, subword_emb, Wq_c, bq_c, Wk_s, bk_s, Wv_s, bv_s, Wq_s, bq_s, Wk_c, bk_c, Wv_c, bv_c, Wg, bg):
        import jax, jax.numpy as jnp
        import numpy as np
        H = 128
        B = 8
        L_CHAR = 256
        L_SUB = 128

        def _linear(x, W, b):
            return jnp.einsum('blh,oh->blo', x, W) + b

        def _interp_linear(x, out_len):
            L_in = x.shape[1]
            pos = (jnp.arange(out_len, dtype=x.dtype) + 0.5) * (L_in / out_len) - 0.5
            pos = jnp.clip(pos, 0.0, L_in - 1)
            lo = jnp.floor(pos).astype(jnp.int32)
            hi = jnp.minimum(lo + 1, L_in - 1)
            w = (pos - lo.astype(x.dtype))[None, :, None]
            return x[:, lo] * (1 - w) + x[:, hi] * w
        h = char_emb.shape[-1]
        scale = 1.0 / jnp.sqrt(jnp.asarray(h, char_emb.dtype))
        Q_char = _linear(char_emb, Wq_c, bq_c)
        K_sub = _linear(subword_emb, Wk_s, bk_s)
        V_sub = _linear(subword_emb, Wv_s, bv_s)
        scores = jnp.einsum('bqh,bkh->bqk', Q_char, K_sub) * scale
        char2sub = jnp.einsum('bqk,bkh->bqh', jax.nn.softmax(scores, axis=-1), V_sub)
        Q_sub = _linear(subword_emb, Wq_s, bq_s)
        K_char = _linear(char_emb, Wk_c, bk_c)
        V_char = _linear(char_emb, Wv_c, bv_c)
        scores2 = jnp.einsum('bqh,bkh->bqk', Q_sub, K_char) * scale
        sub2char = jnp.einsum('bqk,bkh->bqh', jax.nn.softmax(scores2, axis=-1), V_char)
        L_char = char_emb.shape[1]
        if sub2char.shape[1] != L_char:
            sub2char = _interp_linear(sub2char, L_char)
        gate_in = jnp.concatenate([char2sub, sub2char], axis=-1)
        gate = jax.nn.sigmoid(jnp.einsum('blh,oh->blo', gate_in, Wg) + bg)
        return gate * char2sub + (1 - gate) * sub2char

    def _L1_ffn_ref(x, Wqkv, q_scale, k_scale, Wo, ln_g, ln_b, W1, b1, W2, b2):
        import jax, jax.numpy as jnp
        import numpy as np
        DIM = 128
        DEPTH = 6
        HEADS = 16
        DIM_HEAD = 64
        WINDOW = 32
        INNER = HEADS * DIM_HEAD
        DIM_INNER = int(DIM * 4 * 2 / 3)
        QK_SCALE = 8.0

        def shift_tokens(t):
            a, s = jnp.split(t, 2, -1)
            s = jnp.pad(s, ((0, 0), (1, 0), (0, 0)))[:, :-1]
            return jnp.concatenate([a, s], -1)

        def l2norm(t):
            return t / jnp.maximum(jnp.linalg.norm(t, axis=-1, keepdims=True), 1e-12)

        def rotate_half(x):
            x1, x2 = jnp.split(x, 2, -1)
            return jnp.concatenate([-x2, x1], -1)

        def rotary_tables(n):
            half = jnp.arange(0, DIM_HEAD, 2, dtype=jnp.float32)
            inv_freq = 1.0 / 10000.0 ** (half / DIM_HEAD)
            t = jnp.arange(n, dtype=jnp.float32)
            freqs = t[:, None] * inv_freq[None, :]
            freqs = jnp.concatenate([freqs, freqs], -1)
            base_scale = (half + 0.4 * DIM_HEAD) / (1.4 * DIM_HEAD)
            power = (t - n // 2) / (WINDOW // 2)
            scale = base_scale[None, :] ** power[:, None]
            scale = jnp.concatenate([scale, scale], -1)
            return (freqs, scale)

        def local_attention(q, k, v):
            b, h, n, d = q.shape
            w = WINDOW
            nw = n // w
            bq = q.reshape(b, h, nw, w, d)
            bk = k.reshape(b, h, nw, w, d)
            bv = v.reshape(b, h, nw, w, d)

            def look(t):
                p = jnp.pad(t, ((0, 0), (0, 0), (1, 0), (0, 0), (0, 0)))
                return jnp.concatenate([p[:, :, :nw], p[:, :, 1:]], axis=3)
            bk2, bv2 = (look(bk), look(bv))
            seq = jnp.arange(n).reshape(nw, w)
            seq_p = jnp.pad(seq, ((1, 0), (0, 0)), constant_values=-1)
            jt = jnp.concatenate([seq_p[:nw], seq_p[1:]], axis=1)
            it = seq[:, :, None]
            jb = jt[:, None, :]
            mask = (it < jb) | (it > jb + w) | (jb == -1)
            sim = jnp.einsum('bhwie,bhwje->bhwij', bq, bk2) * QK_SCALE
            sim = jnp.where(mask, -jnp.finfo(sim.dtype).max, sim)
            attn = jax.nn.softmax(sim, -1)
            out = jnp.einsum('bhwij,bhwje->bhwie', attn, bv2)
            return out.reshape(b, h, n, d)

        def attn_layer(x, Wqkv, qs, ksc, Wo):
            b, n, _ = x.shape
            qkv = x @ Wqkv
            q, k, v = jnp.split(qkv, 3, -1)
            sh = lambda t: t.reshape(b, n, HEADS, DIM_HEAD).transpose(0, 2, 1, 3)
            q, k, v = (sh(q), sh(k), sh(v))
            q = l2norm(q) * qs
            k = l2norm(k) * ksc
            freqs, scale = rotary_tables(n)
            cos, sin = (jnp.cos(freqs), jnp.sin(freqs))
            q = q * cos * scale + rotate_half(q) * sin * scale
            inv = 1.0 / scale
            k = k * cos * inv + rotate_half(k) * sin * inv
            out = local_attention(q, k, v)
            out = out.transpose(0, 2, 1, 3).reshape(b, n, INNER)
            return out @ Wo

        def ffn_layer(x, g, bln, W1, b1, W2, b2):
            mu = x.mean(-1, keepdims=True)
            var = ((x - mu) ** 2).mean(-1, keepdims=True)
            xn = (x - mu) / jnp.sqrt(var + 1e-05) * g + bln
            hg = xn @ W1 + b1
            a, gate = jnp.split(hg, 2, -1)
            return a * jax.nn.gelu(gate, approximate=False) @ W2 + b2
        for i in range(DEPTH):
            x = attn_layer(shift_tokens(x), Wqkv[i], q_scale[i], k_scale[i], Wo[i]) + x
            x = ffn_layer(shift_tokens(x), ln_g[i], ln_b[i], W1[i], b1[i], W2[i], b2[i]) + x
        return x
    x = x + _L0_attn_ref(_layernorm(x, axis=-1), L0_attn_Wq, L0_attn_Wk, L0_attn_Wv, L0_attn_Wo)
    x = x + _L0_xattn_ref(_layernorm(x, axis=-1), ctx_1024, ctx_1024, L0_xattn_wq1, L0_xattn_wk1, L0_xattn_wq2, L0_xattn_wk2, L0_xattn_wv, L0_xattn_wo, L0_xattn_gain)
    x = x + _L0_ffn_ref(_layernorm(x, axis=-1), L0_ffn_scores, L0_ffn_expert_weights, L0_ffn_expert_indices, L0_ffn_w1, L0_ffn_w2, L0_ffn_bias)
    x = x + _L1_attn_ref(_layernorm(x, axis=-1), L1_attn_w_qkv, L1_attn_w_out, L1_attn_b_out)
    x = x + _L1_xattn_ref(_layernorm(x, axis=-1), ctx_1024, L1_xattn_Wq_c, L1_xattn_bq_c, L1_xattn_Wk_s, L1_xattn_bk_s, L1_xattn_Wv_s, L1_xattn_bv_s, L1_xattn_Wq_s, L1_xattn_bq_s, L1_xattn_Wk_c, L1_xattn_bk_c, L1_xattn_Wv_c, L1_xattn_bv_c, L1_xattn_Wg, L1_xattn_bg)
    x = x + _L1_ffn_ref(_layernorm(x, axis=-1), L1_ffn_Wqkv, L1_ffn_q_scale, L1_ffn_k_scale, L1_ffn_Wo, L1_ffn_ln_g, L1_ffn_ln_b, L1_ffn_W1, L1_ffn_b1, L1_ffn_W2, L1_ffn_b2)
    return x

_drawn_inputs = setup_inputs


def setup_inputs(seed=0):
    import zlib

    import numpy as np

    out = dict(_drawn_inputs(seed))
    spreads = {'L0_ffn_bias': (0.0, 0.1),
     'L1_attn_b_out': (0.0, 0.1),
     'L1_ffn_q_scale': (1.0, 0.6),
     'L1_ffn_k_scale': (1.0, 0.6),
     'L1_ffn_ln_g': (1.0, 0.6),
     'L1_ffn_ln_b': (0.0, 0.8),
     'L1_ffn_b1': (0.0, 0.8),
     'L1_ffn_b2': (0.0, 0.1)}
    factors = {'L1_xattn_Wq_c': 8.0,
     'L1_xattn_bq_c': 64.0,
     'L1_xattn_Wk_s': 8.0,
     'L1_xattn_bk_s': 64.0,
     'L1_xattn_bv_s': 8.0,
     'L1_xattn_Wq_s': 8.0,
     'L1_xattn_bq_s': 64.0,
     'L1_xattn_Wk_c': 8.0,
     'L1_xattn_bk_c': 64.0,
     'L1_xattn_bv_c': 8.0,
     'L1_xattn_Wg': 8.0,
     'L1_xattn_bg': 64.0,
     'L1_ffn_W1': 5.17,
     'L1_ffn_W2': 5.071}
    for name, (base, spread) in spreads.items():
        noise = np.random.default_rng([zlib.crc32(name.encode()), seed]).standard_normal(out[name].shape)
        drawn = base * np.exp(spread * noise) if base else spread * noise
        out[name] = jnp.asarray(drawn.astype(out[name].dtype))
    for name, factor in factors.items():
        out[name] = (out[name] * factor).astype(out[name].dtype)
    return out
```

```python
from contextlib import ExitStack

import numpy as np

import concourse.bass as bass
from concourse import mybir

P = 128
B, S, D = 8, 128, 128
H = 16
PAD = 32
HC = P // PAD
NC = H // HC
G = 4
BANK = 512
WIN = 96
HD_A, VD_A = 16, 64
HD_S = 8
E_EXP, FF, TOPK = 8, 512, 2
MOE_T = 512
HD_F, WINDOW, DEPTH, INNER, DI = 64, 32, 6, 1024, 341
QK_SCALE, MASKED = 8.0, -1e30
LN_EPS = 1e-5

F32 = mybir.dt.float32
BF16 = mybir.dt.bfloat16
I32 = mybir.dt.int32
ALU = mybir.AluOpType
ACT = mybir.ActivationFunctionType
AX = mybir.AxisListType.X


class Stage:

    def __init__(self, nc, name):
        self.nc, self.name, self.ctx, self.sems = nc, name, ExitStack(), []
        self.ctx.callback(self.clear)

    def clear(self):
        if self.sems:
            self.nc.clear_and_free_semaphores(self.sems)
            self.nc.all_engine_barrier()

    def sb(self, name, shape, dt=F32):
        return self.ctx.enter_context(self.nc.sbuf_tensor(f"{self.name}_{name}", shape, dt))

    def ps(self, name, cols=BANK):
        return self.ctx.enter_context(self.nc.psum_tensor(f"{self.name}_{name}", [P, cols], F32))

    def sem(self, name):
        self.sems.append(self.nc.alloc_semaphore(f"{self.name}_{name}"))
        return self.sems[-1]


def over(ap, n):
    return ap.unsqueeze(1).to_broadcast([ap.shape[0], n, ap.shape[1]])


def along(ap, n):
    return ap.unsqueeze(2).to_broadcast([ap.shape[0], ap.shape[1], n])


class LayerNorm:

    def __init__(self, nc, st, glob, count=B):
        self.nc, self.x, self.g, self.n = nc, glob["x"], glob, count
        self.stats = st.sb("ln_stats", [P, B, 6])
        self.mv = st.sb("ln_mv", [P, B, 2])
        self.ve = st.sb("ln_var_eps", [P, B])
        self.rstd = st.sb("ln_rstd", [P, B])
        self.xh = st.sb("x_hat", [P, D])
        self.xT = st.sb("x_hat_T", [P, S])
        self.psX = st.ps("ps_x")
        self.stats_done = st.sem("ln_stats_done")
        self.mv_done = st.sem("ln_mv_done")
        self.ve_done = st.sem("ln_ve_done")
        self.rstd_done = st.sem("ln_rstd_done")
        self.xh_ready = st.sem("xh_ready")
        self.psx_ready = st.sem("psx_ready")
        self.xT_ready = st.sem("xT_ready")

    def dve_stats(self, dve):
        nc, n = self.nc, self.n
        for b in range(n):
            nc.vector.bn_stats(self.stats[:, b, :], self.x[:, b, :]).then_inc(self.stats_done, 1)
        for b in range(n):
            dve.wait_ge(self.stats_done, b + 1)
            nc.vector.bn_aggr(self.mv[:, b, :], self.stats[:, b, :]).then_inc(self.mv_done, 1)
        dve.wait_ge(self.mv_done, n)
        nc.vector.tensor_scalar(self.ve[:, 0:n], self.mv[:, 0:n, 1], LN_EPS, None,
                                ALU.add).then_inc(self.ve_done, 1)

    def pool_rstd(self, pool):
        pool.wait_ge(self.ve_done, 1)
        self.nc.gpsimd.tensor_tensor(self.rstd[:, 0:self.n], self.ve[:, 0:self.n],
                                     self.g["mhalf"][:, 0:self.n], ALU.pow).then_inc(self.rstd_done, 1)

    def dve_normalise(self, dve, b):
        dve.wait_ge(self.rstd_done, 1)
        self.nc.vector.tensor_scalar(self.xh[:, :], self.x[:, bass.ds(b, 1), :],
                                     self.mv[:, bass.ds(b, 1), 0], self.rstd[:, bass.ds(b, 1)],
                                     ALU.subtract, ALU.mult).then_inc(self.xh_ready, 1)

    def pe_transpose(self, pe, b):
        pe.wait_ge(self.xh_ready, b + 1)
        self.nc.tensor.transpose(self.psX[:, 0:S], self.xh[:, :],
                                 self.g["ident"][:, :]).then_inc(self.psx_ready, 1)

    def act_store(self, act, b):
        act.wait_ge(self.psx_ready, b + 1)
        self.nc.scalar.copy(self.xT[:, :], self.psX[:, 0:S]).then_inc(self.xT_ready, 1)


class SoftmaxHeads:

    RING = 2

    def __init__(self, nc, st, glob, groups, scale):
        self.nc, self.groups, self.scale, self.g = nc, groups, scale, glob
        self.psS = [st.ps(f"ps_scores{i}") for i in range(2)]
        self.psT = [st.ps(f"ps_probsT{i}") for i in range(2)]
        self.mx = [st.sb(f"row_max{i}", [P, G]) for i in range(2)]
        self.dif = [st.sb(f"dif{i}", [P, BANK]) for i in range(2)]
        self.prob = [st.sb(f"prob{i}", [P, BANK]) for i in range(2)]
        self.probT = [st.sb(f"probT{i}", [P, BANK]) for i in range(2)]
        self.scores_ready = st.sem("scores_ready")
        self.max_done = st.sem("max_done")
        self.dif_done = st.sem("dif_done")
        self.exp_done = st.sem("exp_done")
        self.transposed = st.sem("transposed")
        self.probT_done = st.sem("probT_done")
        self.values_done = st.sem("values_done")

    def credit(self, eng, *sems):
        for s in sems:
            eng.sem_inc(s, self.RING)

    def u(self, t, g):
        return t * self.groups + g

    def heads(self, ap):
        return ap.rearrange("p (h m) -> p h m", h=G)

    def pe_scores(self, pe, t, g, product):
        u = self.u(t, g)
        pe.wait_ge(self.dif_done, u + 1)
        product(self.psS[g % 2], g).then_inc(self.scores_ready, 1)

    def dve_shift(self, dve, t, g):
        u, i = self.u(t, g), g % 2
        dve.wait_ge(self.scores_ready, u + 1)
        self.nc.vector.tensor_reduce(self.mx[i][:, :], self.heads(self.psS[i][:, :]), AX,
                                     ALU.max).then_inc(self.max_done, 1)
        dve.wait_ge(self.exp_done, u + 1)
        dve.wait_ge(self.max_done, u + 1)
        self.nc.vector.tensor_tensor(self.heads(self.dif[i][:, :]), self.heads(self.psS[i][:, :]),
                                     along(self.mx[i][:, :], S),
                                     ALU.subtract).then_inc(self.dif_done, 1)

    def act_exp(self, act, t, g):
        u, i = self.u(t, g), g % 2
        act.wait_ge(self.dif_done, u + 1 + self.RING)
        act.wait_ge(self.transposed, u + 1)
        self.nc.scalar.activation(self.prob[i][:, :], self.dif[i][:, :], ACT.Exp,
                                  scale=self.scale).then_inc(self.exp_done, 1)

    def pe_transpose(self, pe, t, g):
        u, i = self.u(t, g), g % 2
        pe.wait_ge(self.exp_done, u + 1 + self.RING)
        pe.wait_ge(self.probT_done, u + 1)
        for j in range(G):
            last = self.nc.tensor.transpose(self.psT[i][:, j * S:(j + 1) * S],
                                            self.prob[i][:, j * S:(j + 1) * S], self.g["ident"][:, :])
        last.then_inc(self.transposed, 1)

    def act_store(self, act, t, g):
        u, i = self.u(t, g), g % 2
        act.wait_ge(self.transposed, u + 1 + self.RING)
        act.wait_ge(self.values_done, u + 1)
        self.nc.scalar.copy(self.probT[i][:, :], self.psT[i][:, :]).then_inc(self.probT_done, 1)

    def pe_values(self, pe, t, g, product):
        u, i = self.u(t, g), g % 2
        pe.wait_ge(self.probT_done, u + 1 + self.RING)
        product([self.probT[i][:, j * S:(j + 1) * S] for j in range(G)], g).then_inc(self.values_done, 1)

    def pe_all(self, pe, t, scores, values):
        n = self.groups
        self.pe_scores(pe, t, 0, scores)
        for g in range(n):
            if g + 1 < n:
                self.pe_scores(pe, t, g + 1, scores)
            if g:
                self.pe_values(pe, t, g - 1, values)
            self.pe_transpose(pe, t, g)
        self.pe_values(pe, t, n - 1, values)

    def act_all(self, act, t):
        self.act_exp(act, t, 0)
        for g in range(self.groups):
            if g + 1 < self.groups:
                self.act_exp(act, t, g + 1)
            self.act_store(act, t, g)

    def dve_all(self, dve, t):
        for g in range(self.groups):
            self.dve_shift(dve, t, g)


def load_stage(nc, glob, dram):
    st = Stage(nc, "load")
    with st.ctx:
        ctx = st.sb("ctx", [P, B, D])
        psC = [st.ps(f"ps_ctx{i}") for i in range(2)]
        loaded, ident_in, x_in = st.sem("ctx_in"), st.sem("ident_in"), st.sem("x_in")
        transposed = st.sem("ctx_transposed")
        stored, ready = st.sem("ctx_stored"), st.sem("const_ready")
        with nc.Block() as block:
            @block.sync
            def _(sp):
                sp.dma_start(ctx[:, :, :], dram["ctx_1024"].rearrange("b p d -> p b d")).then_inc(loaded, 16)
                sp.dma_start(glob["x"][:, :, :], dram["x"].rearrange("b p d -> p b d")).then_inc(x_in, 16)
                sp.wait_ge(x_in, 16)

            @block.gpsimd
            def _(pool):
                nc.gpsimd.memset(glob["mhalf"][:, :], -0.5).then_inc(ready, 1)
                pool.dma_start(glob["ident"][:, :], dram["c_ident"]).then_inc(ident_in, 16)
                pool.wait_ge(ready, 1)

            @block.tensor
            def _(pe):
                pe.wait_ge(ident_in, 16)
                pe.wait_ge(loaded, 16)
                for b in range(B):
                    nc.tensor.transpose(psC[b // 4][:, b % 4 * S:(b % 4 + 1) * S], ctx[:, b, :],
                                        glob["ident"][:, :]).then_inc(transposed, 1)

            @block.scalar
            def _(act):
                for i in range(2):
                    act.wait_ge(transposed, 4 * i + 4)
                    nc.scalar.copy(glob["ctxT"][:, 4 * i:4 * i + 4, :], psC[i][:, :]).then_inc(stored, 1)
                act.wait_ge(stored, 2)


def taylor_stage(nc, glob, dram):
    st = Stage(nc, "tay")
    with st.ctx:
        ln = LayerNorm(nc, st, glob)
        x = glob["x"]
        wq = st.sb("wq", [P, NC * P])
        wk = st.sb("wk", [P, NC * P])
        wv = st.sb("wv", [P, H * VD_A])
        wo = st.sb("wo", [P, H * VD_A // P, D])
        mask = st.sb("mask", [P, S])
        VW = VD_A + 1
        v = st.sb("v", [P, H * VW + WIN])
        v3 = v[:, 0:H * VW].rearrange("p (h e) -> p h e", e=VW)
        qT = st.sb("qT", [P, NC, S])
        kT = st.sb("kT", [P, NC, S])
        sq = [st.sb(f"square{i}", [P, BANK]) for i in range(2)]
        at = [st.sb(f"weights{i}", [P, BANK]) for i in range(2)]
        rz = st.sb("rz", [P, 2, G])
        yn = st.sb("y", [P, H * VD_A])
        yT = st.sb("yT", [P, H * VD_A])
        psQ = [st.ps(f"ps_proj{i}") for i in range(2)]
        psS = [st.ps(f"ps_scores{i}") for i in range(2)]
        psO = [st.ps(f"ps_out{i}") for i in range(2)]
        psY = ln.psX
        w_in, ones_ready, tables_in = st.sem("w_in"), st.sem("ones_ready"), st.sem("tables_in")
        qk_proj, v_proj = st.sem("qk_proj"), st.sem("v_proj")
        q_stored, k_stored = st.sem("q_stored"), st.sem("k_stored")
        v0_stored, v1_stored = st.sem("v0_stored"), st.sem("v1_stored")
        scores_ready, squared, masked = st.sem("scores_ready"), st.sem("squared"), st.sem("masked")
        out_ready, z_ready, rz_ready = st.sem("out_ready"), st.sem("z_ready"), st.sem("rz_ready")
        y_ready, yT_ready = st.sem("y_ready"), st.sem("yT_ready")
        yT0_stored, yT1_stored = st.sem("yT0_stored"), st.sem("yT1_stored")
        o_ready, added = st.sem("o_ready"), st.sem("added")

        with nc.Block() as block:
            @block.sync
            def _(sp):
                sp.dma_start(wq[:, :], dram["L0_attn_Wq"]).then_inc(w_in, 16)
                sp.dma_start(wk[:, :], dram["L0_attn_Wk"]).then_inc(w_in, 16)
                sp.dma_start(wv[:, :], dram["L0_attn_Wv"]).then_inc(w_in, 16)
                sp.dma_start(wo[:, :, :], dram["L0_attn_Wo"].rearrange("(c p) n -> p c n", p=P)).then_inc(w_in, 16)
                sp.dma_start(mask[:, :], dram["c_causalT"]).then_inc(tables_in, 16)

            @block.gpsimd
            def _(pool):
                nc.gpsimd.memset(v[:, :], 1.0).then_inc(ones_ready, 1)
                ln.pool_rstd(pool)

            @block.tensor
            def _(pe):
                pe.wait_ge(w_in, 64)
                with pe.Fori(0, B) as b:
                    ln.pe_transpose(pe, b)
                    pe.wait_ge(ln.xT_ready, b + 1)
                    for i, w in enumerate((wq, wk)):
                        for c in range(NC):
                            last = nc.tensor.matmul(psQ[i][:, c * S:(c + 1) * S], w[:, c * P:(c + 1) * P],
                                                    ln.xT[:, :], start=True, stop=True)
                        last.then_inc(qk_proj, 1)
                    for i in range(2):
                        nc.tensor.matmul(psO[i][:, :], ln.xT[:, :], wv[:, i * BANK:(i + 1) * BANK],
                                         start=True, stop=True).then_inc(v_proj, 1)
                    pe.wait_ge(q_stored, b + 1)
                    pe.wait_ge(k_stored, b + 1)

                    def scores(g):
                        if g >= 2:
                            pe.wait_ge(squared, b * NC + g - 1)
                        for j in range(G):
                            r = g * PAD
                            last = nc.tensor.matmul(psS[g % 2][:, j * S:(j + 1) * S], kT[r:r + HD_A, j, :],
                                                    qT[r:r + HD_A, j, :], start=True, stop=True)
                        last.then_inc(scores_ready, 1)

                    scores(0)
                    for g in range(NC):
                        if g + 1 < NC:
                            scores(g + 1)
                        if g == 0:
                            pe.wait_ge(v0_stored, b + 1)
                            pe.wait_ge(v1_stored, b + 1)
                            pe.wait_ge(ones_ready, 1)
                        if g >= 2:
                            pe.wait_ge(y_ready, b * NC + g - 1)
                        pe.wait_ge(masked, b * NC + g + 1)
                        for j in range(G):
                            c = (g * G + j) * VW
                            last = nc.tensor.matmul(psO[g % 2][:, j * S:j * S + WIN],
                                                    at[g % 2][:, j * S:(j + 1) * S], v[:, c:c + WIN],
                                                    start=True, stop=True)
                        last.then_inc(out_ready, 1)
                    pe.wait_ge(y_ready, b * NC + NC)
                    for c in range(8):
                        last = nc.tensor.transpose(psQ[c // 4][:, c % 4 * S:(c % 4 + 1) * S],
                                                   yn[:, c * P:(c + 1) * P], glob["ident"][:, :])
                        if c % 4 == 3:
                            last.then_inc(yT_ready, 1)
                    pe.wait_ge(yT0_stored, b + 1)
                    pe.wait_ge(yT1_stored, b + 1)
                    for c in range(8):
                        last = nc.tensor.matmul(psY[:, 0:D], yT[:, c * P:(c + 1) * P], wo[:, c, :],
                                                start=(c == 0), stop=(c == 7))
                    last.then_inc(o_ready, 1)

            @block.scalar
            def _(act):
                act.wait_ge(ones_ready, 1)
                with act.Fori(0, B) as b:
                    ln.act_store(act, b)
                    act.wait_ge(qk_proj, 2 * b + 1)
                    nc.scalar.copy(qT[:, :, :], psQ[0][:, :]).then_inc(q_stored, 1)
                    act.wait_ge(v_proj, 2 * b + 1)
                    nc.scalar.copy(v3[:, 0:8, 0:VD_A],
                                   psO[0][:, :].rearrange("p (h e) -> p h e", h=8)).then_inc(v0_stored, 1)
                    for g in range(NC):
                        act.wait_ge(scores_ready, b * NC + g + 1)
                        if g >= 2:
                            act.wait_ge(masked, b * NC + g - 1)
                        nc.scalar.activation(sq[g % 2][:, :], psS[g % 2][:, :], ACT.Square, bias=1.0,
                                             scale=0.25).then_inc(squared, 1)
                    act.wait_ge(yT_ready, 2 * b + 1)
                    nc.scalar.copy(yT[:, 0:BANK], psQ[0][:, :]).then_inc(yT0_stored, 1)

            @block.vector
            def _(dve):
                ln.dve_stats(dve)
                dve.wait_ge(tables_in, 16)
                dve.wait_ge(ones_ready, 1)
                with dve.Fori(0, B) as b:
                    ln.dve_normalise(dve, b)
                    dve.wait_ge(qk_proj, 2 * b + 2)
                    nc.vector.tensor_copy(kT[:, :, :], psQ[1][:, :]).then_inc(k_stored, 1)
                    dve.wait_ge(v_proj, 2 * b + 2)
                    nc.vector.tensor_copy(v3[:, 8:16, 0:VD_A],
                                          psO[1][:, :].rearrange("p (h e) -> p h e", h=8)).then_inc(v1_stored, 1)

                    def weights(g):
                        dve.wait_ge(squared, b * NC + g + 1)
                        if g >= 2:
                            dve.wait_ge(out_ready, b * NC + g - 1)
                        nc.vector.scalar_tensor_tensor(
                            at[g % 2][:, :].rearrange("p (h m) -> p h m", h=G),
                            sq[g % 2][:, :].rearrange("p (h m) -> p h m", h=G), 1.0,
                            over(mask[:, :], G), ALU.add, ALU.mult).then_inc(masked, 1)

                    def normalise(g):
                        o3 = psO[g % 2][:, :].rearrange("p (h e) -> p h e", h=G)
                        dve.wait_ge(out_ready, b * NC + g + 1)
                        nc.vector.tensor_scalar(rz[:, 0, :], o3[:, :, VD_A], 2e-12, None,
                                                ALU.add).then_inc(z_ready, 1)
                        dve.wait_ge(z_ready, b * NC + g + 1)
                        nc.vector.reciprocal(rz[:, 1, :], rz[:, 0, :]).then_inc(rz_ready, 1)
                        dve.wait_ge(rz_ready, b * NC + g + 1)
                        nc.vector.tensor_tensor(
                            yn[:, g * G * VD_A:(g + 1) * G * VD_A].rearrange("p (h e) -> p h e", h=G),
                            o3[:, :, 0:VD_A], along(rz[:, 1, :], VD_A), ALU.mult).then_inc(y_ready, 1)

                    for g in range(NC):
                        weights(g)
                        if g:
                            normalise(g - 1)
                    normalise(NC - 1)
                    dve.wait_ge(yT_ready, 2 * b + 2)
                    nc.vector.tensor_copy(yT[:, BANK:], psQ[1][:, :]).then_inc(yT1_stored, 1)
                    dve.wait_ge(o_ready, b + 1)
                    xb = x[:, bass.ds(b, 1), :]
                    nc.vector.tensor_tensor(xb, xb, psY[:, 0:D], ALU.add).then_inc(added, 1)
                dve.wait_ge(added, B)


def diff_stage(nc, glob, dram):
    st = Stage(nc, "dif")
    with st.ctx:
        NM = 2
        VW = HD_S + 1
        VB = H * VW
        ln = LayerNorm(nc, st, glob)
        at = SoftmaxHeads(nc, st, glob, NM * NC, float(HD_S) ** -0.5)
        x, ctxT = glob["x"], glob["ctxT"]
        w = [st.sb(f"w{i}", [P, NC * P]) for i in range(4)]
        wv, wo, gain = st.sb("wv", [P, D]), st.sb("wo", [P, D]), st.sb("gain", [P, 1])
        v = st.sb("v", [P, B * VB + WIN])
        v4 = v[:, 0:B * VB].rearrange("p (b h e) -> p b h e", b=B, e=VW)
        qk = [st.sb(f"qkT{i}", [P, NC, S]) for i in range(4)]
        rz = st.sb("rz", [P, NM, H])
        rzg = st.sb("rz_gain", [P, H])
        m1, m2, o = (st.sb(n, [P, H, HD_S]) for n in ("map1", "map2", "o"))
        cen, sqr, oN = (st.sb(n, [P, H, HD_S]) for n in ("centred", "squares", "o_norm"))
        red = st.sb("head_sums", [P, 4, H])
        rs = st.sb("head_rstd", [P, H])
        oT = st.sb("oT", [P, S])
        psP = [at.psT[0], at.psT[1]]
        psO, psY, psF = st.ps("ps_out"), st.ps("ps_y"), ln.psX
        w_in, const_in, ones_ready = st.sem("w_in"), st.sem("const_in"), st.sem("ones_ready")
        v_proj, v_stored = st.sem("v_proj"), st.sem("v_stored")
        qk_proj, qk_stored = st.sem("qk_proj"), st.sem("qk_stored")
        rz_ready, rzg_ready = st.sem("rz_ready"), st.sem("rzg_ready")
        maps_ready, o_ready, sum_ready = st.sem("maps_ready"), st.sem("o_ready"), st.sem("sum_ready")
        mean_ready, cen_ready = st.sem("mean_ready"), st.sem("cen_ready")
        sqr_ready, var_ready, ve_ready = st.sem("sqr_ready"), st.sem("var_ready"), st.sem("ve_ready")
        rs_ready, oN_ready, oT_ready = st.sem("rs_ready"), st.sem("oN_ready"), st.sem("oT_ready")
        oT_stored, y_ready, added = st.sem("oT_stored"), st.sem("y_ready"), st.sem("added")

        def window(ap, h):
            return ap[:, h * VW:h * VW + WIN]

        with nc.Block() as block:
            @block.sync
            def _(sp):
                for i, n in enumerate(("wq1", "wk1", "wq2", "wk2")):
                    sp.dma_start(w[i][:, :], dram["L0_xattn_" + n]).then_inc(w_in, 16)
                sp.dma_start(wv[:, :], dram["L0_xattn_wv"]).then_inc(w_in, 16)
                sp.dma_start(wo[:, :], dram["L0_xattn_wo"]).then_inc(w_in, 16)
                sp.dma_start(gain[:, :], dram["L0_xattn_gain"].unsqueeze(0).to_broadcast([P, 1])).then_inc(const_in, 16)

            @block.gpsimd
            def _(pool):
                nc.gpsimd.memset(v[:, :], 1.0).then_inc(ones_ready, 1)
                ln.pool_rstd(pool)
                with pool.Fori(0, B) as b:
                    pool.wait_ge(ve_ready, b + 1)
                    nc.gpsimd.tensor_tensor(rs[:, :], red[:, 3, :], glob["mhalf"][:, 0:H],
                                            ALU.pow).then_inc(rs_ready, 1)

            @block.tensor
            def _(pe):
                at.credit(pe, at.transposed, at.values_done)
                pe.wait_ge(w_in, 96)
                for b in range(B):
                    nc.tensor.matmul(psP[b // 4][:, b % 4 * D:(b % 4 + 1) * D], ctxT[:, b, :], wv[:, :],
                                     start=True, stop=True).then_inc(v_proj, 1)
                pe.wait_ge(v_stored, 2)
                with pe.Fori(0, B) as b:
                    ln.pe_transpose(pe, b)
                    pe.wait_ge(ln.xT_ready, b + 1)
                    for i in range(4):
                        ps = (psO, psY, psP[0], psP[1])[i]
                        rhs = ln.xT[:, :] if i % 2 == 0 else ctxT[:, bass.ds(b, 1), :]
                        for c in range(NC):
                            last = nc.tensor.matmul(ps[:, c * S:(c + 1) * S], w[i][:, c * P:(c + 1) * P], rhs,
                                                    start=True, stop=True)
                        last.then_inc(qk_proj, 1)
                    pe.wait_ge(qk_stored, 4 * b + 4)

                    def scores(ps, u):
                        m, g = u // NC, u % NC
                        r = g * PAD
                        for j in range(G):
                            last = nc.tensor.matmul(ps[:, j * S:(j + 1) * S], qk[2 * m][r:r + HD_S, j, :],
                                                    qk[2 * m + 1][r:r + HD_S, j, :], start=True, stop=True)
                        return last

                    def values(probT, u):
                        m, g = u // NC, u % NC
                        for j in range(G):
                            h = g * G + j
                            last = nc.tensor.matmul(window(psO[:, m * 256:(m + 1) * 256], h), probT[j],
                                                    v[:, bass.ds(b * VB + h * VW, WIN)], start=True, stop=True)
                        return last

                    at.pe_all(pe, b, scores, values)
                    pe.wait_ge(oN_ready, b + 1)
                    nc.tensor.transpose(psF[:, 0:S], oN[:, :, :].rearrange("p h e -> p (h e)"),
                                        glob["ident"][:, :]).then_inc(oT_ready, 1)
                    pe.wait_ge(oT_stored, b + 1)
                    nc.tensor.matmul(psY[:, 0:D], oT[:, :], wo[:, :], start=True, stop=True).then_inc(y_ready, 1)

            @block.scalar
            def _(act):
                at.credit(act, at.exp_done, at.probT_done)
                with act.Fori(0, B) as b:
                    ln.act_store(act, b)
                    for i in range(4):
                        act.wait_ge(qk_proj, 4 * b + i + 1)
                        ps = (psO, psY, psP[0], psP[1])[i]
                        nc.scalar.copy(qk[i][:, :, :], ps[:, :]).then_inc(qk_stored, 1)
                    at.act_all(act, b)
                    act.wait_ge(oT_ready, b + 1)
                    nc.scalar.copy(oT[:, :], psF[:, 0:S]).then_inc(oT_stored, 1)

            @block.vector
            def _(dve):
                at.credit(dve, at.dif_done)
                ln.dve_stats(dve)
                dve.wait_ge(const_in, 16)
                dve.wait_ge(ones_ready, 1)
                for i in range(2):
                    dve.wait_ge(v_proj, 4 * i + 4)
                    for k in range(4):
                        last = nc.vector.tensor_copy(
                            v4[:, 4 * i + k, :, 0:HD_S],
                            psP[i][:, k * D:(k + 1) * D].rearrange("p (h e) -> p h e", e=HD_S))
                    last.then_inc(v_stored, 1)
                with dve.Fori(0, B) as b:
                    ln.dve_normalise(dve, b)
                    at.dve_all(dve, b)
                    o4 = psO[:, :].rearrange("p (m c) -> p m c", m=NM)[:, :, 0:VB].rearrange(
                        "p m (h e) -> p m h e", e=VW)
                    dve.wait_ge(at.values_done, NM * NC * (b + 1) + at.RING)
                    nc.vector.reciprocal(rz[:, :, :], o4[:, :, :, HD_S]).then_inc(rz_ready, 1)
                    dve.wait_ge(rz_ready, b + 1)
                    nc.vector.tensor_scalar(rzg[:, :], rz[:, 1, :], gain[:, 0:1], None,
                                            ALU.mult).then_inc(rzg_ready, 1)
                    nc.vector.tensor_tensor(m1[:, :, :], o4[:, 0, :, 0:HD_S], along(rz[:, 0, :], HD_S), ALU.mult)
                    dve.wait_ge(rzg_ready, b + 1)
                    nc.vector.tensor_tensor(m2[:, :, :], o4[:, 1, :, 0:HD_S], along(rzg[:, :], HD_S),
                                            ALU.mult).then_inc(maps_ready, 1)
                    dve.wait_ge(maps_ready, b + 1)
                    nc.vector.tensor_tensor(o[:, :, :], m1[:, :, :], m2[:, :, :], ALU.subtract).then_inc(o_ready, 1)
                    dve.wait_ge(o_ready, b + 1)
                    nc.vector.tensor_reduce(red[:, 0, :], o[:, :, :], AX, ALU.add).then_inc(sum_ready, 1)
                    dve.wait_ge(sum_ready, b + 1)
                    nc.vector.tensor_scalar(red[:, 1, :], red[:, 0, :], 1.0 / HD_S, None,
                                            ALU.mult).then_inc(mean_ready, 1)
                    dve.wait_ge(mean_ready, b + 1)
                    nc.vector.tensor_tensor(cen[:, :, :], o[:, :, :], along(red[:, 1, :], HD_S),
                                            ALU.subtract).then_inc(cen_ready, 1)
                    dve.wait_ge(cen_ready, b + 1)
                    nc.vector.tensor_tensor(sqr[:, :, :], cen[:, :, :], cen[:, :, :], ALU.mult).then_inc(sqr_ready, 1)
                    dve.wait_ge(sqr_ready, b + 1)
                    nc.vector.tensor_reduce(red[:, 2, :], sqr[:, :, :], AX, ALU.add).then_inc(var_ready, 1)
                    dve.wait_ge(var_ready, b + 1)
                    nc.vector.tensor_scalar(red[:, 3, :], red[:, 2, :], 1.0 / HD_S, LN_EPS, ALU.mult,
                                            ALU.add).then_inc(ve_ready, 1)
                    dve.wait_ge(rs_ready, b + 1)
                    nc.vector.tensor_tensor(oN[:, :, :], cen[:, :, :], along(rs[:, :], HD_S),
                                            ALU.mult).then_inc(oN_ready, 1)
                    dve.wait_ge(y_ready, b + 1)
                    xb = x[:, bass.ds(b, 1), :]
                    nc.vector.tensor_tensor(xb, xb, psY[:, 0:D], ALU.add).then_inc(added, 1)
                dve.wait_ge(added, B)


def expert_stage(nc, glob, dram):
    st = Stage(nc, "moe")
    with st.ctx:
        NT = MOE_T // P
        FC = FF // P
        ln = LayerNorm(nc, st, glob, NT)
        x = glob["x"]
        xT = st.sb("x_hat_T4", [P, MOE_T])
        xh = st.sb("x_hat4", [P, NT, D])
        w1 = [st.sb(f"w1_{i}", [P, FF]) for i in range(2)]
        w2 = [st.sb(f"w2_{i}", [P, FC, D]) for i in range(2)]
        hT = [st.sb(f"hT{i}", [P, FC, MOE_T]) for i in range(2)]
        idx = st.sb("idx", [P, NT, TOPK], I32)
        wts = st.sb("wts", [P, NT, TOPK])
        eid = st.sb("expert_ids", [P, E_EXP])
        hit = st.sb("hit", [P, NT, E_EXP, TOPK])
        share = st.sb("share", [P, NT, E_EXP, TOPK])
        gate = st.sb("gate", [P, NT, E_EXP])
        bias = st.sb("bias", [P, D])
        psH = [st.ps(f"ps_h{i}") for i in range(2)]
        psY = [st.ps(f"ps_y{i}") for i in range(2)]
        psX = st.ps("ps_x4")
        w1_in = [st.sem(f"w1_{i}_in") for i in range(2)]
        w2_in = [st.sem(f"w2_{i}_in") for i in range(2)]
        route_in, id_in, bias_in = st.sem("route_in"), st.sem("id_in"), st.sem("bias_in")
        hit_ready, share_ready, gate_ready = st.sem("hit_ready"), st.sem("share_ready"), st.sem("gate_ready")
        xh_ready, x_transposed, xT_ready = st.sem("xh4_ready"), st.sem("x_transposed"), st.sem("xT4_ready")
        h_ready, h_stored, y_ready, y_added = (st.sem("h_ready"), st.sem("h_stored"), st.sem("y_ready"),
                                               st.sem("y_added"))
        biased = st.sem("biased")

        with nc.Block() as block:
            @block.sync
            def _(sp):
                idx_v = dram["L0_ffn_expert_indices"].rearrange("(j p) k -> p j k", p=P)
                wts_v = dram["L0_ffn_expert_weights"].rearrange("(j p) k -> p j k", p=P)

                def expert(e, i):
                    sp.dma_start(w1[i][:, :], dram["L0_ffn_w1"][bass.ds(e, 1), :, :].rearrange(
                        "a p n -> p (a n)")).then_inc(w1_in[i], 16)
                    sp.dma_start(w2[i][:, :, :], dram["L0_ffn_w2"][bass.ds(e, 1), :, :].rearrange(
                        "a (c p) n -> p (a c) n", p=P)).then_inc(w2_in[i], 16)

                sp.dma_start(idx[:, :, :], idx_v).then_inc(route_in, 16)
                sp.dma_start(wts[:, :, :], wts_v).then_inc(route_in, 16)
                sp.dma_start(eid[:, :], dram["c_experts"].unsqueeze(0).to_broadcast([P, E_EXP])).then_inc(id_in, 16)
                sp.dma_start(bias[:, :], dram["L0_ffn_bias"].unsqueeze(0).to_broadcast([P, D])).then_inc(bias_in, 16)
                expert(0, 0)
                expert(1, 1)
                with sp.Fori(1, E_EXP // 2) as n:
                    for i in range(2):
                        sp.wait_ge(y_ready, 2 * n + i - 1)
                        expert(2 * n + i, i)

            @block.gpsimd
            def _(pool):
                ln.pool_rstd(pool)

            @block.tensor
            def _(pe):
                pe.wait_ge(xh_ready, NT)
                for j in range(NT):
                    last = nc.tensor.transpose(psX[:, j * S:(j + 1) * S], xh[:, j, :], glob["ident"][:, :])
                last.then_inc(x_transposed, 1)
                pe.wait_ge(xT_ready, 1)

                def up(e, i, n):
                    pe.wait_ge(w1_in[i], (n + 1) * 16)
                    for c in range(FC):
                        pe.wait_ge(h_stored, FC * e + c + 1)
                        nc.tensor.matmul(psH[c % 2][:, :], w1[i][:, c * P:(c + 1) * P], xT[:, :],
                                         start=True, stop=True).then_inc(h_ready, 1)

                def down(e, i, n):
                    pe.wait_ge(w2_in[i], (n + 1) * 16)
                    pe.wait_ge(h_stored, FC * e + FC + 2)
                    pe.wait_ge(y_added, e + 1)
                    for j in range(NT):
                        for c in range(FC):
                            last = nc.tensor.matmul(psY[i][:, j * D:(j + 1) * D], hT[i][:, c, j * P:(j + 1) * P],
                                                    w2[i][:, c, :], start=(c == 0), stop=(c == FC - 1))
                    last.then_inc(y_ready, 1)

                up(0, 0, 0)
                with pe.Fori(0, E_EXP // 2 - 1) as n:
                    up(2 * n + 1, 1, n)
                    down(2 * n, 0, n)
                    up(2 * n + 2, 0, n + 1)
                    down(2 * n + 1, 1, n)
                n = E_EXP // 2 - 1
                up(2 * n + 1, 1, n)
                down(2 * n, 0, n)
                down(2 * n + 1, 1, n)

            @block.scalar
            def _(act):
                act.sem_inc(h_stored, 2)
                act.wait_ge(x_transposed, 1)
                nc.scalar.copy(xT[:, :], psX[:, :]).then_inc(xT_ready, 1)
                with act.Fori(0, E_EXP // 2) as n:
                    for i in range(2):
                        e = 2 * n
                        act.wait_ge(y_added, e + i + 1)
                        for c in range(FC):
                            act.wait_ge(h_ready, FC * e + FC * i + c + 1)
                            nc.scalar.activation(hT[i][:, c, :], psH[c % 2][:, :], ACT.Gelu).then_inc(h_stored, 1)

            @block.vector
            def _(dve):
                dve.sem_inc(y_added, 2)
                ln.dve_stats(dve)
                dve.wait_ge(route_in, 32)
                dve.wait_ge(id_in, 16)
                for j in range(NT):
                    nc.vector.tensor_tensor(hit[:, j, :, :], over(idx[:, j, :], E_EXP), along(eid[:, :], TOPK),
                                            ALU.is_equal).then_inc(hit_ready, 1)
                for j in range(NT):
                    dve.wait_ge(hit_ready, j + 1)
                    nc.vector.tensor_tensor(share[:, j, :, :], hit[:, j, :, :], over(wts[:, j, :], E_EXP),
                                            ALU.mult).then_inc(share_ready, 1)
                dve.wait_ge(share_ready, NT)
                nc.vector.tensor_reduce(gate[:, :, :], share[:, :, :, :], AX, ALU.add).then_inc(gate_ready, 1)
                dve.wait_ge(ln.rstd_done, 1)
                for j in range(NT):
                    nc.vector.tensor_scalar(xh[:, j, :], x[:, j, :], ln.mv[:, j, 0:1], ln.rstd[:, j:j + 1],
                                            ALU.subtract, ALU.mult).then_inc(xh_ready, 1)
                dve.wait_ge(xh_ready, NT)
                dve.wait_ge(bias_in, 16)
                nc.vector.tensor_tensor(x[:, :, :], x[:, :, :], over(bias[:, :], B), ALU.add).then_inc(biased, 1)
                dve.wait_ge(biased, 1)
                dve.wait_ge(gate_ready, 1)
                with dve.Fori(0, E_EXP // 2) as n:
                    for i in range(2):
                        e = 2 * n
                        dve.wait_ge(y_ready, e + i + 1)
                        dve.wait_ge(y_added, e + i + 2)
                        for j in range(NT):
                            last = nc.vector.scalar_tensor_tensor(
                                x[:, j, :], psY[i][:, j * D:(j + 1) * D], gate[:, j, bass.ds(e + i, 1)],
                                x[:, j, :], ALU.mult, ALU.add)
                        last.then_inc(y_added, 1)
                dve.wait_ge(y_added, E_EXP + 2)


def rope_stage(nc, glob, dram):
    st = Stage(nc, "rope")
    with st.ctx:
        VW = HD_S + 1
        HALF = HD_S // 2
        ln = LayerNorm(nc, st, glob)
        at = SoftmaxHeads(nc, st, glob, NC, float(HD_S) ** -0.5)
        x = glob["x"]
        w, wo, bo = st.sb("w_qkv", [P, 3 * D]), st.sb("w_out", [P, D]), st.sb("b_out", [P, D])
        cos, sin = st.sb("cos", [P, HD_S]), st.sb("sin", [P, HD_S])
        v = st.sb("v", [P, H * VW + WIN])
        v3 = v[:, 0:H * VW].rearrange("p (h e) -> p h e", e=VW)
        rc, rsn = st.sb("rot_cos", [P, 2 * H, HD_S]), st.sb("rot_sin", [P, 2 * H, HD_S])
        pad = st.sb("qk_padded", [P, 2, NC, HC, PAD])
        qkT = [st.sb(f"qkT{i}", [P, NC, S]) for i in range(2)]
        rz, on, oT = st.sb("rz", [P, H]), st.sb("o", [P, H, HD_S]), st.sb("oT", [P, S])
        psO, psY, psF = st.ps("ps_out"), st.ps("ps_y"), ln.psX
        w_in, tab_in, bo_in = st.sem("w_in"), st.sem("tab_in"), st.sem("bo_in")
        ones_ready, zero_ready = st.sem("ones_ready"), st.sem("zero_ready")
        proj, rc_ready, rs_ready = st.sem("proj"), st.sem("rc_ready"), st.sem("rs_ready")
        v_stored, rot_ready = st.sem("v_stored"), st.sem("rot_ready")
        qk_transposed, qk_stored = st.sem("qk_transposed"), st.sem("qk_stored")
        rz_ready, on_ready, oT_ready = st.sem("rz_ready"), st.sem("o_ready"), st.sem("oT_ready")
        oT_stored, y_ready, yb_added, added = (st.sem("oT_stored"), st.sem("y_ready"), st.sem("bias_added"),
                                               st.sem("added"))

        with nc.Block() as block:
            @block.sync
            def _(sp):
                sp.dma_start(w[:, :], dram["L1_attn_w_qkv"]).then_inc(w_in, 16)
                sp.dma_start(wo[:, :], dram["L1_attn_w_out"]).then_inc(w_in, 16)
                sp.dma_start(cos[:, :], dram["c_rope8_cos"]).then_inc(tab_in, 16)
                sp.dma_start(sin[:, :], dram["c_rope8_sin"]).then_inc(tab_in, 16)
                sp.dma_start(bo[:, :], dram["L1_attn_b_out"].unsqueeze(0).to_broadcast([P, D])).then_inc(bo_in, 16)

            @block.gpsimd
            def _(pool):
                nc.gpsimd.memset(v[:, :], 1.0).then_inc(ones_ready, 1)
                nc.gpsimd.memset(pad[:, :, :, :, :].rearrange("p a c q e -> p (a c q e)"), 0.0).then_inc(zero_ready, 1)
                ln.pool_rstd(pool)

            @block.tensor
            def _(pe):
                at.credit(pe, at.transposed, at.values_done)
                pe.wait_ge(w_in, 32)
                with pe.Fori(0, B) as b:
                    ln.pe_transpose(pe, b)
                    pe.wait_ge(ln.xT_ready, b + 1)
                    nc.tensor.matmul(psO[:, 0:3 * D], ln.xT[:, :], w[:, :], start=True, stop=True).then_inc(proj, 1)
                    pe.wait_ge(rot_ready, 2 * NC * (b + 1))
                    for i in range(2):
                        for c in range(NC):
                            last = nc.tensor.transpose(at.psT[i][:, c * S:(c + 1) * S],
                                                       pad[:, i, c, :, :].rearrange("p q e -> p (q e)"),
                                                       glob["ident"][:, :])
                        last.then_inc(qk_transposed, 1)
                    pe.wait_ge(qk_stored, 2 * b + 2)
                    pe.wait_ge(v_stored, b + 1)

                    def scores(ps, g):
                        r = g * PAD
                        for j in range(G):
                            last = nc.tensor.matmul(ps[:, j * S:(j + 1) * S], qkT[0][r:r + HD_S, j, :],
                                                    qkT[1][r:r + HD_S, j, :], start=True, stop=True)
                        return last

                    def values(probT, g):
                        for j in range(G):
                            c = (g * G + j) * VW
                            last = nc.tensor.matmul(psO[:, c:c + WIN], probT[j], v[:, c:c + WIN],
                                                    start=True, stop=True)
                        return last

                    at.pe_all(pe, b, scores, values)
                    pe.wait_ge(on_ready, b + 1)
                    nc.tensor.transpose(psF[:, 0:S], on[:, :, :].rearrange("p h e -> p (h e)"),
                                        glob["ident"][:, :]).then_inc(oT_ready, 1)
                    pe.wait_ge(oT_stored, b + 1)
                    nc.tensor.matmul(psY[:, 0:D], oT[:, :], wo[:, :], start=True, stop=True).then_inc(y_ready, 1)

            @block.scalar
            def _(act):
                at.credit(act, at.exp_done, at.probT_done)
                with act.Fori(0, B) as b:
                    ln.act_store(act, b)
                    for i in range(2):
                        act.wait_ge(qk_transposed, 2 * b + i + 1)
                        nc.scalar.copy(qkT[i][:, :, :], at.psT[i][:, :]).then_inc(qk_stored, 1)
                    at.act_all(act, b)
                    act.wait_ge(oT_ready, b + 1)
                    nc.scalar.copy(oT[:, :], psF[:, 0:S]).then_inc(oT_stored, 1)

            @block.vector
            def _(dve):
                at.credit(dve, at.dif_done)
                ln.dve_stats(dve)
                dve.wait_ge(tab_in, 32)
                dve.wait_ge(bo_in, 16)
                dve.wait_ge(ones_ready, 1)
                dve.wait_ge(zero_ready, 1)
                with dve.Fori(0, B) as b:
                    ln.dve_normalise(dve, b)
                    dve.wait_ge(proj, b + 1)
                    qk3 = psO[:, 0:2 * D].rearrange("p (h e) -> p h e", e=HD_S)
                    nc.vector.tensor_tensor(rc[:, :, :], qk3, over(cos[:, :], 2 * H), ALU.mult).then_inc(rc_ready, 1)
                    nc.vector.tensor_tensor(rsn[:, :, 0:HALF], qk3[:, :, HALF:], over(sin[:, 0:HALF], 2 * H), ALU.mult)
                    nc.vector.tensor_tensor(rsn[:, :, HALF:], qk3[:, :, 0:HALF], over(sin[:, HALF:], 2 * H),
                                            ALU.mult).then_inc(rs_ready, 1)
                    nc.vector.tensor_copy(v3[:, :, 0:HD_S], psO[:, 2 * D:3 * D].rearrange(
                        "p (h e) -> p h e", e=HD_S)).then_inc(v_stored, 1)
                    dve.wait_ge(rs_ready, b + 1)
                    for i in range(2):
                        for c in range(NC):
                            hs = bass.ds(i * H + c, HC, step=NC)
                            nc.vector.tensor_tensor(pad[:, i, c, :, 0:HD_S], rc[:, hs, :], rsn[:, hs, :],
                                                    ALU.add).then_inc(rot_ready, 1)
                    at.dve_all(dve, b)
                    dve.wait_ge(at.values_done, NC * (b + 1) + at.RING)
                    o3 = psO[:, 0:H * VW].rearrange("p (h e) -> p h e", e=VW)
                    nc.vector.reciprocal(rz[:, :], o3[:, :, HD_S]).then_inc(rz_ready, 1)
                    dve.wait_ge(rz_ready, b + 1)
                    nc.vector.tensor_tensor(on[:, :, :], o3[:, :, 0:HD_S], along(rz[:, :], HD_S),
                                            ALU.mult).then_inc(on_ready, 1)
                    xb = x[:, bass.ds(b, 1), :]
                    nc.vector.tensor_tensor(xb, xb, over(bo[:, :], 1), ALU.add).then_inc(yb_added, 1)
                    dve.wait_ge(y_ready, b + 1)
                    dve.wait_ge(yb_added, b + 1)
                    nc.vector.tensor_tensor(xb, xb, psY[:, 0:D], ALU.add).then_inc(added, 1)
                dve.wait_ge(added, B)


def cross_stage(nc, glob, dram):
    st = Stage(nc, "cross")
    with st.ctx:
        ln = LayerNorm(nc, st, glob)
        x, ctxT = glob["x"], glob["ctxT"]
        SCALE = float(D) ** -0.5
        names = ("Wq_c", "Wk_s", "Wq_s", "Wk_c")
        w = [st.sb(n, [P, D]) for n in names]
        bias = [st.sb("b" + n[1:], [P, 1]) for n in names]
        wvs, wvc = st.sb("Wv_s", [P, D]), st.sb("Wv_c", [P, D])
        bv = st.sb("bv", [P, 2, D])
        wg, bg = st.sb("Wg", [P, 2, D]), st.sb("bg", [P, D])
        VW = D + 1
        vs = st.sb("v_sub", [P, B, VW])
        vc = st.sb("v_char", [P, VW])
        qk = st.sb("qkT", [P, 4, S])
        mx, nmx = st.sb("row_max", [P, 2]), st.sb("minus_max", [P, 2])
        prob, probT = st.sb("prob", [P, 2, S]), st.sb("probT", [P, 2, S])
        rz = st.sb("rz", [P, 2])
        att = st.sb("attended", [P, 2, D])
        attT = st.sb("attendedT", [P, 2, D])
        zb, ez, den, gt, df, gd = (st.sb(n, [P, D]) for n in ("gate_in", "exp_gate", "den", "gate", "delta",
                                                             "gated"))
        psV = [st.ps("ps_proj0"), st.ps("ps_proj1")]
        psS, psT, psO, psG = st.ps("ps_scores"), st.ps("ps_T"), st.ps("ps_out"), st.ps("ps_gate")
        sems = ["w_in", "b_in", "bv_in", "ones_ready", "vs_proj", "vs_stored", "qk_proj", "qk_stored", "vc_proj",
                "vc_stored", "scores_ready", "max_done", "nmax_done", "exp_done", "transposed", "probT_stored",
                "out_ready", "rz_ready", "att_ready", "att_transposed", "attT_stored", "gate_mm", "zb_ready",
                "ez_ready", "den_ready", "gt_ready", "df_ready", "gd_ready", "s_added", "added"]
        q = {n: st.sem(n) for n in sems}

        with nc.Block() as block:
            @block.sync
            def _(sp):
                for i, n in enumerate(names):
                    sp.dma_start(w[i][:, :], dram["L1_xattn_" + n]).then_inc(q["w_in"], 16)
                    sp.dma_start(bias[i][:, :], dram["L1_xattn_b" + n[1:]].unsqueeze(1)).then_inc(q["b_in"], 16)
                sp.dma_start(wvs[:, :], dram["L1_xattn_Wv_s"]).then_inc(q["w_in"], 16)
                sp.dma_start(wvc[:, :], dram["L1_xattn_Wv_c"]).then_inc(q["w_in"], 16)
                sp.dma_start(wg[:, :, :], dram["L1_xattn_Wg"].rearrange("(c p) n -> p c n", p=P)).then_inc(q["w_in"], 16)
                for i, n in enumerate(("bv_s", "bv_c")):
                    sp.dma_start(bv[:, i, :], dram["L1_xattn_" + n].unsqueeze(0).to_broadcast([P, D])).then_inc(
                        q["bv_in"], 16)
                sp.dma_start(bg[:, :], dram["L1_xattn_bg"].unsqueeze(0).to_broadcast([P, D])).then_inc(q["bv_in"], 16)

            @block.gpsimd
            def _(pool):
                nc.gpsimd.memset(vs[:, :, :].rearrange("p b e -> p (b e)"), 1.0).then_inc(q["ones_ready"], 1)
                nc.gpsimd.memset(vc[:, :], 1.0).then_inc(q["ones_ready"], 1)
                ln.pool_rstd(pool)

            @block.tensor
            def _(pe):
                pe.wait_ge(q["w_in"], 7 * 16)
                for b in range(B):
                    nc.tensor.matmul(psV[b // 4][:, b % 4 * D:(b % 4 + 1) * D], ctxT[:, b, :], wvs[:, :],
                                     start=True, stop=True).then_inc(q["vs_proj"], 1)
                pe.wait_ge(q["vs_stored"], 2)
                with pe.Fori(0, B) as b:
                    ln.pe_transpose(pe, b)
                    pe.wait_ge(ln.xT_ready, b + 1)
                    for i in range(4):
                        rhs = ln.xT[:, :] if i in (0, 3) else ctxT[:, bass.ds(b, 1), :]
                        last = nc.tensor.matmul(psV[0][:, i * S:(i + 1) * S], w[i][:, :], rhs, start=True, stop=True)
                    last.then_inc(q["qk_proj"], 1)
                    nc.tensor.matmul(psV[1][:, 0:D], ln.xT[:, :], wvc[:, :], start=True, stop=True).then_inc(
                        q["vc_proj"], 1)
                    pe.wait_ge(q["qk_stored"], 4 * b + 4)
                    for m in range(2):
                        last = nc.tensor.matmul(psS[:, m * S:(m + 1) * S], qk[:, 2 * m, :], qk[:, 2 * m + 1, :],
                                                start=True, stop=True)
                    last.then_inc(q["scores_ready"], 1)
                    pe.wait_ge(q["exp_done"], 2 * b + 2)
                    for m in range(2):
                        last = nc.tensor.transpose(psT[:, m * S:(m + 1) * S], prob[:, m, :], glob["ident"][:, :])
                    last.then_inc(q["transposed"], 1)
                    pe.wait_ge(q["probT_stored"], b + 1)
                    pe.wait_ge(q["vc_stored"], b + 1)
                    nc.tensor.matmul(psO[:, 0:VW], probT[:, 0, :], vs[:, bass.ds(b, 1), :], start=True, stop=True)
                    nc.tensor.matmul(psO[:, 256:256 + VW], probT[:, 1, :], vc[:, :], start=True,
                                     stop=True).then_inc(q["out_ready"], 1)
                    pe.wait_ge(q["att_ready"], 2 * b + 2)
                    for m in range(2):
                        last = nc.tensor.transpose(psT[:, m * S:(m + 1) * S], att[:, m, :], glob["ident"][:, :])
                    last.then_inc(q["att_transposed"], 1)
                    pe.wait_ge(q["attT_stored"], b + 1)
                    for m in range(2):
                        last = nc.tensor.matmul(psG[:, 0:D], attT[:, m, :], wg[:, m, :], start=(m == 0), stop=(m == 1))
                    last.then_inc(q["gate_mm"], 1)

            @block.scalar
            def _(act):
                act.wait_ge(q["b_in"], 64)
                with act.Fori(0, B) as b:
                    ln.act_store(act, b)
                    act.wait_ge(q["qk_proj"], b + 1)
                    for i in range(4):
                        nc.scalar.activation(qk[:, i, :], psV[0][:, i * S:(i + 1) * S], ACT.Identity,
                                             bias=bias[i][:, 0:1]).then_inc(q["qk_stored"], 1)
                    act.wait_ge(q["nmax_done"], b + 1)
                    for m in range(2):
                        nc.scalar.activation(prob[:, m, :], psS[:, m * S:(m + 1) * S], ACT.Exp, bias=nmx[:, m:m + 1],
                                             scale=SCALE).then_inc(q["exp_done"], 1)
                    act.wait_ge(q["transposed"], b + 1)
                    nc.scalar.copy(probT[:, :, :], psT[:, 0:2 * S]).then_inc(q["probT_stored"], 1)
                    act.wait_ge(q["att_transposed"], b + 1)
                    nc.scalar.copy(attT[:, :, :], psT[:, 0:2 * S]).then_inc(q["attT_stored"], 1)
                    act.wait_ge(q["zb_ready"], b + 1)
                    nc.scalar.activation(ez[:, :], zb[:, :], ACT.Exp, scale=-1.0).then_inc(q["ez_ready"], 1)

            @block.vector
            def _(dve):
                def then(ins, name, b):
                    ins.then_inc(q[name], 1)
                    dve.wait_ge(q[name], b + 1)

                ln.dve_stats(dve)
                dve.wait_ge(q["ones_ready"], 2)
                dve.wait_ge(q["bv_in"], 48)
                for i in range(2):
                    dve.wait_ge(q["vs_proj"], 4 * i + 4)
                    nc.vector.tensor_copy(vs[:, 4 * i:4 * i + 4, 0:D],
                                          psV[i][:, :].rearrange("p (b e) -> p b e", b=4)).then_inc(q["vs_stored"], 1)
                with dve.Fori(0, B) as b:
                    ln.dve_normalise(dve, b)
                    dve.wait_ge(q["vc_proj"], b + 1)
                    nc.vector.tensor_copy(vc[:, 0:D], psV[1][:, 0:D]).then_inc(q["vc_stored"], 1)
                    dve.wait_ge(q["scores_ready"], b + 1)
                    then(nc.vector.tensor_reduce(mx[:, :], psS[:, 0:2 * S].rearrange("p (m t) -> p m t", m=2), AX,
                                                 ALU.max), "max_done", b)
                    nc.vector.tensor_scalar(nmx[:, :], mx[:, :], -SCALE, None, ALU.mult).then_inc(q["nmax_done"], 1)
                    dve.wait_ge(q["out_ready"], b + 1)
                    o3 = psO[:, :].rearrange("p (m c) -> p m c", m=2)
                    then(nc.vector.reciprocal(rz[:, :], o3[:, :, D]), "rz_ready", b)
                    for m in range(2):
                        nc.vector.scalar_tensor_tensor(att[:, m, :], o3[:, m, 0:D], rz[:, m:m + 1], bv[:, m, :],
                                                       ALU.mult, ALU.add).then_inc(q["att_ready"], 1)
                    dve.wait_ge(q["att_ready"], 2 * b + 2)
                    nc.vector.tensor_tensor(df[:, :], att[:, 0, :], att[:, 1, :], ALU.subtract).then_inc(
                        q["df_ready"], 1)
                    xb = x[:, bass.ds(b, 1), :]
                    nc.vector.tensor_tensor(xb, xb, over(att[:, 1, :], 1), ALU.add).then_inc(q["s_added"], 1)
                    dve.wait_ge(q["gate_mm"], b + 1)
                    nc.vector.tensor_tensor(zb[:, :], psG[:, 0:D], bg[:, :], ALU.add).then_inc(q["zb_ready"], 1)
                    dve.wait_ge(q["ez_ready"], b + 1)
                    then(nc.vector.tensor_scalar(den[:, :], ez[:, :], 1.0, None, ALU.add), "den_ready", b)
                    then(nc.vector.reciprocal(gt[:, :], den[:, :]), "gt_ready", b)
                    dve.wait_ge(q["df_ready"], b + 1)
                    then(nc.vector.tensor_tensor(gd[:, :], gt[:, :], df[:, :], ALU.mult), "gd_ready", b)
                    dve.wait_ge(q["s_added"], b + 1)
                    nc.vector.tensor_tensor(xb, xb, over(gd[:, :], 1), ALU.add).then_inc(q["added"], 1)
                dve.wait_ge(q["added"], B)


class Signal:

    CREDIT = 2

    def __init__(self, st, name, eng, by_engine):
        self.sem = st.sem(name)
        by_engine.setdefault(eng, []).append(self)

    def seen(self, n):
        return n + 1 + self.CREDIT

    def prior(self, n):
        return n + self.CREDIT

    def freed(self, n):
        return n - 1 + self.CREDIT


def local_stage(nc, glob, dram):
    st = Stage(nc, "loc")
    with st.ctx:
        x, ident = glob["x"], glob["ident"]
        C4 = 2 * INNER // BANK
        VC = INNER // BANK
        HP = BANK // HD_F
        QC = INNER // P
        NG = H // G
        VW = HD_F + 1
        HALF = HD_F // 2
        DH = D // 2
        FCH = [P, P, DI - 2 * P]
        wqkv, wo = st.sb("w_qkv", [P, 3 * INNER]), st.sb("w_o", [P, QC, D])
        w1, w2 = st.sb("w1", [P, 2 * DI]), st.sb("w2", [P, 3, D])
        b1, lng, b2 = st.sb("b1", [P, 2, 3]), st.sb("ln_gb", [P, 2]), st.sb("b2", [P, D])
        shift = st.sb("shift", [P, P])
        band = st.sb("band", [P, S])
        identb, maskb = st.sb("ident_bf", [P, P], BF16), st.sb("mask_bf", [P, BANK], BF16)
        rotc, qks, rot = (st.sb(n, [P, 2, 2 * HD_F]) for n in ("rot_const", "qk_scale", "rot"))
        xin = st.sb("x_in", [P, D])
        xsT = [st.sb(f"xsT{i}", [P, S]) for i in range(2)]
        raw, sq, t1, t2, sm, qn = ([st.sb(f"{n}{i}", [P, HP, HD_F]) for i in range(2)]
                                   for n in ("raw", "squares", "rot_a", "rot_b", "rotated", "qk_norm"))
        ssq, ssc, rn = ([st.sb(f"{n}{i}", [P, HP]) for i in range(2)] for n in ("ssq", "ssq_max", "r_norm"))
        qT = [st.sb(f"qT{i}", [P, QC, S]) for i in range(2)]
        kT = [st.sb(f"kT{i}", [P, 2, QC, S]) for i in range(2)]
        v = [st.sb(f"v{i}", [P, H * VW + WIN]) for i in range(2)]
        v3 = [a[:, 0:H * VW].rearrange("p (h e) -> p h e", e=VW) for a in v]
        mx = [st.sb(f"row_max{i}", [P, G]) for i in range(2)]
        dif, prob, probT = ([st.sb(f"{n}{i}", [P, BANK]) for i in range(2)] for n in ("dif", "prob", "probT"))
        rz = st.sb("rz", [P, G])
        y, yT = st.sb("y", [P, INNER]), st.sb("yT", [P, INNER])
        xs, xh = st.sb("xs", [P, B, D]), st.sb("x_hat", [P, B, D])
        stats, mv = st.sb("stats", [P, B, 6]), st.sb("mv", [P, B, 2])
        ve, rstd = st.sb("var_eps", [P, B]), st.sb("rstd", [P, B])
        xnT = st.sb("xnT", [P, B * S])
        gl = [st.sb(f"gelu{i}", [P, BANK]) for i in range(2)]
        hT = st.sb("hT", [P, 3, BANK])
        bank = [st.ps(f"bank{i}") for i in range(8)]
        psX, psQ, psS, psTP, psTQ, psO = bank[0], bank[1:3], bank[3:5], bank[5], bank[6], bank[7]
        psY = psX

        x0 = st.sb("x_before", [P, B, D])
        in_stats, in_mv, in_ve, in_rstd = (st.sem(n) for n in ("in_stats", "in_mv", "in_var_eps", "in_rstd"))
        x0_kept = st.sem("x0_kept")
        own = {}

        def sig(name, eng):
            return Signal(st, name, eng, own)

        const_in, wa_in, wf_in = st.sem("const_in"), st.sem("w_attn_in"), st.sem("w_ffn_in")
        band_in, bf_ready = st.sem("band_in"), st.sem("bf_ready")
        ones_ready, zeros_ready = st.sem("ones_ready"), st.sem("zeros_ready")
        rot_ready = sig("rot_ready", "dve")
        xin_ready = sig("xin_ready", "pool")
        psx_ready, xsT_ready = sig("psx_ready", "pe"), sig("xsT_ready", "act")
        psq_ready, psq_read = sig("psq_ready", "pe"), sig("psq_read", "act")
        raw_ready, rotab_ready = sig("raw_ready", "act"), sig("rotab_ready", "dve")
        ssq_ready, ssc_ready = sig("ssq_ready", "dve"), sig("ssc_ready", "dve")
        sum_ready, rn_ready, qn_ready = sig("sum_ready", "pool"), sig("rn_ready", "pool"), sig("qn_ready", "dve")
        qk_transposed, qk_stored = sig("qk_transposed", "pe"), sig("qk_stored", "act")
        v_stored = sig("v_stored", "act")
        scores_ready, max_ready, dif_ready = sig("scores_ready", "pe"), sig("max_ready", "dve"), sig("dif_ready", "dve")
        exp_ready, p_transposed, p_stored = sig("exp_ready", "act"), sig("p_transposed", "pe"), sig("p_stored", "act")
        out_ready, rz_ready, y_ready = sig("out_ready", "pe"), sig("rz_ready", "dve"), sig("y_ready", "dve")
        yT_stored, o_ready, added = sig("yT_stored", "act"), sig("o_ready", "pe"), sig("added", "dve")
        sh_ready, xs0_ready, xs1_ready = sig("sh_ready", "pe"), sig("xs0_ready", "pool"), sig("xs1_ready", "act")
        stats_ready, mv_ready, ve_ready = sig("stats_ready", "dve"), sig("mv_ready", "dve"), sig("ve_ready", "dve")
        rstd_ready, xh_ready, b2_added = sig("rstd_ready", "pool"), sig("xh_ready", "dve"), sig("b2_added", "dve")
        xh_transposed, xnT_ready = sig("xh_transposed", "pe"), sig("xnT_ready", "act")
        up_ready, gelu_ready, h_ready = sig("up_ready", "pe"), sig("gelu_ready", "act"), sig("h_ready", "dve")
        down_ready, f_added = sig("down_ready", "pe"), sig("f_added", "dve")

        def load_attn(sp, l):
            sp.dma_start(wqkv[:, :], dram["L1_ffn_Wqkv"][bass.ds(l, 1), :, :].rearrange("a p n -> p (a n)")).then_inc(
                wa_in, 16)
            sp.dma_start(wo[:, :, :], dram["L1_ffn_Wo"][bass.ds(l, 1), :, :].rearrange(
                "a (c p) n -> p (a c) n", p=P)).then_inc(wa_in, 16)
            sp.dma_start(qks[:, :, :], dram["qk_scale"][bass.ds(l, 1), :].to_broadcast([P, 4 * HD_F])).then_inc(
                wa_in, 16)

        def load_ffn(sp, l):
            sp.dma_start(w1[:, :], dram["L1_ffn_W1"][bass.ds(l, 1), :, :].rearrange("a p n -> p (a n)")).then_inc(
                wf_in, 16)
            sp.dma_start(w2[:, :, :], dram["L1_ffn_W2"][bass.ds(l, 1), :, :].rearrange(
                "a (c p) n -> p (a c) n", p=P)).then_inc(wf_in, 16)
            sp.dma_start(b1[:, :, :], dram["L1_ffn_b1"][bass.ds(l, 1), :, :].rearrange(
                "a p n -> p (a n)")).then_inc(wf_in, 16)
            sp.dma_start(lng[:, :], dram["ln_gb"][bass.ds(l, 1), :, :].rearrange("a p n -> p (a n)")).then_inc(
                wf_in, 16)
            sp.dma_start(b2[:, :], dram["L1_ffn_b2"][bass.ds(l, 1), :].to_broadcast([P, D])).then_inc(wf_in, 16)

        with nc.Block() as block:
            @block.sync
            def _(sp):
                sp.dma_start(shift[:, :], dram["c_shift"]).then_inc(const_in, 16)
                sp.dma_start(rotc[:, :, :], dram["c_rot"]).then_inc(const_in, 16)
                load_attn(sp, 0)
                sp.dma_start(band[:, :], dram["c_band"]).then_inc(band_in, 16)
                sp.wait_ge(const_in, 32)

            @block.gpsimd
            def _(pool):
                for i in range(2):
                    nc.gpsimd.memset(v[i][:, :], 1.0).then_inc(ones_ready, 1)
                for i in range(2):
                    nc.gpsimd.memset(kT[i][:, :, :, :].rearrange("p r c n -> p (r c n)"), 0.0).then_inc(zeros_ready, 1)
                for s in own["pool"]:
                    pool.sem_inc(s.sem, s.CREDIT)
                pool.wait_ge(in_ve, 1)
                nc.gpsimd.tensor_tensor(rstd[:, :], ve[:, :], glob["mhalf"][:, 0:B], ALU.pow).then_inc(in_rstd, 1)
                pool.wait_ge(ones_ready, 2)

            @block.tensor
            def _(pe):
                for s in own["pe"]:
                    pe.sem_inc(s.sem, s.CREDIT)

            @block.scalar
            def _(act):
                for s in own["act"]:
                    act.sem_inc(s.sem, s.CREDIT)
                nc.scalar.copy(x0[:, :, :], x[:, :, :]).then_inc(x0_kept, 1)
                nc.scalar.copy(identb[:, :], ident[:, :]).then_inc(bf_ready, 1)
                act.wait_ge(band_in, 16)
                nc.scalar.copy(maskb[:, :].rearrange("p (h m) -> p h m", h=G), over(band[:, :], G)).then_inc(
                    bf_ready, 1)

            @block.vector
            def _(dve):
                for s in own["dve"]:
                    dve.sem_inc(s.sem, s.CREDIT)
                for b in range(B):
                    nc.vector.bn_stats(stats[:, b, :], x[:, b, :]).then_inc(in_stats, 1)
                for b in range(B):
                    dve.wait_ge(in_stats, b + 1)
                    nc.vector.bn_aggr(mv[:, b, :], stats[:, b, :]).then_inc(in_mv, 1)
                dve.wait_ge(in_mv, B)
                nc.vector.tensor_scalar(ve[:, :], mv[:, :, 1], LN_EPS, None, ALU.add).then_inc(in_ve, 1)
                dve.wait_ge(in_rstd, 1)
                dve.wait_ge(x0_kept, 1)
                for b in range(B):
                    nc.vector.tensor_scalar(x[:, b, :], x[:, b, :], mv[:, b, 0:1], rstd[:, b:b + 1],
                                            ALU.subtract, ALU.mult)

        ORDER = [(1, "qk3"), (2, "qk0"), (2, "qk1"), (-1, "y0"), (-1, "y1"), (1, "v0"), (2, "qk2"), (1, "v1")]
        FIRST, LAST = -2, B
        LOOP = (1, 5)

        def uses_before(b, what):
            n = 0
            for step in range(FIRST, LAST + 1):
                for off, name in ORDER:
                    if step == b and name == what:
                        return n
                    n += 0 <= step + off < B

        def use(l, b, what):
            at = uses_before(b, what) if isinstance(b, int) else (
                uses_before(LOOP[0], what) + (b - LOOP[0]) * len(ORDER))
            return l * (B * len(ORDER)) + at

        def bank_of(parity_step, what):
            return psQ[uses_before(parity_step, what) % 2]

        def pipeline(eng, slots):
            for b in range(FIRST, LOOP[0]):
                slots(b, b % 2, b)
            with eng.Fori(0, (LOOP[1] - LOOP[0]) // 2) as n:
                for i in range(2):
                    slots(2 * n + (LOOP[0] + i), (LOOP[0] + i) % 2, LOOP[0] + i)
            for b in range(LOOP[1], LAST + 1):
                slots(b, b % 2, b)

        def there(b, off):
            return not isinstance(b, int) or 0 <= b + off < B

        def lag(b, g, n):
            return (0, g - n) if 0 <= g - n < 4 else ((-1, g - n + 4) if g < n else (1, g - n - 4))

        PIECE_LEAD = 7

        def piece_at(g, behind=0):
            n = g + PIECE_LEAD - behind
            return n // 4, n % 4

        def attention(l):
            with nc.Block() as block:
                @block.sync
                def _(sp):
                    load_ffn(sp, l)

                @block.gpsimd
                def _(pool):
                    def front(b, k):
                        n = (l * B + b) * C4 + k
                        i = k % 2
                        pool.wait_ge(rotab_ready.sem, rotab_ready.seen(n))
                        pool.wait_ge(qn_ready.sem, qn_ready.freed(n))
                        nc.gpsimd.tensor_tensor(sm[i][:, :, :], t1[i][:, :, :], t2[i][:, :, :],
                                                ALU.add).then_inc(sum_ready.sem, 1)
                        pool.wait_ge(ssc_ready.sem, ssc_ready.seen(n))
                        nc.gpsimd.tensor_tensor(rn[i][:, :], ssc[i][:, :], glob["mhalf"][:, 0:HP],
                                                ALU.pow).then_inc(rn_ready.sem, 1)

                    def slots(b, p, sb):
                        for g in range(NG):
                            if g == 0 and there(b, 2):
                                nc.gpsimd.tensor_copy(xin[:, :], x[:, bass.ds(b + 2, 1), :]).then_inc(
                                    xin_ready.sem, 1)
                            off, k = piece_at(g)
                            if there(b, off):
                                front(b + off, k)

                    pipeline(pool, slots)

                @block.tensor
                def _(pe):
                    pe.wait_ge(wa_in, (l + 1) * 48)

                    def shifted(b, full):
                        t = l * B + b
                        if full:
                            pe.wait_ge(added.sem, added.seen(t - 4))
                        pe.wait_ge(xin_ready.sem, xin_ready.seen(t))
                        nc.tensor.matmul(psX[0:DH, 0:S], xin[:, 0:DH], ident[:, :], start=True, stop=True)
                        nc.tensor.matmul(psX[DH:D, 0:S], xin[:, DH:D], shift[:, :], start=True,
                                         stop=True).then_inc(psx_ready.sem, 1)

                    def project(b, sb, off, what, p, k):
                        if what == "qk0":
                            pe.wait_ge(xsT_ready.sem, xsT_ready.seen(l * B + b + off))
                        pe.wait_ge(psq_read.sem, psq_read.freed(use(l, b, what)))
                        nc.tensor.matmul(bank_of(sb, what)[:, :], xsT[p][:, :], wqkv[:, k * BANK:(k + 1) * BANK],
                                         start=True, stop=True).then_inc(psq_ready.sem, 1)

                    def turn_qk(b, k):
                        n = (l * B + b) * C4 + k
                        pe.wait_ge(qn_ready.sem, qn_ready.seen(n))
                        pe.wait_ge(qk_stored.sem, qk_stored.prior(n))
                        for c in range(4):
                            last = nc.tensor.transpose(psTQ[:, c * S:(c + 1) * S],
                                                       qn[k % 2][:, 2 * c:2 * c + 2, :].rearrange("p h e -> p (h e)"),
                                                       ident[:, :])
                        last.then_inc(qk_transposed.sem, 1)

                    def scores(b, p, g):
                        n = (l * B + b) * NG + g
                        if g == 0:
                            pe.wait_ge(qk_stored.sem, qk_stored.seen((l * B + b) * C4 + C4 - 1))
                        pe.wait_ge(dif_ready.sem, dif_ready.freed(n))
                        ps = psS[g % 2]
                        nc.tensor.matmul(ps[:, :], identb[:, :], maskb[:, :], start=True, stop=False)
                        for j in range(G):
                            c = g % 2 * G + j
                            last = nc.tensor.matmul(ps[:, j * S:(j + 1) * S], qT[p][:, c, :],
                                                    kT[p][:, g // 2, c, :], start=False, stop=(j == G - 1))
                        last.then_inc(scores_ready.sem, 1)

                    def turn_p(b, g):
                        n = (l * B + b) * NG + g
                        pe.wait_ge(exp_ready.sem, exp_ready.seen(n))
                        pe.wait_ge(p_stored.sem, p_stored.prior(n))
                        for j in range(G):
                            last = nc.tensor.transpose(psTP[:, j * S:(j + 1) * S],
                                                       prob[g % 2][:, j * S:(j + 1) * S], ident[:, :])
                        last.then_inc(p_transposed.sem, 1)

                    def values(b, p, g):
                        n = (l * B + b) * NG + g
                        pe.wait_ge(p_stored.sem, p_stored.seen(n))
                        pe.wait_ge(y_ready.sem, y_ready.prior(n))
                        if g == 0:
                            pe.wait_ge(v_stored.sem, v_stored.seen((l * B + b) * VC + VC - 1))
                        for j in range(G):
                            c = (g * G + j) * VW
                            last = nc.tensor.matmul(psO[:, j * S:j * S + WIN], probT[g % 2][:, j * S:(j + 1) * S],
                                                    v[p][:, c:c + WIN], start=True, stop=True)
                        last.then_inc(out_ready.sem, 1)

                    def turn_y(b, sb, i):
                        what = f"y{i}"
                        pe.wait_ge(psq_read.sem, psq_read.freed(use(l, b, what)))
                        pe.wait_ge(y_ready.sem, y_ready.seen((l * B + b - 1) * NG + 2 * i + 1))
                        for c in range(4):
                            cc = 4 * i + c
                            last = nc.tensor.transpose(bank_of(sb, what)[:, c * S:(c + 1) * S],
                                                       y[:, cc * P:(cc + 1) * P], ident[:, :])
                        last.then_inc(psq_ready.sem, 1)

                    def output(b):
                        t = l * B + b
                        pe.wait_ge(yT_stored.sem, yT_stored.seen(2 * t + 1))
                        for c in range(QC):
                            last = nc.tensor.matmul(psY[:, 0:D], yT[:, c * P:(c + 1) * P], wo[:, c, :],
                                                    start=(c == 0), stop=(c == QC - 1))
                        last.then_inc(o_ready.sem, 1)

                    def slots(b, p, sb):
                        for g in range(NG):
                            if g == 0 and there(b, 2):
                                shifted(b + 2, sb >= LOOP[0])
                            off, k = piece_at(g)
                            if there(b, off):
                                project(b, sb, off, f"qk{k}", (p + off) % 2, k)
                            off, k = lag(b, g, 1)
                            if there(b, off):
                                turn_p(b + off, k)
                            off, k = lag(b, g, -1)
                            if there(b, off):
                                scores(b + off, (p + off) % 2, k)
                            off, k = piece_at(g, 2)
                            if there(b, off):
                                turn_qk(b + off, k)
                            off, k = lag(b, g, 2)
                            if there(b, off):
                                values(b + off, (p + off) % 2, k)
                            if g == 2:
                                if there(b, -1):
                                    turn_y(b, sb, 0)
                                    turn_y(b, sb, 1)
                                if there(b, 1):
                                    project(b, sb, 1, "v0", (p + 1) % 2, C4)
                            if g == 3:
                                if there(b, 1):
                                    project(b, sb, 1, "v1", (p + 1) % 2, C4 + 1)
                                if there(b, -1):
                                    output(b - 1)

                    pipeline(pe, slots)

                @block.scalar
                def _(act):
                    def store_x(b, p):
                        t = l * B + b
                        act.wait_ge(psx_ready.sem, psx_ready.seen(t))
                        nc.scalar.copy(xsT[p][:, :], psX[:, 0:S]).then_inc(xsT_ready.sem, 1)

                    def store_raw(b, sb, off, k):
                        n = (l * B + b + off) * C4 + k
                        what = f"qk{k}"
                        act.wait_ge(psq_ready.sem, psq_ready.seen(use(l, b, what)))
                        act.wait_ge(rotab_ready.sem, rotab_ready.freed(n))
                        nc.scalar.copy(raw[k % 2][:, :, :], bank_of(sb, what)[:, :]).then_inc(raw_ready.sem, 1)
                        act.wait_ge(ssq_ready.sem, ssq_ready.freed(n))
                        nc.scalar.square(sq[k % 2][:, :, :], bank_of(sb, what)[:, :]).then_inc(psq_read.sem, 1)

                    def store_v(b, sb, p, i):
                        u = use(l, b, f"v{i}")
                        act.wait_ge(psq_ready.sem, psq_ready.seen(u))
                        nc.scalar.copy(v3[p][:, i * HP:(i + 1) * HP, 0:HD_F],
                                       bank_of(sb, f"v{i}")[:, :].rearrange("p (h e) -> p h e", h=HP)).then_inc(
                            psq_read.sem, 1)
                        act.wait_ge(psq_read.sem, psq_read.seen(u))
                        act.sem_inc(v_stored.sem, 1)

                    def store_qk(b, p, k):
                        n = (l * B + b) * C4 + k
                        c = k % 2 * 4
                        act.wait_ge(qk_transposed.sem, qk_transposed.seen(n))
                        if k < 2:
                            nc.scalar.copy(qT[p][:, c:c + 4, :], psTQ[:, :]).then_inc(qk_stored.sem, 1)
                        else:
                            nc.scalar.copy(kT[p][0:HD_F, 0, c:c + 4, :], psTQ[0:HD_F, :])
                            nc.scalar.copy(kT[p][HD_F:P, 1, c:c + 4, :], psTQ[HD_F:P, :]).then_inc(qk_stored.sem, 1)

                    def exponent(b, g):
                        n = (l * B + b) * NG + g
                        act.wait_ge(dif_ready.sem, dif_ready.seen(n))
                        act.wait_ge(p_transposed.sem, p_transposed.freed(n))
                        nc.scalar.activation(prob[g % 2][:, :], dif[g % 2][:, :], ACT.Exp).then_inc(exp_ready.sem, 1)

                    def store_p(b, g):
                        n = (l * B + b) * NG + g
                        act.wait_ge(p_transposed.sem, p_transposed.seen(n))
                        act.wait_ge(out_ready.sem, out_ready.freed(n))
                        nc.scalar.copy(probT[g % 2][:, :], psTP[:, :]).then_inc(p_stored.sem, 1)

                    def store_y(b, sb, i):
                        u = use(l, b, f"y{i}")
                        act.wait_ge(psq_ready.sem, psq_ready.seen(u))
                        nc.scalar.copy(yT[:, i * BANK:(i + 1) * BANK], bank_of(sb, f"y{i}")[:, :]).then_inc(
                            psq_read.sem, 1)
                        act.wait_ge(psq_read.sem, psq_read.seen(u))
                        act.sem_inc(yT_stored.sem, 1)

                    act.wait_ge(zeros_ready, 2)

                    def slots(b, p, sb):
                        for g in range(NG):
                            if g == 0 and there(b, 2):
                                store_x(b + 2, p)
                            off, k = piece_at(g)
                            if there(b, off):
                                store_raw(b, sb, off, k)
                            off, k = lag(b, g, 0)
                            if there(b, off):
                                exponent(b + off, k)
                            off, k = lag(b, g, 1)
                            if there(b, off):
                                store_p(b + off, k)
                            off, k = piece_at(g, 2)
                            if there(b, off):
                                store_qk(b + off, (p + off) % 2, k)
                            if g == 2:
                                if there(b, -1):
                                    store_y(b, sb, 0)
                                    store_y(b, sb, 1)
                                if there(b, 1):
                                    store_v(b, sb, (p + 1) % 2, 0)
                            if g == 3 and there(b, 1):
                                store_v(b, sb, (p + 1) % 2, 1)

                    pipeline(act, slots)

                @block.vector
                def _(dve):
                    dve.wait_ge(wa_in, (l + 1) * 48)
                    nc.vector.tensor_tensor(rot[:, :, :], rotc[:, :, :], qks[:, :, :], ALU.mult).then_inc(
                        rot_ready.sem, 1)
                    dve.wait_ge(rot_ready.sem, rot_ready.seen(l))

                    def rotate(b, k):
                        n = (l * B + b) * C4 + k
                        i, kind = k % 2, k // 2
                        cos, sin = rot[:, kind, 0:HD_F], rot[:, kind, HD_F:]
                        dve.wait_ge(raw_ready.sem, raw_ready.seen(n))
                        dve.wait_ge(sum_ready.sem, sum_ready.freed(n))
                        nc.vector.tensor_tensor(t1[i][:, :, :], raw[i][:, :, :], over(cos, HP), ALU.mult)
                        nc.vector.tensor_tensor(t2[i][:, :, 0:HALF], raw[i][:, :, HALF:], over(sin[:, 0:HALF], HP),
                                                ALU.mult)
                        nc.vector.tensor_tensor(t2[i][:, :, HALF:], raw[i][:, :, 0:HALF], over(sin[:, HALF:], HP),
                                                ALU.mult).then_inc(rotab_ready.sem, 1)

                    def norms(b, off, k):
                        n = (l * B + b + off) * C4 + k
                        i = k % 2
                        dve.wait_ge(psq_read.sem, psq_read.seen(use(l, b, f"qk{k}")))
                        nc.vector.tensor_reduce(ssq[i][:, :], sq[i][:, :, :], AX, ALU.add).then_inc(ssq_ready.sem, 1)
                        dve.wait_ge(ssq_ready.sem, ssq_ready.seen(n))
                        dve.wait_ge(rn_ready.sem, rn_ready.freed(n))
                        nc.vector.tensor_scalar(ssc[i][:, :], ssq[i][:, :], 1e-24, None, ALU.max).then_inc(
                            ssc_ready.sem, 1)

                    def scale_qk(b, k):
                        n = (l * B + b) * C4 + k
                        i = k % 2
                        dve.wait_ge(sum_ready.sem, sum_ready.seen(n))
                        dve.wait_ge(rn_ready.sem, rn_ready.seen(n))
                        dve.wait_ge(qk_transposed.sem, qk_transposed.freed(n))
                        nc.vector.tensor_tensor(qn[i][:, :, :], sm[i][:, :, :], along(rn[i][:, :], HD_F),
                                                ALU.mult).then_inc(qn_ready.sem, 1)

                    def less_max(b, g):
                        n = (l * B + b) * NG + g
                        i = g % 2
                        s3 = psS[i][:, :].rearrange("p (h m) -> p h m", h=G)
                        dve.wait_ge(scores_ready.sem, scores_ready.seen(n))
                        nc.vector.tensor_reduce(mx[i][:, :], s3, AX, ALU.max).then_inc(max_ready.sem, 1)
                        dve.wait_ge(exp_ready.sem, exp_ready.freed(n))
                        dve.wait_ge(max_ready.sem, max_ready.seen(n))
                        nc.vector.tensor_tensor(dif[i][:, :].rearrange("p (h m) -> p h m", h=G), s3,
                                                along(mx[i][:, :], S), ALU.subtract).then_inc(dif_ready.sem, 1)

                    def normalise(b, g):
                        n = (l * B + b) * NG + g
                        o3 = psO[:, :].rearrange("p (h e) -> p h e", h=G)
                        dve.wait_ge(out_ready.sem, out_ready.seen(n))
                        nc.vector.reciprocal(rz[:, :], o3[:, :, HD_F]).then_inc(rz_ready.sem, 1)
                        dve.wait_ge(rz_ready.sem, rz_ready.seen(n))
                        if g % 2 == 0:
                            dve.wait_ge(yT_stored.sem, yT_stored.prior(2 * (l * B + b) + g // 2) - 1)
                        nc.vector.tensor_tensor(
                            y[:, g * G * HD_F:(g + 1) * G * HD_F].rearrange("p (h e) -> p h e", h=G),
                            o3[:, :, 0:HD_F], along(rz[:, :], HD_F), ALU.mult).then_inc(y_ready.sem, 1)

                    def slots(b, p, sb):
                        for g in range(NG):
                            off, k = lag(b, g, 0)
                            if there(b, off):
                                less_max(b + off, k)
                            off, k = piece_at(g)
                            if there(b, off):
                                rotate(b + off, k)
                                norms(b, off, k)
                            off, k = piece_at(g, 1)
                            if there(b, off):
                                scale_qk(b + off, k)
                            off, k = lag(b, g, 2)
                            if there(b, off):
                                normalise(b + off, k)
                        if there(b, -1):
                            t = l * B + b - 1
                            dve.wait_ge(o_ready.sem, o_ready.seen(t))
                            xb = x[:, bass.ds(b - 1, 1), :]
                            nc.vector.tensor_tensor(xb, xb, psY[:, 0:D], ALU.add).then_inc(added.sem, 1)

                    pipeline(dve, slots)

        def feed_forward(l, prefetch):
            psF, psT2, psUp, psDn = bank[0], bank[1:3], bank[3:7], bank[7]
            with nc.Block() as block:
                @block.sync
                def _(sp):
                    if prefetch:
                        load_attn(sp, l + 1)

                @block.gpsimd
                def _(pool):
                    nc.gpsimd.tensor_copy(xs[:, :, 0:DH], x[:, :, 0:DH]).then_inc(xs0_ready.sem, 1)
                    pool.wait_ge(ve_ready.sem, ve_ready.seen(l))
                    nc.gpsimd.tensor_tensor(rstd[:, :], ve[:, :], glob["mhalf"][:, 0:B], ALU.pow).then_inc(
                        rstd_ready.sem, 1)

                @block.tensor
                def _(pe):
                    nc.tensor.matmul(psF[:, :], shift[:, :], x[:, :, DH:D], start=True, stop=True).then_inc(
                        sh_ready.sem, 1)
                    for i in range(2):
                        pe.wait_ge(xh_ready.sem, xh_ready.seen(l * B + 4 * i + 3))
                        for k in range(4):
                            last = nc.tensor.transpose(psT2[i][:, k * S:(k + 1) * S], xh[:, 4 * i + k, :], ident[:, :])
                        last.then_inc(xh_transposed.sem, 1)
                    pe.wait_ge(wf_in, (l + 1) * 80)

                    def up(i, c):
                        n = (l * 2 + i) * 3 + c
                        if c == 0:
                            pe.wait_ge(xnT_ready.sem, xnT_ready.seen(2 * l + i))
                        pe.wait_ge(h_ready.sem, h_ready.freed(n))
                        r = (3 * i + c) % 2
                        for a in range(2):
                            o = a * DI + c * P
                            last = nc.tensor.matmul(psUp[2 * r + a][0:FCH[c], :], w1[:, o:o + FCH[c]],
                                                    xnT[:, i * BANK:(i + 1) * BANK], start=True, stop=True)
                        last.then_inc(up_ready.sem, 1)

                    def down(i):
                        n = l * 2 + i
                        pe.wait_ge(h_ready.sem, h_ready.seen(n * 3 + 2))
                        pe.wait_ge(f_added.sem, f_added.prior(n))
                        for k in range(4):
                            for c in range(3):
                                last = nc.tensor.matmul(psDn[:, k * D:(k + 1) * D], hT[0:FCH[c], c, k * P:(k + 1) * P],
                                                        w2[0:FCH[c], c, :], start=(c == 0), stop=(c == 2))
                        last.then_inc(down_ready.sem, 1)

                    for i in range(2):
                        for c in range(3):
                            up(i, c)
                        down(i)

                @block.scalar
                def _(act):
                    act.wait_ge(sh_ready.sem, sh_ready.seen(l))
                    nc.scalar.copy(xs[:, :, DH:D], psF[:, :].rearrange("p (b e) -> p b e", b=B)).then_inc(
                        xs1_ready.sem, 1)
                    act.wait_ge(wf_in, (l + 1) * 80)
                    for i in range(2):
                        act.wait_ge(xh_transposed.sem, xh_transposed.seen(2 * l + i))
                        nc.scalar.activation(xnT[:, i * BANK:(i + 1) * BANK], psT2[i][:, :], ACT.Identity,
                                             bias=lng[:, 1:2], scale=lng[:, 0:1]).then_inc(xnT_ready.sem, 1)
                    for i in range(2):
                        for c in range(3):
                            n = (l * 2 + i) * 3 + c
                            r = (3 * i + c) % 2
                            act.wait_ge(up_ready.sem, up_ready.seen(n))
                            act.wait_ge(h_ready.sem, h_ready.freed(n))
                            nc.scalar.activation(gl[r][0:FCH[c], :], psUp[2 * r + 1][0:FCH[c], :], ACT.Gelu,
                                                 bias=b1[0:FCH[c], 1, c:c + 1]).then_inc(gelu_ready.sem, 1)

                @block.vector
                def _(dve):
                    dve.wait_ge(xs0_ready.sem, xs0_ready.seen(l))
                    dve.wait_ge(xs1_ready.sem, xs1_ready.seen(l))
                    for b in range(B):
                        nc.vector.bn_stats(stats[:, b, :], xs[:, b, :]).then_inc(stats_ready.sem, 1)
                    dve.wait_ge(wf_in, (l + 1) * 80)
                    dve.wait_ge(stats_ready.sem, stats_ready.seen(l * B + B - 1))
                    nc.vector.tensor_tensor(x[:, :, :], x[:, :, :], over(b2[:, :], B), ALU.add).then_inc(
                        b2_added.sem, 1)
                    for b in range(B):
                        nc.vector.bn_aggr(mv[:, b, :], stats[:, b, :]).then_inc(mv_ready.sem, 1)
                    dve.wait_ge(mv_ready.sem, mv_ready.seen(l * B + B - 1))
                    nc.vector.tensor_scalar(ve[:, :], mv[:, :, 1], LN_EPS, None, ALU.add).then_inc(ve_ready.sem, 1)
                    dve.wait_ge(rstd_ready.sem, rstd_ready.seen(l))
                    for b in range(B):
                        nc.vector.tensor_scalar(xh[:, b, :], xs[:, b, :], mv[:, b, 0:1], rstd[:, b:b + 1],
                                                ALU.subtract, ALU.mult).then_inc(xh_ready.sem, 1)
                    dve.wait_ge(b2_added.sem, b2_added.seen(l))
                    for i in range(2):
                        for c in range(3):
                            n = (l * 2 + i) * 3 + c
                            r = (3 * i + c) % 2
                            dve.wait_ge(up_ready.sem, up_ready.seen(n))
                            dve.wait_ge(gelu_ready.sem, gelu_ready.seen(n))
                            if c == 0:
                                dve.wait_ge(down_ready.sem, down_ready.prior(2 * l + i))
                            nc.vector.scalar_tensor_tensor(
                                hT[0:FCH[c], c, :], psUp[2 * r][0:FCH[c], :], b1[0:FCH[c], 0, c:c + 1],
                                gl[r][0:FCH[c], :], ALU.add, ALU.mult).then_inc(h_ready.sem, 1)
                        dve.wait_ge(down_ready.sem, down_ready.seen(2 * l + i))
                        xh4 = x[:, 4 * i:4 * i + 4, :]
                        nc.vector.tensor_tensor(xh4, xh4, psDn[:, :].rearrange("p (b e) -> p b e", b=4),
                                                ALU.add).then_inc(f_added.sem, 1)

        with nc.Fori(0, DEPTH - 1) as l:
            attention(l)
            feed_forward(l, True)
        attention(DEPTH - 1)
        feed_forward(DEPTH - 1, False)
        with nc.Block() as block:
            @block.vector
            def _(dve):
                nc.vector.tensor_tensor(x[:, :, :], x[:, :, :], x0[:, :, :], ALU.add)


def store_stage(nc, glob, out):
    st = Stage(nc, "store")
    with st.ctx:
        stored = st.sem("out_stored")
        with nc.Block() as block:
            @block.sync
            def _(sp):
                sp.dma_start(out.rearrange("b p d -> p b d"), glob["x"][:, :, :]).then_inc(stored, 16)
                sp.wait_ge(stored, 16)


STAGES = [taylor_stage, diff_stage, expert_stage, rope_stage, cross_stage, local_stage]


def decoder(nc, dram, out):
    st = Stage(nc, "all")
    with st.ctx:
        glob = {"x": st.sb("x", [P, B, D]), "ident": st.sb("ident", [P, P]),
                "ctxT": st.sb("ctxT", [P, B, S]), "mhalf": st.sb("mhalf", [P, BANK // 4])}
        load_stage(nc, glob, dram)
        for stage in STAGES:
            stage(nc, glob, dram)
        store_stage(nc, glob, out)


def _pad_heads(w, hd):
    out = np.zeros((w.shape[0], NC, HC, PAD), w.dtype)
    out[..., :hd] = w.reshape(w.shape[0], HC, NC, hd).transpose(0, 2, 1, 3)
    return out.reshape(w.shape[0], H * PAD)


def _tables():
    t = {}
    t["c_ident"] = np.eye(P, dtype=np.float32)
    n = np.arange(P)
    t["c_experts"] = np.arange(E_EXP, dtype=np.float32)
    inv = 1.0 / 10000.0 ** (np.arange(0, HD_S, 2, dtype=np.float32) / np.float32(HD_S))
    f = n[:, None].astype(np.float32) * inv[None, :].astype(np.float32)
    t["c_rope8_cos"] = np.concatenate([np.cos(f)] * 2, 1).astype(np.float32)
    t["c_rope8_sin"] = np.concatenate([-np.sin(f), np.sin(f)], 1).astype(np.float32)
    half = np.arange(0, HD_F, 2, dtype=np.float64)
    f = n[:, None] * (1.0 / 10000.0 ** (half / HD_F))[None, :]
    power = (n - P // 2) / (WINDOW // 2)
    scale = ((half + 0.4 * HD_F) / (1.4 * HD_F))[None, :] ** power[:, None]
    rot = np.concatenate([np.cos(f), np.cos(f), -np.sin(f), np.sin(f)], 1)
    scale = np.concatenate([scale] * 4, 1)
    t["c_rot"] = np.stack([rot * scale * QK_SCALE, rot / scale], 1).astype(np.float32)
    t["c_shift"] = np.eye(P, k=1, dtype=np.float32)
    seen = (n[None, :] <= n[:, None]) & (n[None, :] >= n[:, None] - WINDOW)
    t["c_band"] = np.where(seen, 0.0, MASKED).astype(np.float32)
    t["c_causalT"] = (n[:, None] <= n[None, :]).astype(np.float32)
    return t


def _arrays(inputs):
    a = {k: np.ascontiguousarray(v) for k, v in inputs.items()}
    a["L0_attn_Wq"] = _pad_heads(a["L0_attn_Wq"], HD_A)
    a["L0_attn_Wk"] = _pad_heads(a["L0_attn_Wk"], HD_A)
    for n in ("wq1", "wk1", "wq2", "wk2", "wv"):
        full = np.zeros((H, HD_S, H, HD_S), np.float32)
        w = a["L0_xattn_" + n]
        for h in range(H):
            full[h, :, h, :] = w[h].T
        full = full.reshape(D, D)
        a["L0_xattn_" + n] = full if n == "wv" else _pad_heads(full, HD_S)
    for n in ("L0_xattn_wo", "L1_attn_w_qkv", "L1_attn_w_out", *("L1_xattn_" + m for m in (
            "Wq_c", "Wk_s", "Wv_s", "Wq_s", "Wk_c", "Wv_c", "Wg"))):
        a[n] = a[n].T
    w = a["L1_ffn_Wqkv"].reshape(DEPTH, D, 3, 2, 8, HD_F).copy()
    qk = w[:, :, 0:2].transpose(0, 1, 2, 4, 3, 5).reshape(DEPTH, D, 2 * INNER)
    a["L1_ffn_Wqkv"] = np.concatenate([qk, w[:, :, 2].reshape(DEPTH, D, INNER)], 2)
    a["qk_scale"] = np.concatenate([a[f"L1_ffn_{n}_scale"].reshape(DEPTH, 2, 32)[:, o, :].reshape(DEPTH, HD_F)
                                    for n in "qk" for o in ([0, 1], [1, 0])], 1)
    del a["L1_ffn_q_scale"], a["L1_ffn_k_scale"]
    a["ln_gb"] = np.stack([a.pop("L1_ffn_ln_g"), a.pop("L1_ffn_ln_b")], 2)
    rows = 3 * P - DI
    a["L1_ffn_W2"] = np.pad(a["L1_ffn_W2"], ((0, 0), (0, rows), (0, 0)))
    a["L1_ffn_b1"] = np.pad(a["L1_ffn_b1"].reshape(DEPTH, 2, DI), ((0, 0), (0, 0), (0, rows))).reshape(
        DEPTH, 6, P).transpose(0, 2, 1)
    a.update(_tables())
    a.pop("L0_ffn_scores")
    return {k: np.ascontiguousarray(v if v.ndim else v.reshape(1)) for k, v in a.items()}


def kernel(**inputs):
    import concourse.bacc as _bacc
    from concourse.bass_utils import run_bass_kernel_spmd as _run

    nc = _bacc.Bacc("TRN2", target_bir_lowering=False, num_devices=1)
    arrays = {f"in_{k}": v for k, v in _arrays(inputs).items()}
    dram = {k[3:]: nc.dram_tensor(k, v.shape, mybir.dt.from_np(v.dtype), kind="ExternalInput").ap()
            for k, v in arrays.items()}
    out = nc.dram_tensor("out_x", (B, S, D), F32, kind="ExternalOutput").ap()
    decoder(nc, dram, out)
    return _run(nc, [arrays], core_ids=[0]).results[0]["out_x"]
```

```python
from contextlib import ExitStack

import numpy as np

import concourse.bass as bass
from concourse import mybir

P = 128
B, S, D = 8, 128, 128
H = 16
PAD = 32
HC = P // PAD
NC = H // HC
G = 4
BANK = 512
WIN = 96
HD_A, VD_A = 16, 64
HD_S = 8
E_EXP, FF, TOPK = 8, 512, 2
MOE_T = 512
HD_F, WINDOW, DEPTH, INNER, DI = 64, 32, 6, 1024, 341
QK_SCALE, MASKED = 8.0, -1e30
LN_EPS = 1e-5

F32 = mybir.dt.float32
BF16 = mybir.dt.bfloat16
I32 = mybir.dt.int32
ALU = mybir.AluOpType
ACT = mybir.ActivationFunctionType
AX = mybir.AxisListType.X


class Stage:

    def __init__(self, nc, name):
        self.nc, self.name, self.ctx, self.sems = nc, name, ExitStack(), []
        self.ctx.callback(self.clear)

    def clear(self):
        if self.sems:
            self.nc.clear_and_free_semaphores(self.sems)
            self.nc.all_engine_barrier()

    def sb(self, name, shape, dt=F32):
        return self.ctx.enter_context(self.nc.sbuf_tensor(f"{self.name}_{name}", shape, dt))

    def ps(self, name, cols=BANK):
        return self.ctx.enter_context(self.nc.psum_tensor(f"{self.name}_{name}", [P, cols], F32))

    def sem(self, name):
        self.sems.append(self.nc.alloc_semaphore(f"{self.name}_{name}"))
        return self.sems[-1]


def over(ap, n):
    return ap.unsqueeze(1).to_broadcast([ap.shape[0], n, ap.shape[1]])


def along(ap, n):
    return ap.unsqueeze(2).to_broadcast([ap.shape[0], ap.shape[1], n])


class LayerNorm:

    def __init__(self, nc, st, glob, count=B):
        self.nc, self.x, self.g, self.n = nc, glob["x"], glob, count
        self.stats = st.sb("ln_stats", [P, B, 6])
        self.mv = st.sb("ln_mv", [P, B, 2])
        self.ve = st.sb("ln_var_eps", [P, B])
        self.rstd = st.sb("ln_rstd", [P, B])
        self.xh = st.sb("x_hat", [P, D])
        self.xT = st.sb("x_hat_T", [P, S])
        self.psX = st.ps("ps_x")
        self.stats_done = st.sem("ln_stats_done")
        self.mv_done = st.sem("ln_mv_done")
        self.ve_done = st.sem("ln_ve_done")
        self.rstd_done = st.sem("ln_rstd_done")
        self.xh_ready = st.sem("xh_ready")
        self.psx_ready = st.sem("psx_ready")
        self.xT_ready = st.sem("xT_ready")

    def dve_stats(self, dve):
        nc, n = self.nc, self.n
        for b in range(n):
            nc.vector.bn_stats(self.stats[:, b, :], self.x[:, b, :]).then_inc(self.stats_done, 1)
        for b in range(n):
            dve.wait_ge(self.stats_done, b + 1)
            nc.vector.bn_aggr(self.mv[:, b, :], self.stats[:, b, :]).then_inc(self.mv_done, 1)
        dve.wait_ge(self.mv_done, n)
        nc.vector.tensor_scalar(self.ve[:, 0:n], self.mv[:, 0:n, 1], LN_EPS, None,
                                ALU.add).then_inc(self.ve_done, 1)

    def pool_rstd(self, pool):
        pool.wait_ge(self.ve_done, 1)
        self.nc.gpsimd.tensor_tensor(self.rstd[:, 0:self.n], self.ve[:, 0:self.n],
                                     self.g["mhalf"][:, 0:self.n], ALU.pow).then_inc(self.rstd_done, 1)

    def dve_normalise(self, dve, b):
        dve.wait_ge(self.rstd_done, 1)
        self.nc.vector.tensor_scalar(self.xh[:, :], self.x[:, bass.ds(b, 1), :],
                                     self.mv[:, bass.ds(b, 1), 0], self.rstd[:, bass.ds(b, 1)],
                                     ALU.subtract, ALU.mult).then_inc(self.xh_ready, 1)

    def pe_transpose(self, pe, b):
        pe.wait_ge(self.xh_ready, b + 1)
        self.nc.tensor.transpose(self.psX[:, 0:S], self.xh[:, :],
                                 self.g["ident"][:, :]).then_inc(self.psx_ready, 1)

    def act_store(self, act, b):
        act.wait_ge(self.psx_ready, b + 1)
        self.nc.scalar.copy(self.xT[:, :], self.psX[:, 0:S]).then_inc(self.xT_ready, 1)


class Pipeline:

    FIRST, LAST = -2, B
    LOOP = (1, 5)

    @classmethod
    def run(cls, eng, slots):
        for b in range(cls.FIRST, cls.LOOP[0]):
            slots(b, b % 2, b)
        with eng.Fori(0, (cls.LOOP[1] - cls.LOOP[0]) // 2) as n:
            for i in range(2):
                slots(2 * n + (cls.LOOP[0] + i), (cls.LOOP[0] + i) % 2, cls.LOOP[0] + i)
        for b in range(cls.LOOP[1], cls.LAST + 1):
            slots(b, b % 2, b)

    @staticmethod
    def there(sb, off):
        return 0 <= sb + off < B


def ago(g, n, groups):
    return (g - n) // groups, (g - n) % groups


class SoftmaxHeads:

    RING = 2

    def __init__(self, nc, st, glob, groups, scale):
        self.nc, self.groups, self.scale, self.g = nc, groups, scale, glob
        self.psS = [st.ps(f"ps_scores{i}") for i in range(2)]
        self.psT = st.ps("ps_probsT")
        self.mx = [st.sb(f"row_max{i}", [P, G]) for i in range(2)]
        self.dif = [st.sb(f"dif{i}", [P, BANK]) for i in range(2)]
        self.prob = [st.sb(f"prob{i}", [P, BANK]) for i in range(2)]
        self.probT = [st.sb(f"probT{i}", [P, BANK]) for i in range(2)]
        self.scores_ready = st.sem("scores_ready")
        self.max_done = st.sem("max_done")
        self.dif_done = st.sem("dif_done")
        self.exp_done = st.sem("exp_done")
        self.transposed = st.sem("transposed")
        self.probT_done = st.sem("probT_done")
        self.values_done = st.sem("values_done")

    def credit(self, eng, *sems):
        for s in sems:
            eng.sem_inc(s, self.RING)

    def all_heads(self, ap):
        return ap.rearrange("p (h m) -> p h m", h=G)

    def slot(self, b, sb, g, n, work, *args):
        off, k = ago(g, n, self.groups)
        if Pipeline.there(sb, off):
            work(b, off, k, *args)

    def pe_scores(self, b, off, g, pe, queries, keys):
        u = (b + off) * self.groups + g
        pe.wait_ge(self.dif_done, u + 1)
        self.nc.tensor.matmul(self.psS[g % 2][:, :], queries(b, off, g), keys(b, off, g), start=True,
                              stop=True).then_inc(self.scores_ready, 1)

    def dve_shift(self, b, off, g, dve):
        u, i = (b + off) * self.groups + g, g % 2
        dve.wait_ge(self.scores_ready, u + 1)
        self.nc.vector.tensor_reduce(self.mx[i][:, :], self.all_heads(self.psS[i][:, :]), AX,
                                     ALU.max).then_inc(self.max_done, 1)
        dve.wait_ge(self.exp_done, u + 1)
        dve.wait_ge(self.max_done, u + 1)
        self.nc.vector.tensor_tensor(self.all_heads(self.dif[i][:, :]), self.all_heads(self.psS[i][:, :]),
                                     along(self.mx[i][:, :], S),
                                     ALU.subtract).then_inc(self.dif_done, 1)

    def act_exp(self, b, off, g, act):
        u, i = (b + off) * self.groups + g, g % 2
        act.wait_ge(self.dif_done, u + 1 + self.RING)
        act.wait_ge(self.transposed, u + 1)
        self.nc.scalar.activation(self.prob[i][:, :], self.dif[i][:, :], ACT.Exp,
                                  scale=self.scale).then_inc(self.exp_done, 1)

    def pe_transpose(self, b, off, g, pe):
        u, i = (b + off) * self.groups + g, g % 2
        pe.wait_ge(self.exp_done, u + 1 + self.RING)
        pe.wait_ge(self.probT_done, u + self.RING)
        for j in range(G):
            last = self.nc.tensor.transpose(self.psT[:, j * S:(j + 1) * S],
                                            self.prob[i][:, j * S:(j + 1) * S], self.g["ident"][:, :])
        last.then_inc(self.transposed, 1)

    def act_store(self, b, off, g, act):
        u, i = (b + off) * self.groups + g, g % 2
        act.wait_ge(self.transposed, u + 1 + self.RING)
        act.wait_ge(self.values_done, u + 1)
        self.nc.scalar.copy(self.probT[i][:, :], self.psT[:, :]).then_inc(self.probT_done, 1)

    def pe_values(self, b, off, g, pe, product):
        u, i = (b + off) * self.groups + g, g % 2
        pe.wait_ge(self.probT_done, u + 1 + self.RING)
        for j in range(G):
            last = product(self.probT[i][:, j * S:(j + 1) * S], b, off, g, j)
        last.then_inc(self.values_done, 1)

    def pe_slot(self, pe, b, sb, g, queries, keys, product):
        self.slot(b, sb, g, 1, self.pe_transpose, pe)
        self.slot(b, sb, g, -1, self.pe_scores, pe, queries, keys)
        self.slot(b, sb, g, 2, self.pe_values, pe, product)

    def act_slot(self, act, b, sb, g):
        self.slot(b, sb, g, 0, self.act_exp, act)
        self.slot(b, sb, g, 1, self.act_store, act)

    def dve_slot(self, dve, b, sb, g):
        self.slot(b, sb, g, 0, self.dve_shift, dve)


def load_stage(nc, glob, dram):
    st = Stage(nc, "load")
    with st.ctx:
        ctx = st.sb("ctx", [P, B, D])
        psC = [st.ps(f"ps_ctx{i}") for i in range(2)]
        loaded, ident_in, x_in = st.sem("ctx_in"), st.sem("ident_in"), st.sem("x_in")
        transposed = st.sem("ctx_transposed")
        stored, ready = st.sem("ctx_stored"), st.sem("const_ready")
        with nc.Block() as block:
            @block.sync
            def _(sp):
                sp.dma_start(ctx[:, :, :], dram["ctx_1024"].rearrange("b p d -> p b d")).then_inc(loaded, 16)
                sp.dma_start(glob["x"][:, :, :], dram["x"].rearrange("b p d -> p b d")).then_inc(x_in, 16)
                sp.wait_ge(x_in, 16)

            @block.gpsimd
            def _(pool):
                nc.gpsimd.memset(glob["mhalf"][:, :], -0.5).then_inc(ready, 1)
                pool.dma_start(glob["ident"][:, :], dram["c_ident"]).then_inc(ident_in, 16)
                pool.wait_ge(ready, 1)

            @block.tensor
            def _(pe):
                pe.wait_ge(ident_in, 16)
                pe.wait_ge(loaded, 16)
                for b in range(B):
                    nc.tensor.transpose(psC[b // 4][:, b % 4 * S:(b % 4 + 1) * S], ctx[:, b, :],
                                        glob["ident"][:, :]).then_inc(transposed, 1)

            @block.scalar
            def _(act):
                for i in range(2):
                    act.wait_ge(transposed, 4 * i + 4)
                    nc.scalar.copy(glob["ctxT"][:, 4 * i:4 * i + 4, :], psC[i][:, :]).then_inc(stored, 1)
                act.wait_ge(stored, 2)


def taylor_stage(nc, glob, dram):
    st = Stage(nc, "tay")
    with st.ctx:
        ln = LayerNorm(nc, st, glob)
        x = glob["x"]
        wq = st.sb("wq", [P, NC * P])
        wk = st.sb("wk", [P, NC * P])
        wv = st.sb("wv", [P, H * VD_A])
        wo = st.sb("wo", [P, H * VD_A // P, D])
        mask = st.sb("mask", [P, S])
        VW = VD_A + 1
        v = st.sb("v", [P, H * VW + WIN])
        v3 = v[:, 0:H * VW].rearrange("p (h e) -> p h e", e=VW)
        qT = st.sb("qT", [P, NC, S])
        kT = st.sb("kT", [P, NC, S])
        sq = [st.sb(f"square{i}", [P, BANK]) for i in range(2)]
        at = [st.sb(f"weights{i}", [P, BANK]) for i in range(2)]
        rz = st.sb("rz", [P, 2, G])
        yn = st.sb("y", [P, H * VD_A])
        yT = st.sb("yT", [P, H * VD_A])
        psQ = [st.ps(f"ps_proj{i}") for i in range(2)]
        psS = [st.ps(f"ps_scores{i}") for i in range(2)]
        psO = [st.ps(f"ps_out{i}") for i in range(2)]
        psY = ln.psX
        w_in, ones_ready, tables_in = st.sem("w_in"), st.sem("ones_ready"), st.sem("tables_in")
        qk_proj, v_proj = st.sem("qk_proj"), st.sem("v_proj")
        q_stored, k_stored = st.sem("q_stored"), st.sem("k_stored")
        v0_stored, v1_stored = st.sem("v0_stored"), st.sem("v1_stored")
        scores_ready, squared, masked = st.sem("scores_ready"), st.sem("squared"), st.sem("masked")
        out_ready, z_ready, rz_ready = st.sem("out_ready"), st.sem("z_ready"), st.sem("rz_ready")
        y_ready, yT_ready = st.sem("y_ready"), st.sem("yT_ready")
        yT0_stored, yT1_stored = st.sem("yT0_stored"), st.sem("yT1_stored")
        o_ready, added = st.sem("o_ready"), st.sem("added")

        with nc.Block() as block:
            @block.sync
            def _(sp):
                sp.dma_start(wq[:, :], dram["L0_attn_Wq"]).then_inc(w_in, 16)
                sp.dma_start(wk[:, :], dram["L0_attn_Wk"]).then_inc(w_in, 16)
                sp.dma_start(wv[:, :], dram["L0_attn_Wv"]).then_inc(w_in, 16)
                sp.dma_start(wo[:, :, :], dram["L0_attn_Wo"].rearrange("(c p) n -> p c n", p=P)).then_inc(w_in, 16)
                sp.dma_start(mask[:, :], dram["c_causalT"]).then_inc(tables_in, 16)

            @block.gpsimd
            def _(pool):
                nc.gpsimd.memset(v[:, :], 1.0).then_inc(ones_ready, 1)
                ln.pool_rstd(pool)

            @block.tensor
            def _(pe):
                pe.wait_ge(w_in, 64)
                with pe.Fori(0, B) as b:
                    ln.pe_transpose(pe, b)
                    pe.wait_ge(ln.xT_ready, b + 1)
                    for i, w in enumerate((wq, wk)):
                        for c in range(NC):
                            last = nc.tensor.matmul(psQ[i][:, c * S:(c + 1) * S], w[:, c * P:(c + 1) * P],
                                                    ln.xT[:, :], start=True, stop=True)
                        last.then_inc(qk_proj, 1)
                    for i in range(2):
                        nc.tensor.matmul(psO[i][:, :], ln.xT[:, :], wv[:, i * BANK:(i + 1) * BANK],
                                         start=True, stop=True).then_inc(v_proj, 1)
                    pe.wait_ge(q_stored, b + 1)
                    pe.wait_ge(k_stored, b + 1)

                    def scores(g):
                        if g >= 2:
                            pe.wait_ge(squared, b * NC + g - 1)
                        for j in range(G):
                            r = g * PAD
                            last = nc.tensor.matmul(psS[g % 2][:, j * S:(j + 1) * S], kT[r:r + HD_A, j, :],
                                                    qT[r:r + HD_A, j, :], start=True, stop=True)
                        last.then_inc(scores_ready, 1)

                    scores(0)
                    for g in range(NC):
                        if g + 1 < NC:
                            scores(g + 1)
                        if g == 0:
                            pe.wait_ge(v0_stored, b + 1)
                            pe.wait_ge(v1_stored, b + 1)
                            pe.wait_ge(ones_ready, 1)
                        if g >= 2:
                            pe.wait_ge(y_ready, b * NC + g - 1)
                        pe.wait_ge(masked, b * NC + g + 1)
                        for j in range(G):
                            c = (g * G + j) * VW
                            last = nc.tensor.matmul(psO[g % 2][:, j * S:j * S + WIN],
                                                    at[g % 2][:, j * S:(j + 1) * S], v[:, c:c + WIN],
                                                    start=True, stop=True)
                        last.then_inc(out_ready, 1)
                    pe.wait_ge(y_ready, b * NC + NC)
                    for c in range(8):
                        last = nc.tensor.transpose(psQ[c // 4][:, c % 4 * S:(c % 4 + 1) * S],
                                                   yn[:, c * P:(c + 1) * P], glob["ident"][:, :])
                        if c % 4 == 3:
                            last.then_inc(yT_ready, 1)
                    pe.wait_ge(yT0_stored, b + 1)
                    pe.wait_ge(yT1_stored, b + 1)
                    for c in range(8):
                        last = nc.tensor.matmul(psY[:, 0:D], yT[:, c * P:(c + 1) * P], wo[:, c, :],
                                                start=(c == 0), stop=(c == 7))
                    last.then_inc(o_ready, 1)

            @block.scalar
            def _(act):
                act.wait_ge(ones_ready, 1)
                with act.Fori(0, B) as b:
                    ln.act_store(act, b)
                    act.wait_ge(qk_proj, 2 * b + 1)
                    nc.scalar.copy(qT[:, :, :], psQ[0][:, :]).then_inc(q_stored, 1)
                    act.wait_ge(v_proj, 2 * b + 1)
                    nc.scalar.copy(v3[:, 0:8, 0:VD_A],
                                   psO[0][:, :].rearrange("p (h e) -> p h e", h=8)).then_inc(v0_stored, 1)
                    for g in range(NC):
                        act.wait_ge(scores_ready, b * NC + g + 1)
                        if g >= 2:
                            act.wait_ge(masked, b * NC + g - 1)
                        nc.scalar.activation(sq[g % 2][:, :], psS[g % 2][:, :], ACT.Square, bias=1.0,
                                             scale=0.25).then_inc(squared, 1)
                    act.wait_ge(yT_ready, 2 * b + 1)
                    nc.scalar.copy(yT[:, 0:BANK], psQ[0][:, :]).then_inc(yT0_stored, 1)

            @block.vector
            def _(dve):
                ln.dve_stats(dve)
                dve.wait_ge(tables_in, 16)
                dve.wait_ge(ones_ready, 1)
                with dve.Fori(0, B) as b:
                    ln.dve_normalise(dve, b)
                    dve.wait_ge(qk_proj, 2 * b + 2)
                    nc.vector.tensor_copy(kT[:, :, :], psQ[1][:, :]).then_inc(k_stored, 1)
                    dve.wait_ge(v_proj, 2 * b + 2)
                    nc.vector.tensor_copy(v3[:, 8:16, 0:VD_A],
                                          psO[1][:, :].rearrange("p (h e) -> p h e", h=8)).then_inc(v1_stored, 1)

                    def weights(g):
                        dve.wait_ge(squared, b * NC + g + 1)
                        if g >= 2:
                            dve.wait_ge(out_ready, b * NC + g - 1)
                        nc.vector.scalar_tensor_tensor(
                            at[g % 2][:, :].rearrange("p (h m) -> p h m", h=G),
                            sq[g % 2][:, :].rearrange("p (h m) -> p h m", h=G), 1.0,
                            over(mask[:, :], G), ALU.add, ALU.mult).then_inc(masked, 1)

                    def normalise(g):
                        o3 = psO[g % 2][:, :].rearrange("p (h e) -> p h e", h=G)
                        dve.wait_ge(out_ready, b * NC + g + 1)
                        nc.vector.tensor_scalar(rz[:, 0, :], o3[:, :, VD_A], 2e-12, None,
                                                ALU.add).then_inc(z_ready, 1)
                        dve.wait_ge(z_ready, b * NC + g + 1)
                        nc.vector.reciprocal(rz[:, 1, :], rz[:, 0, :]).then_inc(rz_ready, 1)
                        dve.wait_ge(rz_ready, b * NC + g + 1)
                        nc.vector.tensor_tensor(
                            yn[:, g * G * VD_A:(g + 1) * G * VD_A].rearrange("p (h e) -> p h e", h=G),
                            o3[:, :, 0:VD_A], along(rz[:, 1, :], VD_A), ALU.mult).then_inc(y_ready, 1)

                    for g in range(NC):
                        weights(g)
                        if g:
                            normalise(g - 1)
                    normalise(NC - 1)
                    dve.wait_ge(yT_ready, 2 * b + 2)
                    nc.vector.tensor_copy(yT[:, BANK:], psQ[1][:, :]).then_inc(yT1_stored, 1)
                    dve.wait_ge(o_ready, b + 1)
                    xb = x[:, bass.ds(b, 1), :]
                    nc.vector.tensor_tensor(xb, xb, psY[:, 0:D], ALU.add).then_inc(added, 1)
                dve.wait_ge(added, B)


def diff_stage(nc, glob, dram):
    st = Stage(nc, "dif")
    with st.ctx:
        NM = 2
        NG = NM * H // G
        VW = HD_S + 1
        VB = H * VW
        ln = LayerNorm(nc, st, glob)
        at = SoftmaxHeads(nc, st, glob, NG, float(HD_S) ** -0.5)
        there = Pipeline.there
        x, ctxT = glob["x"], glob["ctxT"]
        w = [st.sb(n, [P, D]) for n in ("wq1", "wq2", "wk1", "wk2")]
        wv, wo, gain = st.sb("wv", [P, D]), st.sb("wo", [P, D]), st.sb("gain", [P, 1])
        own_rows = st.sb("own_rows", [P, H])
        v = st.sb("v", [P, B * VB + WIN])
        v4 = v[:, 0:B * VB].rearrange("p (b h e) -> p b h e", b=B, e=VW)
        qT = [st.sb(f"qT{i}", [P, NM, S]) for i in range(2)]
        kT = st.sb("kT", [P, NM, S])
        kz = [st.sb(f"k_own{i}", [P, NM, H, S]) for i in range(2)]
        rz = st.sb("rz", [P, NM, H])
        rzg = st.sb("rz_gain", [P, H])
        m1, m2, o = (st.sb(n, [P, H, HD_S]) for n in ("map1", "map2", "o"))
        cen, sqr, oN = (st.sb(n, [P, H, HD_S]) for n in ("centred", "squares", "o_norm"))
        red = st.sb("head_sums", [P, 4, H])
        rs = st.sb("head_rstd", [P, H])
        oT = st.sb("oT", [P, S])
        psP, psO, psY = st.ps("ps_proj"), [st.ps(f"ps_out{i}") for i in range(2)], st.ps("ps_y")
        psF = psY[:, 256:256 + S]
        w_in, const_in, ones_ready = st.sem("w_in"), st.sem("const_in"), st.sem("ones_ready")
        v_proj, v_stored = st.sem("v_proj"), st.sem("v_stored")
        qk_proj, q_stored, k_stored = st.sem("qk_proj"), st.sem("q_stored"), st.sem("k_stored")
        kz_ready = st.sem("kz_ready")
        rz_ready, rzg_ready = st.sem("rz_ready"), st.sem("rzg_ready")
        maps_ready, o_ready, sum_ready = st.sem("maps_ready"), st.sem("o_ready"), st.sem("sum_ready")
        mean_ready, cen_ready = st.sem("mean_ready"), st.sem("cen_ready")
        sqr_ready, var_ready, ve_ready = st.sem("sqr_ready"), st.sem("var_ready"), st.sem("ve_ready")
        rs_ready, oN_ready, oT_ready = st.sem("rs_ready"), st.sem("oN_ready"), st.sem("oT_ready")
        oT_stored, y_ready, added = st.sem("oT_stored"), st.sem("y_ready"), st.sem("added")

        with nc.Block() as block:
            @block.sync
            def _(sp):
                for i, n in enumerate(("wq1", "wq2", "wk1", "wk2")):
                    sp.dma_start(w[i][:, :], dram["L0_xattn_" + n]).then_inc(w_in, 16)
                sp.dma_start(wv[:, :], dram["L0_xattn_wv"]).then_inc(w_in, 16)
                sp.dma_start(wo[:, :], dram["L0_xattn_wo"]).then_inc(w_in, 16)
                sp.dma_start(own_rows[:, :], dram["c_own_rows8"]).then_inc(const_in, 16)
                sp.dma_start(gain[:, :], dram["L0_xattn_gain"].unsqueeze(0).to_broadcast([P, 1])).then_inc(const_in, 16)

            @block.gpsimd
            def _(pool):
                nc.gpsimd.memset(v[:, :], 1.0).then_inc(ones_ready, 1)
                ln.pool_rstd(pool)
                pool.wait_ge(const_in, 32)

                def own_keys(b, sb, p, m):
                    pool.wait_ge(k_stored, b + 2)
                    if there(sb, -1):
                        pool.wait_ge(at.scores_ready, b * NG)
                    nc.gpsimd.tensor_tensor(kz[p][:, m, :, :], over(kT[:, m, :], H), along(own_rows[:, :], S),
                                            ALU.mult).then_inc(kz_ready, 1)

                def slots(b, p, sb):
                    if there(sb, 1):
                        own_keys(b, sb, 1 - p, 0)
                    if there(sb, -1):
                        pool.wait_ge(ve_ready, b)
                        nc.gpsimd.tensor_tensor(rs[:, :], red[:, 3, :], glob["mhalf"][:, 0:H],
                                                ALU.pow).then_inc(rs_ready, 1)
                    if there(sb, 1):
                        own_keys(b, sb, 1 - p, 1)

                Pipeline.run(pool, slots)

            @block.tensor
            def _(pe):
                at.credit(pe, at.transposed, at.values_done)
                pe.wait_ge(w_in, 96)
                for b in range(B):
                    nc.tensor.matmul(psO[b // 4][:, b % 4 * D:(b % 4 + 1) * D], ctxT[:, b, :], wv[:, :],
                                     start=True, stop=True).then_inc(v_proj, 1)
                pe.wait_ge(v_stored, 2)

                def slots(b, p, sb):
                    def queries(b, off, g):
                        return qT[(p + off) % 2][:, g // G, :]

                    def keys(b, off, g):
                        if g % G == 0:
                            pe.wait_ge(kz_ready, NM * (b + off) + g // G + 1)
                        if g == 0:
                            pe.wait_ge(q_stored, b + off + 1)
                        h = g % G * G
                        return kz[(p + off) % 2][:, g // G, h:h + G, :]

                    def product(probT, b, off, g, j):
                        h = g % G * G + j
                        c = g // G * 256 + h * VW
                        return nc.tensor.matmul(psO[(p + off) % 2][:, c:c + WIN], probT,
                                                v[:, bass.ds((b + off) * VB + h * VW, WIN)], start=True, stop=True)

                    for g in range(NG):
                        at.pe_slot(pe, b, sb, g, queries, keys, product)
                        if g == 1 and there(sb, 2):
                            ln.pe_transpose(pe, b + 2)
                        if g == 3 and there(sb, 2):
                            pe.wait_ge(ln.xT_ready, b + 3)
                            if there(sb, 1):
                                pe.wait_ge(q_stored, b + 2)
                                pe.wait_ge(k_stored, b + 2)
                            for i in range(4):
                                rhs = ln.xT[:, :] if i < 2 else ctxT[:, bass.ds(b + 2, 1), :]
                                last = nc.tensor.matmul(psP[:, i * S:(i + 1) * S], w[i][:, :], rhs,
                                                        start=True, stop=True)
                            last.then_inc(qk_proj, 1)
                        if g == 5 and there(sb, -1):
                            pe.wait_ge(oN_ready, b)
                            nc.tensor.transpose(psF, oN[:, :, :].rearrange("p h e -> p (h e)"),
                                                glob["ident"][:, :]).then_inc(oT_ready, 1)
                        if g == 6 and there(sb, -1):
                            pe.wait_ge(oT_stored, b)
                            nc.tensor.matmul(psY[:, 0:D], oT[:, :], wo[:, :], start=True,
                                             stop=True).then_inc(y_ready, 1)

                Pipeline.run(pe, slots)

            @block.scalar
            def _(act):
                at.credit(act, at.exp_done, at.probT_done)

                def slots(b, p, sb):
                    for g in range(NG):
                        at.act_slot(act, b, sb, g)
                        if g == 1 and there(sb, 2):
                            ln.act_store(act, b + 2)
                        if g == 5 and there(sb, -1):
                            act.wait_ge(oT_ready, b)
                            nc.scalar.copy(oT[:, :], psF).then_inc(oT_stored, 1)
                        if g == 7 and there(sb, 2):
                            act.wait_ge(qk_proj, b + 3)
                            if there(sb, 0):
                                act.wait_ge(at.scores_ready, (b + 1) * NG)
                            nc.scalar.copy(qT[p][:, :, :], psP[:, 0:NM * S]).then_inc(q_stored, 1)
                            if there(sb, 1):
                                act.wait_ge(kz_ready, NM * (b + 2))
                            nc.scalar.copy(kT[:, :, :], psP[:, NM * S:]).then_inc(k_stored, 1)

                Pipeline.run(act, slots)

            @block.vector
            def _(dve):
                at.credit(dve, at.dif_done)
                ln.dve_stats(dve)
                dve.wait_ge(const_in, 32)
                dve.wait_ge(ones_ready, 1)
                for i in range(2):
                    dve.wait_ge(v_proj, 4 * i + 4)
                    for k in range(4):
                        last = nc.vector.tensor_copy(
                            v4[:, 4 * i + k, :, 0:HD_S],
                            psO[i][:, k * D:(k + 1) * D].rearrange("p (h e) -> p h e", e=HD_S))
                    last.then_inc(v_stored, 1)

                def combine(b, p):
                    o4 = psO[p][:, :].rearrange("p (m c) -> p m c", m=NM)[:, :, 0:VB].rearrange(
                        "p m (h e) -> p m h e", e=VW)
                    dve.wait_ge(at.values_done, NG * b + at.RING)
                    nc.vector.reciprocal(rz[:, :, :], o4[:, :, :, HD_S]).then_inc(rz_ready, 1)
                    dve.wait_ge(rz_ready, b)
                    nc.vector.tensor_scalar(rzg[:, :], rz[:, 1, :], gain[:, 0:1], None,
                                            ALU.mult).then_inc(rzg_ready, 1)
                    nc.vector.tensor_tensor(m1[:, :, :], o4[:, 0, :, 0:HD_S], along(rz[:, 0, :], HD_S), ALU.mult)
                    dve.wait_ge(rzg_ready, b)
                    nc.vector.tensor_tensor(m2[:, :, :], o4[:, 1, :, 0:HD_S], along(rzg[:, :], HD_S),
                                            ALU.mult).then_inc(maps_ready, 1)
                    dve.wait_ge(maps_ready, b)
                    nc.vector.tensor_tensor(o[:, :, :], m1[:, :, :], m2[:, :, :], ALU.subtract).then_inc(o_ready, 1)
                    dve.wait_ge(o_ready, b)
                    nc.vector.tensor_reduce(red[:, 0, :], o[:, :, :], AX, ALU.add).then_inc(sum_ready, 1)
                    dve.wait_ge(sum_ready, b)
                    nc.vector.tensor_scalar(red[:, 1, :], red[:, 0, :], 1.0 / HD_S, None,
                                            ALU.mult).then_inc(mean_ready, 1)
                    dve.wait_ge(mean_ready, b)
                    nc.vector.tensor_tensor(cen[:, :, :], o[:, :, :], along(red[:, 1, :], HD_S),
                                            ALU.subtract).then_inc(cen_ready, 1)
                    dve.wait_ge(cen_ready, b)
                    nc.vector.tensor_tensor(sqr[:, :, :], cen[:, :, :], cen[:, :, :], ALU.mult).then_inc(sqr_ready, 1)
                    dve.wait_ge(sqr_ready, b)
                    nc.vector.tensor_reduce(red[:, 2, :], sqr[:, :, :], AX, ALU.add).then_inc(var_ready, 1)
                    dve.wait_ge(var_ready, b)
                    nc.vector.tensor_scalar(red[:, 3, :], red[:, 2, :], 1.0 / HD_S, LN_EPS, ALU.mult,
                                            ALU.add).then_inc(ve_ready, 1)

                def slots(b, p, sb):
                    for g in range(NG):
                        at.dve_slot(dve, b, sb, g)
                        if g == 0 and there(sb, 2):
                            if there(sb, 1):
                                dve.wait_ge(ln.psx_ready, b + 2)
                            ln.dve_normalise(dve, b + 2)
                        if g == 2 and there(sb, -1):
                            combine(b, 1 - p)
                        if g == 4 and there(sb, -1):
                            dve.wait_ge(rs_ready, b)
                            nc.vector.tensor_tensor(oN[:, :, :], cen[:, :, :], along(rs[:, :], HD_S),
                                                    ALU.mult).then_inc(oN_ready, 1)
                        if g == 7 and there(sb, -1):
                            dve.wait_ge(y_ready, b)
                            xb = x[:, bass.ds(b - 1, 1), :]
                            nc.vector.tensor_tensor(xb, xb, psY[:, 0:D], ALU.add).then_inc(added, 1)

                Pipeline.run(dve, slots)
                dve.wait_ge(added, B)


def expert_stage(nc, glob, dram):
    st = Stage(nc, "moe")
    with st.ctx:
        NT = MOE_T // P
        FC = FF // P
        ln = LayerNorm(nc, st, glob, NT)
        x = glob["x"]
        xT = st.sb("x_hat_T4", [P, MOE_T])
        xh = st.sb("x_hat4", [P, NT, D])
        w1 = [st.sb(f"w1_{i}", [P, FF]) for i in range(2)]
        w2 = [st.sb(f"w2_{i}", [P, FC, D]) for i in range(2)]
        hT = [st.sb(f"hT{i}", [P, FC, MOE_T]) for i in range(2)]
        idx = st.sb("idx", [P, NT, TOPK], I32)
        wts = st.sb("wts", [P, NT, TOPK])
        eid = st.sb("expert_ids", [P, E_EXP])
        hit = st.sb("hit", [P, NT, E_EXP, TOPK])
        share = st.sb("share", [P, NT, E_EXP, TOPK])
        gate = st.sb("gate", [P, NT, E_EXP])
        bias = st.sb("bias", [P, D])
        psH = [st.ps(f"ps_h{i}") for i in range(2)]
        psY = [st.ps(f"ps_y{i}") for i in range(2)]
        psX = st.ps("ps_x4")
        w1_in = [st.sem(f"w1_{i}_in") for i in range(2)]
        w2_in = [st.sem(f"w2_{i}_in") for i in range(2)]
        route_in, id_in, bias_in = st.sem("route_in"), st.sem("id_in"), st.sem("bias_in")
        hit_ready, share_ready, gate_ready = st.sem("hit_ready"), st.sem("share_ready"), st.sem("gate_ready")
        xh_ready, x_transposed, xT_ready = st.sem("xh4_ready"), st.sem("x_transposed"), st.sem("xT4_ready")
        h_ready, h_stored, y_ready, y_added = (st.sem("h_ready"), st.sem("h_stored"), st.sem("y_ready"),
                                               st.sem("y_added"))
        biased = st.sem("biased")

        with nc.Block() as block:
            @block.sync
            def _(sp):
                idx_v = dram["L0_ffn_expert_indices"].rearrange("(j p) k -> p j k", p=P)
                wts_v = dram["L0_ffn_expert_weights"].rearrange("(j p) k -> p j k", p=P)

                def expert(e, i):
                    sp.dma_start(w1[i][:, :], dram["L0_ffn_w1"][bass.ds(e, 1), :, :].rearrange(
                        "a p n -> p (a n)")).then_inc(w1_in[i], 16)
                    sp.dma_start(w2[i][:, :, :], dram["L0_ffn_w2"][bass.ds(e, 1), :, :].rearrange(
                        "a (c p) n -> p (a c) n", p=P)).then_inc(w2_in[i], 16)

                sp.dma_start(idx[:, :, :], idx_v).then_inc(route_in, 16)
                sp.dma_start(wts[:, :, :], wts_v).then_inc(route_in, 16)
                sp.dma_start(eid[:, :], dram["c_experts"].unsqueeze(0).to_broadcast([P, E_EXP])).then_inc(id_in, 16)
                sp.dma_start(bias[:, :], dram["L0_ffn_bias"].unsqueeze(0).to_broadcast([P, D])).then_inc(bias_in, 16)
                expert(0, 0)
                expert(1, 1)
                with sp.Fori(1, E_EXP // 2) as n:
                    for i in range(2):
                        sp.wait_ge(y_ready, 2 * n + i - 1)
                        expert(2 * n + i, i)

            @block.gpsimd
            def _(pool):
                ln.pool_rstd(pool)

            @block.tensor
            def _(pe):
                pe.wait_ge(xh_ready, NT)
                for j in range(NT):
                    last = nc.tensor.transpose(psX[:, j * S:(j + 1) * S], xh[:, j, :], glob["ident"][:, :])
                last.then_inc(x_transposed, 1)
                pe.wait_ge(xT_ready, 1)

                def up(e, i, n):
                    pe.wait_ge(w1_in[i], (n + 1) * 16)
                    for c in range(FC):
                        pe.wait_ge(h_stored, FC * e + c + 1)
                        nc.tensor.matmul(psH[c % 2][:, :], w1[i][:, c * P:(c + 1) * P], xT[:, :],
                                         start=True, stop=True).then_inc(h_ready, 1)

                def down(e, i, n):
                    pe.wait_ge(w2_in[i], (n + 1) * 16)
                    pe.wait_ge(h_stored, FC * e + FC + 2)
                    pe.wait_ge(y_added, e + 1)
                    for j in range(NT):
                        for c in range(FC):
                            last = nc.tensor.matmul(psY[i][:, j * D:(j + 1) * D], hT[i][:, c, j * P:(j + 1) * P],
                                                    w2[i][:, c, :], start=(c == 0), stop=(c == FC - 1))
                    last.then_inc(y_ready, 1)

                up(0, 0, 0)
                with pe.Fori(0, E_EXP // 2 - 1) as n:
                    up(2 * n + 1, 1, n)
                    down(2 * n, 0, n)
                    up(2 * n + 2, 0, n + 1)
                    down(2 * n + 1, 1, n)
                n = E_EXP // 2 - 1
                up(2 * n + 1, 1, n)
                down(2 * n, 0, n)
                down(2 * n + 1, 1, n)

            @block.scalar
            def _(act):
                act.sem_inc(h_stored, 2)
                act.wait_ge(x_transposed, 1)
                nc.scalar.copy(xT[:, :], psX[:, :]).then_inc(xT_ready, 1)
                with act.Fori(0, E_EXP // 2) as n:
                    for i in range(2):
                        e = 2 * n
                        act.wait_ge(y_added, e + i + 1)
                        for c in range(FC):
                            act.wait_ge(h_ready, FC * e + FC * i + c + 1)
                            nc.scalar.activation(hT[i][:, c, :], psH[c % 2][:, :], ACT.Gelu).then_inc(h_stored, 1)

            @block.vector
            def _(dve):
                dve.sem_inc(y_added, 2)
                ln.dve_stats(dve)
                dve.wait_ge(route_in, 32)
                dve.wait_ge(id_in, 16)
                for j in range(NT):
                    nc.vector.tensor_tensor(hit[:, j, :, :], over(idx[:, j, :], E_EXP), along(eid[:, :], TOPK),
                                            ALU.is_equal).then_inc(hit_ready, 1)
                for j in range(NT):
                    dve.wait_ge(hit_ready, j + 1)
                    nc.vector.tensor_tensor(share[:, j, :, :], hit[:, j, :, :], over(wts[:, j, :], E_EXP),
                                            ALU.mult).then_inc(share_ready, 1)
                dve.wait_ge(share_ready, NT)
                nc.vector.tensor_reduce(gate[:, :, :], share[:, :, :, :], AX, ALU.add).then_inc(gate_ready, 1)
                dve.wait_ge(ln.rstd_done, 1)
                for j in range(NT):
                    nc.vector.tensor_scalar(xh[:, j, :], x[:, j, :], ln.mv[:, j, 0:1], ln.rstd[:, j:j + 1],
                                            ALU.subtract, ALU.mult).then_inc(xh_ready, 1)
                dve.wait_ge(xh_ready, NT)
                dve.wait_ge(bias_in, 16)
                nc.vector.tensor_tensor(x[:, :, :], x[:, :, :], over(bias[:, :], B), ALU.add).then_inc(biased, 1)
                dve.wait_ge(biased, 1)
                dve.wait_ge(gate_ready, 1)
                with dve.Fori(0, E_EXP // 2) as n:
                    for i in range(2):
                        e = 2 * n
                        dve.wait_ge(y_ready, e + i + 1)
                        dve.wait_ge(y_added, e + i + 2)
                        for j in range(NT):
                            last = nc.vector.scalar_tensor_tensor(
                                x[:, j, :], psY[i][:, j * D:(j + 1) * D], gate[:, j, bass.ds(e + i, 1)],
                                x[:, j, :], ALU.mult, ALU.add)
                        last.then_inc(y_added, 1)
                dve.wait_ge(y_added, E_EXP + 2)


def rope_stage(nc, glob, dram):
    st = Stage(nc, "rope")
    with st.ctx:
        NG = H // G
        VW = HD_S + 1
        VB = H * VW
        HALF = HD_S // 2
        ln = LayerNorm(nc, st, glob)
        at = SoftmaxHeads(nc, st, glob, NG, float(HD_S) ** -0.5)
        there = Pipeline.there
        x = glob["x"]
        w, wo, bo = st.sb("w_qkv", [P, 3 * D]), st.sb("w_out", [P, D]), st.sb("b_out", [P, D])
        cos, sin = st.sb("cos", [P, HD_S]), st.sb("sin", [P, HD_S])
        own_rows = st.sb("own_rows", [P, H])
        v = st.sb("v", [P, B * VB + WIN])
        v4 = v[:, 0:B * VB].rearrange("p (b h e) -> p b h e", b=B, e=VW)
        rc, rsn, rot = (st.sb(n, [P, 2 * H, HD_S]) for n in ("rot_cos", "rot_sin", "rotated"))
        qT = [st.sb(f"qT{i}", [P, S]) for i in range(2)]
        kT = st.sb("kT", [P, S])
        kz = [st.sb(f"k_own{i}", [P, H, S]) for i in range(2)]
        rz, on, oT = st.sb("rz", [P, H]), st.sb("o", [P, H, HD_S]), st.sb("oT", [P, S])
        psP, psO, psY = st.ps("ps_proj"), [st.ps(f"ps_out{i}") for i in range(2)], st.ps("ps_y")
        psF, psX = psY[:, 256:256 + S], ln.psX
        w_in, tab_in, bo_in = st.sem("w_in"), st.sem("tab_in"), st.sem("bo_in")
        ones_ready = st.sem("ones_ready")
        proj, rc_ready, rs_ready = st.sem("proj"), st.sem("rc_ready"), st.sem("rs_ready")
        v_stored, rot_ready = st.sem("v_stored"), st.sem("rot_ready")
        qk_transposed, q_stored, k_stored = st.sem("qk_transposed"), st.sem("q_stored"), st.sem("k_stored")
        kz_ready = st.sem("kz_ready")
        rz_ready, on_ready, oT_ready = st.sem("rz_ready"), st.sem("o_ready"), st.sem("oT_ready")
        oT_stored, y_ready, yb_added, added = (st.sem("oT_stored"), st.sem("y_ready"), st.sem("bias_added"),
                                               st.sem("added"))

        with nc.Block() as block:
            @block.sync
            def _(sp):
                sp.dma_start(w[:, :], dram["L1_attn_w_qkv"]).then_inc(w_in, 16)
                sp.dma_start(wo[:, :], dram["L1_attn_w_out"]).then_inc(w_in, 16)
                sp.dma_start(cos[:, :], dram["c_rope8_cos"]).then_inc(tab_in, 16)
                sp.dma_start(sin[:, :], dram["c_rope8_sin"]).then_inc(tab_in, 16)
                sp.dma_start(own_rows[:, :], dram["c_own_rows8"]).then_inc(tab_in, 16)
                sp.dma_start(bo[:, :], dram["L1_attn_b_out"].unsqueeze(0).to_broadcast([P, D])).then_inc(bo_in, 16)

            @block.gpsimd
            def _(pool):
                nc.gpsimd.memset(v[:, :], 1.0).then_inc(ones_ready, 1)
                ln.pool_rstd(pool)
                pool.wait_ge(tab_in, 48)

                def slots(b, p, sb):
                    if there(sb, 1):
                        pool.wait_ge(k_stored, b + 2)
                        if there(sb, -1):
                            pool.wait_ge(at.scores_ready, b * NG)
                        nc.gpsimd.tensor_tensor(kz[1 - p][:, :, :], over(kT[:, :], H), along(own_rows[:, :], S),
                                                ALU.mult).then_inc(kz_ready, 1)

                Pipeline.run(pool, slots)

            @block.tensor
            def _(pe):
                at.credit(pe, at.transposed, at.values_done)
                pe.wait_ge(w_in, 32)

                def slots(b, p, sb):
                    def queries(b, off, g):
                        return qT[(p + off) % 2][:, :]

                    def keys(b, off, g):
                        if g == 0:
                            pe.wait_ge(kz_ready, b + off + 1)
                            pe.wait_ge(q_stored, b + off + 1)
                        return kz[(p + off) % 2][:, g * G:(g + 1) * G, :]

                    def product(probT, b, off, g, j):
                        if g == 0 and j == 0:
                            pe.wait_ge(v_stored, b + off + 1)
                        c = (g * G + j) * VW
                        return nc.tensor.matmul(psO[(p + off) % 2][:, c:c + WIN], probT,
                                                v[:, bass.ds((b + off) * VB + c, WIN)], start=True, stop=True)

                    for g in range(NG):
                        at.pe_slot(pe, b, sb, g, queries, keys, product)
                        if g == 1 and there(sb, 2):
                            if there(sb, 1):
                                pe.wait_ge(k_stored, b + 2)
                            ln.pe_transpose(pe, b + 2)
                        if g == 2 and there(sb, 2):
                            pe.wait_ge(ln.xT_ready, b + 3)
                            nc.tensor.matmul(psP[:, 0:3 * D], ln.xT[:, :], w[:, :], start=True,
                                             stop=True).then_inc(proj, 1)
                        if g == 3 and there(sb, -1):
                            pe.wait_ge(on_ready, b)
                            nc.tensor.transpose(psF, on[:, :, :].rearrange("p h e -> p (h e)"),
                                                glob["ident"][:, :]).then_inc(oT_ready, 1)
                        if g == 3 and there(sb, 2):
                            pe.wait_ge(rot_ready, b + 3)
                            for i in range(2):
                                last = nc.tensor.transpose(
                                    psX[:, i * S:(i + 1) * S],
                                    rot[:, i * H:(i + 1) * H, :].rearrange("p h e -> p (h e)"), glob["ident"][:, :])
                            last.then_inc(qk_transposed, 1)
                        if g == 3 and there(sb, -1):
                            pe.wait_ge(oT_stored, b)
                            nc.tensor.matmul(psY[:, 0:D], oT[:, :], wo[:, :], start=True,
                                             stop=True).then_inc(y_ready, 1)

                Pipeline.run(pe, slots)

            @block.scalar
            def _(act):
                at.credit(act, at.exp_done, at.probT_done)

                def slots(b, p, sb):
                    for g in range(NG):
                        at.act_slot(act, b, sb, g)
                        if g == 1 and there(sb, 2):
                            if there(sb, 1):
                                act.wait_ge(proj, b + 2)
                            ln.act_store(act, b + 2)
                        if g == 3 and there(sb, -1):
                            act.wait_ge(oT_ready, b)
                            nc.scalar.copy(oT[:, :], psF).then_inc(oT_stored, 1)
                        if g == 3 and there(sb, 2):
                            act.wait_ge(qk_transposed, b + 3)
                            nc.scalar.copy(qT[p][:, :], psX[:, 0:S]).then_inc(q_stored, 1)
                            if there(sb, 1):
                                act.wait_ge(kz_ready, b + 2)
                            nc.scalar.copy(kT[:, :], psX[:, S:2 * S]).then_inc(k_stored, 1)

                Pipeline.run(act, slots)

            @block.vector
            def _(dve):
                at.credit(dve, at.dif_done)
                ln.dve_stats(dve)
                dve.wait_ge(tab_in, 48)
                dve.wait_ge(bo_in, 16)
                dve.wait_ge(ones_ready, 1)

                def rotate(b, sb):
                    dve.wait_ge(proj, b + 1)
                    qk3 = psP[:, 0:2 * D].rearrange("p (h e) -> p h e", e=HD_S)
                    nc.vector.tensor_tensor(rc[:, :, :], qk3, over(cos[:, :], 2 * H), ALU.mult).then_inc(rc_ready, 1)
                    nc.vector.tensor_tensor(rsn[:, :, 0:HALF], qk3[:, :, HALF:], over(sin[:, 0:HALF], 2 * H), ALU.mult)
                    nc.vector.tensor_tensor(rsn[:, :, HALF:], qk3[:, :, 0:HALF], over(sin[:, HALF:], 2 * H),
                                            ALU.mult).then_inc(rs_ready, 1)
                    nc.vector.tensor_copy(v4[:, bass.ds(b, 1), :, 0:HD_S], psP[:, 2 * D:3 * D].rearrange(
                        "p (h e) -> p h e", e=HD_S)).then_inc(v_stored, 1)
                    if there(sb, -1):
                        dve.wait_ge(qk_transposed, b)
                    dve.wait_ge(rs_ready, b + 1)
                    nc.vector.tensor_tensor(rot[:, :, :], rc[:, :, :], rsn[:, :, :], ALU.add).then_inc(rot_ready, 1)

                def finish(b, p):
                    dve.wait_ge(at.values_done, NG * b + at.RING)
                    o3 = psO[p][:, 0:VB].rearrange("p (h e) -> p h e", e=VW)
                    nc.vector.reciprocal(rz[:, :], o3[:, :, HD_S]).then_inc(rz_ready, 1)
                    dve.wait_ge(rz_ready, b)
                    nc.vector.tensor_tensor(on[:, :, :], o3[:, :, 0:HD_S], along(rz[:, :], HD_S),
                                            ALU.mult).then_inc(on_ready, 1)

                def slots(b, p, sb):
                    for g in range(NG):
                        at.dve_slot(dve, b, sb, g)
                        if g == 0 and there(sb, 2):
                            if there(sb, 1):
                                dve.wait_ge(ln.psx_ready, b + 2)
                            ln.dve_normalise(dve, b + 2)
                        if g == 2 and there(sb, -1):
                            finish(b, 1 - p)
                        if g == 2 and there(sb, 2):
                            rotate(b + 2, sb + 2)
                        if g == 3 and there(sb, -1):
                            xb = x[:, bass.ds(b - 1, 1), :]
                            nc.vector.tensor_tensor(xb, xb, over(bo[:, :], 1), ALU.add).then_inc(yb_added, 1)
                            dve.wait_ge(y_ready, b)
                            dve.wait_ge(yb_added, b)
                            nc.vector.tensor_tensor(xb, xb, psY[:, 0:D], ALU.add).then_inc(added, 1)

                Pipeline.run(dve, slots)
                dve.wait_ge(added, B)


def cross_stage(nc, glob, dram):
    st = Stage(nc, "cross")
    with st.ctx:
        ln = LayerNorm(nc, st, glob)
        x, ctxT = glob["x"], glob["ctxT"]
        SCALE = float(D) ** -0.5
        names = ("Wq_c", "Wk_s", "Wq_s", "Wk_c")
        w = [st.sb(n, [P, D]) for n in names]
        bias = [st.sb("b" + n[1:], [P, 1]) for n in names]
        wvs, wvc = st.sb("Wv_s", [P, D]), st.sb("Wv_c", [P, D])
        bv = st.sb("bv", [P, 2, D])
        wg, bg = st.sb("Wg", [P, 2, D]), st.sb("bg", [P, D])
        VW = D + 1
        vs = st.sb("v_sub", [P, B, VW])
        vc = st.sb("v_char", [P, VW])
        qk = st.sb("qkT", [P, 4, S])
        mx, nmx = st.sb("row_max", [P, 2]), st.sb("minus_max", [P, 2])
        prob, probT = st.sb("prob", [P, 2, S]), st.sb("probT", [P, 2, S])
        rz = st.sb("rz", [P, 2])
        att = st.sb("attended", [P, 2, D])
        attT = st.sb("attendedT", [P, 2, D])
        zb, ez, den, gt, df, gd = (st.sb(n, [P, D]) for n in ("gate_in", "exp_gate", "den", "gate", "delta",
                                                             "gated"))
        psV = [st.ps("ps_proj0"), st.ps("ps_proj1")]
        psS, psT, psO, psG = st.ps("ps_scores"), st.ps("ps_T"), st.ps("ps_out"), st.ps("ps_gate")
        sems = ["w_in", "b_in", "bv_in", "ones_ready", "vs_proj", "vs_stored", "qk_proj", "qk_stored", "vc_proj",
                "vc_stored", "scores_ready", "max_done", "nmax_done", "exp_done", "transposed", "probT_stored",
                "out_ready", "rz_ready", "att_ready", "att_transposed", "attT_stored", "gate_mm", "zb_ready",
                "ez_ready", "den_ready", "gt_ready", "df_ready", "gd_ready", "s_added", "added"]
        q = {n: st.sem(n) for n in sems}

        with nc.Block() as block:
            @block.sync
            def _(sp):
                for i, n in enumerate(names):
                    sp.dma_start(w[i][:, :], dram["L1_xattn_" + n]).then_inc(q["w_in"], 16)
                    sp.dma_start(bias[i][:, :], dram["L1_xattn_b" + n[1:]].unsqueeze(1)).then_inc(q["b_in"], 16)
                sp.dma_start(wvs[:, :], dram["L1_xattn_Wv_s"]).then_inc(q["w_in"], 16)
                sp.dma_start(wvc[:, :], dram["L1_xattn_Wv_c"]).then_inc(q["w_in"], 16)
                sp.dma_start(wg[:, :, :], dram["L1_xattn_Wg"].rearrange("(c p) n -> p c n", p=P)).then_inc(q["w_in"], 16)
                for i, n in enumerate(("bv_s", "bv_c")):
                    sp.dma_start(bv[:, i, :], dram["L1_xattn_" + n].unsqueeze(0).to_broadcast([P, D])).then_inc(
                        q["bv_in"], 16)
                sp.dma_start(bg[:, :], dram["L1_xattn_bg"].unsqueeze(0).to_broadcast([P, D])).then_inc(q["bv_in"], 16)

            @block.gpsimd
            def _(pool):
                nc.gpsimd.memset(vs[:, :, :].rearrange("p b e -> p (b e)"), 1.0).then_inc(q["ones_ready"], 1)
                nc.gpsimd.memset(vc[:, :], 1.0).then_inc(q["ones_ready"], 1)
                ln.pool_rstd(pool)

            @block.tensor
            def _(pe):
                pe.wait_ge(q["w_in"], 7 * 16)
                for b in range(B):
                    nc.tensor.matmul(psV[b // 4][:, b % 4 * D:(b % 4 + 1) * D], ctxT[:, b, :], wvs[:, :],
                                     start=True, stop=True).then_inc(q["vs_proj"], 1)
                pe.wait_ge(q["vs_stored"], 2)
                with pe.Fori(0, B) as b:
                    ln.pe_transpose(pe, b)
                    pe.wait_ge(ln.xT_ready, b + 1)
                    for i in range(4):
                        rhs = ln.xT[:, :] if i in (0, 3) else ctxT[:, bass.ds(b, 1), :]
                        last = nc.tensor.matmul(psV[0][:, i * S:(i + 1) * S], w[i][:, :], rhs, start=True, stop=True)
                    last.then_inc(q["qk_proj"], 1)
                    nc.tensor.matmul(psV[1][:, 0:D], ln.xT[:, :], wvc[:, :], start=True, stop=True).then_inc(
                        q["vc_proj"], 1)
                    pe.wait_ge(q["qk_stored"], 4 * b + 4)
                    for m in range(2):
                        last = nc.tensor.matmul(psS[:, m * S:(m + 1) * S], qk[:, 2 * m, :], qk[:, 2 * m + 1, :],
                                                start=True, stop=True)
                    last.then_inc(q["scores_ready"], 1)
                    pe.wait_ge(q["exp_done"], 2 * b + 2)
                    for m in range(2):
                        last = nc.tensor.transpose(psT[:, m * S:(m + 1) * S], prob[:, m, :], glob["ident"][:, :])
                    last.then_inc(q["transposed"], 1)
                    pe.wait_ge(q["probT_stored"], b + 1)
                    pe.wait_ge(q["vc_stored"], b + 1)
                    nc.tensor.matmul(psO[:, 0:VW], probT[:, 0, :], vs[:, bass.ds(b, 1), :], start=True, stop=True)
                    nc.tensor.matmul(psO[:, 256:256 + VW], probT[:, 1, :], vc[:, :], start=True,
                                     stop=True).then_inc(q["out_ready"], 1)
                    pe.wait_ge(q["att_ready"], 2 * b + 2)
                    for m in range(2):
                        last = nc.tensor.transpose(psT[:, m * S:(m + 1) * S], att[:, m, :], glob["ident"][:, :])
                    last.then_inc(q["att_transposed"], 1)
                    pe.wait_ge(q["attT_stored"], b + 1)
                    for m in range(2):
                        last = nc.tensor.matmul(psG[:, 0:D], attT[:, m, :], wg[:, m, :], start=(m == 0), stop=(m == 1))
                    last.then_inc(q["gate_mm"], 1)

            @block.scalar
            def _(act):
                act.wait_ge(q["b_in"], 64)
                with act.Fori(0, B) as b:
                    ln.act_store(act, b)
                    act.wait_ge(q["qk_proj"], b + 1)
                    for i in range(4):
                        nc.scalar.activation(qk[:, i, :], psV[0][:, i * S:(i + 1) * S], ACT.Identity,
                                             bias=bias[i][:, 0:1]).then_inc(q["qk_stored"], 1)
                    act.wait_ge(q["nmax_done"], b + 1)
                    for m in range(2):
                        nc.scalar.activation(prob[:, m, :], psS[:, m * S:(m + 1) * S], ACT.Exp, bias=nmx[:, m:m + 1],
                                             scale=SCALE).then_inc(q["exp_done"], 1)
                    act.wait_ge(q["transposed"], b + 1)
                    nc.scalar.copy(probT[:, :, :], psT[:, 0:2 * S]).then_inc(q["probT_stored"], 1)
                    act.wait_ge(q["att_transposed"], b + 1)
                    nc.scalar.copy(attT[:, :, :], psT[:, 0:2 * S]).then_inc(q["attT_stored"], 1)
                    act.wait_ge(q["zb_ready"], b + 1)
                    nc.scalar.activation(ez[:, :], zb[:, :], ACT.Exp, scale=-1.0).then_inc(q["ez_ready"], 1)

            @block.vector
            def _(dve):
                def then(ins, name, b):
                    ins.then_inc(q[name], 1)
                    dve.wait_ge(q[name], b + 1)

                ln.dve_stats(dve)
                dve.wait_ge(q["ones_ready"], 2)
                dve.wait_ge(q["bv_in"], 48)
                for i in range(2):
                    dve.wait_ge(q["vs_proj"], 4 * i + 4)
                    nc.vector.tensor_copy(vs[:, 4 * i:4 * i + 4, 0:D],
                                          psV[i][:, :].rearrange("p (b e) -> p b e", b=4)).then_inc(q["vs_stored"], 1)
                with dve.Fori(0, B) as b:
                    ln.dve_normalise(dve, b)
                    dve.wait_ge(q["vc_proj"], b + 1)
                    nc.vector.tensor_copy(vc[:, 0:D], psV[1][:, 0:D]).then_inc(q["vc_stored"], 1)
                    dve.wait_ge(q["scores_ready"], b + 1)
                    then(nc.vector.tensor_reduce(mx[:, :], psS[:, 0:2 * S].rearrange("p (m t) -> p m t", m=2), AX,
                                                 ALU.max), "max_done", b)
                    nc.vector.tensor_scalar(nmx[:, :], mx[:, :], -SCALE, None, ALU.mult).then_inc(q["nmax_done"], 1)
                    dve.wait_ge(q["out_ready"], b + 1)
                    o3 = psO[:, :].rearrange("p (m c) -> p m c", m=2)
                    then(nc.vector.reciprocal(rz[:, :], o3[:, :, D]), "rz_ready", b)
                    for m in range(2):
                        nc.vector.scalar_tensor_tensor(att[:, m, :], o3[:, m, 0:D], rz[:, m:m + 1], bv[:, m, :],
                                                       ALU.mult, ALU.add).then_inc(q["att_ready"], 1)
                    dve.wait_ge(q["att_ready"], 2 * b + 2)
                    nc.vector.tensor_tensor(df[:, :], att[:, 0, :], att[:, 1, :], ALU.subtract).then_inc(
                        q["df_ready"], 1)
                    xb = x[:, bass.ds(b, 1), :]
                    nc.vector.tensor_tensor(xb, xb, over(att[:, 1, :], 1), ALU.add).then_inc(q["s_added"], 1)
                    dve.wait_ge(q["gate_mm"], b + 1)
                    nc.vector.tensor_tensor(zb[:, :], psG[:, 0:D], bg[:, :], ALU.add).then_inc(q["zb_ready"], 1)
                    dve.wait_ge(q["ez_ready"], b + 1)
                    then(nc.vector.tensor_scalar(den[:, :], ez[:, :], 1.0, None, ALU.add), "den_ready", b)
                    then(nc.vector.reciprocal(gt[:, :], den[:, :]), "gt_ready", b)
                    dve.wait_ge(q["df_ready"], b + 1)
                    then(nc.vector.tensor_tensor(gd[:, :], gt[:, :], df[:, :], ALU.mult), "gd_ready", b)
                    dve.wait_ge(q["s_added"], b + 1)
                    nc.vector.tensor_tensor(xb, xb, over(gd[:, :], 1), ALU.add).then_inc(q["added"], 1)
                dve.wait_ge(q["added"], B)


class Signal:

    CREDIT = 2

    def __init__(self, st, name, eng, by_engine):
        self.sem = st.sem(name)
        by_engine.setdefault(eng, []).append(self)

    def seen(self, n):
        return n + 1 + self.CREDIT

    def prior(self, n):
        return n + self.CREDIT

    def freed(self, n):
        return n - 1 + self.CREDIT


def local_stage(nc, glob, dram):
    st = Stage(nc, "loc")
    with st.ctx:
        x, ident = glob["x"], glob["ident"]
        C4 = 2 * INNER // BANK
        VC = INNER // BANK
        HP = BANK // HD_F
        QC = INNER // P
        NG = H // G
        VW = HD_F + 1
        HALF = HD_F // 2
        DH = D // 2
        FFN = "feed-forward"
        FCH = [P, P, DI - 2 * P]
        wqkv, wo = st.sb("w_qkv", [P, 3 * INNER]), st.sb("w_o", [P, QC, D])
        w1, w2 = st.sb("w1", [P, 2 * DI]), st.sb("w2", [P, 3, D])
        b1, lng, b2 = st.sb("b1", [P, 2, 3]), st.sb("ln_gb", [P, 2]), st.sb("b2", [P, D])
        shift = st.sb("shift", [P, P])
        band = st.sb("band", [P, S])
        identb, maskb = st.sb("ident_bf", [P, P], BF16), st.sb("mask_bf", [P, BANK], BF16)
        rotc, qks, rot = (st.sb(n, [P, 2, 2 * HD_F]) for n in ("rot_const", "qk_scale", "rot"))
        xin = st.sb("x_in", [P, D])
        xsT = [st.sb(f"xsT{i}", [P, S]) for i in range(2)]
        raw, sq, t1, t2, sm, qn = ([st.sb(f"{n}{i}", [P, HP, HD_F]) for i in range(2)]
                                   for n in ("raw", "squares", "rot_a", "rot_b", "rotated", "qk_norm"))
        ssq, ssc, rn = ([st.sb(f"{n}{i}", [P, HP]) for i in range(2)] for n in ("ssq", "ssq_max", "r_norm"))
        qT = [st.sb(f"qT{i}", [P, QC, S]) for i in range(2)]
        kT = [st.sb(f"kT{i}", [P, 2, QC, S]) for i in range(2)]
        v = [st.sb(f"v{i}", [P, H * VW + WIN]) for i in range(2)]
        v3 = [a[:, 0:H * VW].rearrange("p (h e) -> p h e", e=VW) for a in v]
        mx = [st.sb(f"row_max{i}", [P, G]) for i in range(2)]
        dif, prob, probT = ([st.sb(f"{n}{i}", [P, BANK]) for i in range(2)] for n in ("dif", "prob", "probT"))
        rz = st.sb("rz", [P, G])
        y, yT = st.sb("y", [P, INNER]), st.sb("yT", [P, INNER])
        HB = B // 2
        xs, xh = st.sb("xs", [P, HB, D]), st.sb("x_hat", [P, HB, D])
        stats, mv = st.sb("stats", [P, B, 6]), st.sb("mv", [P, B, 2])
        ve, rstd = st.sb("var_eps", [P, B]), st.sb("rstd", [P, B])
        ones = st.sb("ones", [P, HB * DH])
        xnT = st.sb("xnT", [P, BANK])
        gl = st.sb("gelu", [P, 3, BANK])
        hT = st.sb("hT", [P, 3, BANK])
        bank = [st.ps(f"bank{i}") for i in range(8)]
        psX, psQ, psS, psTP, psTQ, psO = bank[0], bank[1:3], bank[3:5], bank[5], bank[6], bank[7]
        psY = psX

        x0 = st.sb("x_before", [P, B, D])
        in_stats, in_mv, in_ve, in_rstd = (st.sem(n) for n in ("in_stats", "in_mv", "in_var_eps", "in_rstd"))
        x0_kept = st.sem("x0_kept")
        own = {}

        def sig(name, eng):
            return Signal(st, name, eng, own)

        const_in, wo_in, wf_in = st.sem("const_in"), st.sem("w_o_in"), st.sem("w_ffn_in")
        qks_in, piece_in = st.sem("qk_scale_in"), [st.sem(f"w_piece{k}_in") for k in range(C4 + VC)]
        band_in, bf_ready = st.sem("band_in"), st.sem("bf_ready")
        ones_ready, zeros_ready = st.sem("ones_ready"), st.sem("zeros_ready")
        rot_ready = sig("rot_ready", "dve")
        xin_ready = sig("xin_ready", "pool")
        psx_ready, xsT_ready = sig("psx_ready", "pe"), sig("xsT_ready", "act")
        psq_ready, psq_read = sig("psq_ready", "pe"), sig("psq_read", "act")
        sq_ready, rotab_ready = sig("sq_ready", "act"), sig("rotab_ready", "dve")
        ssq_ready, ssc_ready = sig("ssq_ready", "dve"), sig("ssc_ready", "dve")
        sum_ready, rn_ready, qn_ready = sig("sum_ready", "pool"), sig("rn_ready", "pool"), sig("qn_ready", "dve")
        qk_transposed, qk_stored = sig("qk_transposed", "pe"), sig("qk_stored", "act")
        scores_ready, max_ready, dif_ready = sig("scores_ready", "pe"), sig("max_ready", "dve"), sig("dif_ready", "dve")
        exp_ready, p_transposed, p_stored = sig("exp_ready", "act"), sig("p_transposed", "pe"), sig("p_stored", "act")
        out_ready, rz_ready, y_ready = sig("out_ready", "pe"), sig("rz_ready", "dve"), sig("y_ready", "dve")
        o_ready, added = sig("o_ready", "pe"), sig("added", "dve")
        xs0_ready, stats_ready = sig("xs0_ready", "pool"), sig("stats_ready", "dve")
        mv_ready, ve_ready = sig("mv_ready", "dve"), sig("ve_ready", "dve")
        rstd_ready, xh_ready, b2_added = sig("rstd_ready", "pool"), sig("xh_ready", "dve"), sig("b2_added", "pool")
        up_ready, h_ready = sig("up_ready", "pe"), sig("h_ready", "dve")
        down_ready, f_added = sig("down_ready", "pe"), sig("f_added", "dve")

        def load_piece(sp, l, k):
            sp.dma_start(wqkv[:, k * BANK:(k + 1) * BANK], dram["L1_ffn_Wqkv"][
                bass.ds(l, 1), :, k * BANK:(k + 1) * BANK].rearrange("a p n -> p (a n)")).then_inc(piece_in[k], 16)

        def load_qks(sp, l):
            sp.dma_start(qks[:, :, :], dram["qk_scale"][bass.ds(l, 1), :].to_broadcast([P, 4 * HD_F])).then_inc(
                qks_in, 16)

        def load_wo(sp, l):
            sp.dma_start(wo[:, :, :], dram["L1_ffn_Wo"][bass.ds(l, 1), :, :].rearrange(
                "a (c p) n -> p (a c) n", p=P)).then_inc(wo_in, 16)

        def load_ffn(sp, l):
            sp.dma_start(w1[:, :], dram["L1_ffn_W1"][bass.ds(l, 1), :, :].rearrange("a p n -> p (a n)")).then_inc(
                wf_in, 16)
            sp.dma_start(w2[:, :, :], dram["L1_ffn_W2"][bass.ds(l, 1), :, :].rearrange(
                "a (c p) n -> p (a c) n", p=P)).then_inc(wf_in, 16)
            sp.dma_start(b1[:, :, :], dram["L1_ffn_b1"][bass.ds(l, 1), :, :].rearrange(
                "a p n -> p (a n)")).then_inc(wf_in, 16)
            sp.dma_start(lng[:, :], dram["ln_gb"][bass.ds(l, 1), :, :].rearrange("a p n -> p (a n)")).then_inc(
                wf_in, 16)
            sp.dma_start(b2[:, :], dram["L1_ffn_b2"][bass.ds(l, 1), :].to_broadcast([P, D])).then_inc(wf_in, 16)

        with nc.Block() as block:
            @block.sync
            def _(sp):
                sp.dma_start(shift[:, :], dram["c_shift"]).then_inc(const_in, 16)
                sp.dma_start(rotc[:, :, :], dram["c_rot"]).then_inc(const_in, 16)
                for k in range(C4 + VC):
                    load_piece(sp, 0, k)
                load_qks(sp, 0)
                load_wo(sp, 0)
                load_ffn(sp, 0)
                sp.dma_start(band[:, :], dram["c_band"]).then_inc(band_in, 16)
                sp.wait_ge(const_in, 32)

            @block.gpsimd
            def _(pool):
                for i in range(2):
                    nc.gpsimd.memset(v[i][:, :], 1.0).then_inc(ones_ready, 1)
                for i in range(2):
                    nc.gpsimd.memset(kT[i][:, :, :, :].rearrange("p r c n -> p (r c n)"), 0.0).then_inc(zeros_ready, 1)
                for s in own["pool"]:
                    pool.sem_inc(s.sem, s.CREDIT)
                pool.wait_ge(in_ve, 1)
                nc.gpsimd.tensor_tensor(rstd[:, :], ve[:, :], glob["mhalf"][:, 0:B], ALU.pow).then_inc(in_rstd, 1)
                nc.gpsimd.memset(ones[:, :], 1.0).then_inc(ones_ready, 1)
                pool.wait_ge(ones_ready, 3)

            @block.tensor
            def _(pe):
                for s in own["pe"]:
                    pe.sem_inc(s.sem, s.CREDIT)

            @block.scalar
            def _(act):
                for s in own["act"]:
                    act.sem_inc(s.sem, s.CREDIT)
                nc.scalar.copy(x0[:, :, :], x[:, :, :]).then_inc(x0_kept, 1)
                nc.scalar.copy(identb[:, :], ident[:, :]).then_inc(bf_ready, 1)
                act.wait_ge(band_in, 16)
                nc.scalar.copy(maskb[:, :].rearrange("p (h m) -> p h m", h=G), over(band[:, :], G)).then_inc(
                    bf_ready, 1)

            @block.vector
            def _(dve):
                for s in own["dve"]:
                    dve.sem_inc(s.sem, s.CREDIT)
                for b in range(B):
                    nc.vector.bn_stats(stats[:, b, :], x[:, b, :]).then_inc(in_stats, 1)
                for b in range(B):
                    dve.wait_ge(in_stats, b + 1)
                    nc.vector.bn_aggr(mv[:, b, :], stats[:, b, :]).then_inc(in_mv, 1)
                dve.wait_ge(in_mv, B)
                nc.vector.tensor_scalar(ve[:, :], mv[:, :, 1], LN_EPS, None, ALU.add).then_inc(in_ve, 1)
                dve.wait_ge(in_rstd, 1)
                dve.wait_ge(x0_kept, 1)
                for b in range(B):
                    nc.vector.tensor_scalar(x[:, b, :], x[:, b, :], mv[:, b, 0:1], rstd[:, b:b + 1],
                                            ALU.subtract, ALU.mult)

        ORDER = [(1, "qk3"), (1, "v0"), (FFN, "shift"), (2, "qk0"), (-1, "y0"), (FFN, "xh"), (2, "qk1"), (-1, "y1"),
                 (1, "v1"), (FFN, "gate0"), (FFN, "gate1"), (FFN, "gate2"), (2, "qk2")]
        FILL, PASS, DRAIN = range(-2, 2), range(2, B + 2), range(2, B + 2)

        def ffn_half(b):
            return {HB + 1: 0, B + 1: 1}.get(b)

        def there(sb, off):
            b, steps = sb
            return not (steps is FILL and b + off < 0 or steps is DRAIN and b + off >= B)

        def uses(sb, kind):
            return ffn_half(sb[0]) is not None if kind is FFN else there(sb, kind)

        def first_steps(steps):
            return [(b, FILL) for b in FILL] + ([] if steps is FILL else [(b, steps) for b in steps])

        def uses_before(sb, what):
            n = 0
            for step in first_steps(sb[1]):
                for kind, name in ORDER:
                    if step == sb and name == what:
                        return n
                    n += uses(step, kind)

        PASS_USES = sum(uses((b, PASS), kind) for b in PASS for kind, _ in ORDER)

        def use(l, sb, what):
            return l * PASS_USES + uses_before(sb, what)

        def before(sb):
            steps = first_steps(sb[1])
            return steps[steps.index(sb) - 1]

        def last_use(sb):
            return "qk2" if there(sb, 2) else "v1" if there(sb, 1) else "y1"

        def bank_of(sb, what):
            return psQ[uses_before(sb, what) % 2]

        def pipeline(eng, slots):
            for b in FILL:
                slots(0, b, b % 2, (b, FILL))
            with eng.Fori(0, DEPTH - 1) as l:
                for b in PASS:
                    slots(l, b, b % 2, (b, PASS))
            for b in DRAIN:
                slots(DEPTH - 1, b, b % 2, (b, DRAIN))

        def lag(g, n):
            return (0, g - n) if 0 <= g - n < 4 else ((-1, g - n + 4) if g < n else (1, g - n - 4))

        PIECE_LEAD = 7

        def piece_at(g, behind=0):
            n = g + PIECE_LEAD - behind
            return n // 4, n % 4

        with nc.Block() as block:
            @block.sync
            def _(sp):
                with sp.Fori(0, DEPTH - 1) as l:
                    sp.wait_ge(rot_ready.sem, rot_ready.seen(l))
                    load_qks(sp, l + 1)
                    for b, what, k in ((HB + 1, "qk0", 0), (HB + 1, "qk1", 1), (HB + 1, "qk2", 2),
                                       (HB + 2, "qk3", 3), (HB + 2, "v0", 4), (HB + 2, "v1", 5)):
                        sp.wait_ge(psq_ready.sem, psq_ready.seen(use(l, (b, PASS), what)))
                        load_piece(sp, l + 1, k)
                    sp.wait_ge(o_ready.sem, o_ready.seen(l * B + B - 1))
                    load_wo(sp, l + 1)
                    sp.wait_ge(b2_added.sem, b2_added.seen(2 * l + 1))
                    sp.wait_ge(down_ready.sem, down_ready.seen(2 * l + 1))
                    load_ffn(sp, l + 1)

            @block.gpsimd
            def _(pool):
                def pool_copy(to, a):
                    one = ones[:, 0:D] if len(a.shape) == 2 else ones[:, :].rearrange("p (b e) -> p b e", b=HB)
                    return nc.gpsimd.tensor_tensor(to, a, one, ALU.mult)

                def front(t, k):
                    n = t * C4 + k
                    i = k % 2
                    pool.wait_ge(ssc_ready.sem, ssc_ready.seen(n))
                    nc.gpsimd.tensor_tensor(rn[i][:, :], ssc[i][:, :], glob["mhalf"][:, 0:HP],
                                            ALU.pow).then_inc(rn_ready.sem, 1)
                    pool.wait_ge(rotab_ready.sem, rotab_ready.seen(n))
                    pool.wait_ge(qn_ready.sem, qn_ready.freed(n))
                    nc.gpsimd.tensor_tensor(sm[i][:, :, :], t1[i][:, :, :], t2[i][:, :, :],
                                            ALU.add).then_inc(sum_ready.sem, 1)

                def slots(l, b, p, sb):
                    half = ffn_half(b)
                    for g in range(NG):
                        if g == 0 and there(sb, 2):
                            if b == HB + 2 or sb == (2, PASS) or sb == (2, DRAIN):
                                pool.wait_ge(f_added.sem, f_added.seen(2 * l + (0 if b == HB + 2 else -1)))
                            pool_copy(xin[:, :], x[:, (b + 2) % B, :]).then_inc(xin_ready.sem, 1)
                        if half is not None:
                            f, hb = 2 * l + half, slice(half * HB, (half + 1) * HB)
                            if g == 0:
                                pool.wait_ge(added.sem, added.seen(l * B + half * HB + HB - 1))
                                pool.wait_ge(xh_ready.sem, xh_ready.prior(f))
                                pool_copy(xs[:, :, 0:DH], x[:, hb, 0:DH]).then_inc(xs0_ready.sem, 1)
                            if g == 1:
                                pool.wait_ge(ve_ready.sem, ve_ready.seen(f))
                                nc.gpsimd.tensor_tensor(rstd[:, 0:HB], ve[:, 0:HB], glob["mhalf"][:, 0:HB],
                                                        ALU.pow).then_inc(rstd_ready.sem, 1)
                        off, k = piece_at(g)
                        if there(sb, off):
                            front(l * B + b + off, k)
                        if half is not None and g == 1:
                            pool.wait_ge(wf_in, (l + 1) * 80)
                            pool.wait_ge(xs0_ready.sem, xs0_ready.seen(f))
                            pool.wait_ge(psq_ready.sem, psq_ready.seen(use(l, sb, "shift")))
                            nc.gpsimd.tensor_tensor(x[:, hb, :], x[:, hb, :], over(b2[:, :], HB),
                                                    ALU.add).then_inc(b2_added.sem, 1)

                pipeline(pool, slots)

            @block.tensor
            def _(pe):
                def shifted(t, full):
                    if full:
                        pe.wait_ge(added.sem, added.seen(t - 4))
                    pe.wait_ge(xin_ready.sem, xin_ready.seen(t))
                    nc.tensor.matmul(psX[0:DH, 0:S], xin[:, 0:DH], ident[:, :], start=True, stop=True)
                    nc.tensor.matmul(psX[DH:D, 0:S], xin[:, DH:D], shift[:, :], start=True,
                                     stop=True).then_inc(psx_ready.sem, 1)

                def project(l, b, sb, off, what, p, k):
                    if what == "qk0":
                        pe.wait_ge(xsT_ready.sem, xsT_ready.seen(l * B + b + off))
                    if (b + off) % B == 0:
                        pe.wait_ge(piece_in[k], (l + 1 + (b + off) // B) * 16)
                    pe.wait_ge(psq_read.sem, psq_read.freed(use(l, sb, what)))
                    nc.tensor.matmul(bank_of(sb, what)[:, :], xsT[p][:, :], wqkv[:, k * BANK:(k + 1) * BANK],
                                     start=True, stop=True).then_inc(psq_ready.sem, 1)

                def turn_qk(t, k):
                    n = t * C4 + k
                    pe.wait_ge(qn_ready.sem, qn_ready.seen(n))
                    pe.wait_ge(qk_stored.sem, qk_stored.prior(n))
                    for c in range(4):
                        last = nc.tensor.transpose(psTQ[:, c * S:(c + 1) * S],
                                                   qn[k % 2][:, 2 * c:2 * c + 2, :].rearrange("p h e -> p (h e)"),
                                                   ident[:, :])
                    last.then_inc(qk_transposed.sem, 1)

                def scores(t, p, g):
                    n = t * NG + g
                    if g == 0:
                        pe.wait_ge(qk_stored.sem, qk_stored.seen(t * C4 + C4 - 1))
                    pe.wait_ge(dif_ready.sem, dif_ready.freed(n))
                    ps = psS[g % 2]
                    nc.tensor.matmul(ps[:, :], identb[:, :], maskb[:, :], start=True, stop=False)
                    for j in range(G):
                        c = g % 2 * G + j
                        last = nc.tensor.matmul(ps[:, j * S:(j + 1) * S], qT[p][:, c, :],
                                                kT[p][:, g // 2, c, :], start=False, stop=(j == G - 1))
                    last.then_inc(scores_ready.sem, 1)

                def turn_p(t, g):
                    n = t * NG + g
                    pe.wait_ge(exp_ready.sem, exp_ready.seen(n))
                    pe.wait_ge(p_stored.sem, p_stored.prior(n))
                    for j in range(G):
                        last = nc.tensor.transpose(psTP[:, j * S:(j + 1) * S],
                                                   prob[g % 2][:, j * S:(j + 1) * S], ident[:, :])
                    last.then_inc(p_transposed.sem, 1)

                def values(l, b, t, p, g, sb):
                    n = t * NG + g
                    pe.wait_ge(p_stored.sem, p_stored.seen(n))
                    pe.wait_ge(y_ready.sem, y_ready.prior(n))
                    if g == 0:
                        pe.wait_ge(psq_read.sem, psq_read.seen(use(l, before(sb), last_use(before(sb)))))
                    if g == 1 and ffn_half(b) is not None:
                        pe.wait_ge(h_ready.sem, h_ready.seen((2 * l + ffn_half(b)) * 3 + 2))
                    if g == 2 and b == HB + 2:
                        pe.wait_ge(f_added.sem, f_added.seen(2 * l))
                    if g == 2 and sb in ((2, PASS), (2, DRAIN)):
                        pe.wait_ge(f_added.sem, f_added.seen(2 * l - 1))
                    for j in range(G):
                        c = (g * G + j) * VW
                        last = nc.tensor.matmul(psO[:, j * S:j * S + WIN], probT[g % 2][:, j * S:(j + 1) * S],
                                                v[p][:, c:c + WIN], start=True, stop=True)
                    last.then_inc(out_ready.sem, 1)

                def turn_y(l, b, sb, i):
                    what = f"y{i}"
                    pe.wait_ge(psq_read.sem, psq_read.freed(use(l, sb, what)))
                    pe.wait_ge(y_ready.sem, y_ready.seen((l * B + b - 1) * NG + 2 * i + 1))
                    for c in range(4):
                        cc = 4 * i + c
                        last = nc.tensor.transpose(bank_of(sb, what)[:, c * S:(c + 1) * S],
                                                   y[:, cc * P:(cc + 1) * P], ident[:, :])
                    last.then_inc(psq_ready.sem, 1)

                def output(l, b, sb):
                    pe.wait_ge(psq_read.sem, psq_read.seen(use(l, sb, "y1")))
                    if b % B == 0:
                        pe.wait_ge(wo_in, (l + 1 + b // B) * 16)
                    for c in range(QC):
                        last = nc.tensor.matmul(psY[:, 0:D], yT[:, c * P:(c + 1) * P], wo[:, c, :],
                                                start=(c == 0), stop=(c == QC - 1))
                    last.then_inc(o_ready.sem, 1)

                def ffn_shift(l, f, sb, half):
                    pe.wait_ge(psq_read.sem, psq_read.freed(use(l, sb, "shift")))
                    pe.wait_ge(added.sem, added.seen(l * B + half * HB + HB - 1))
                    nc.tensor.matmul(bank_of(sb, "shift")[:, 0:HB * DH], shift[:, :],
                                     x[:, half * HB:(half + 1) * HB, DH:D], start=True, stop=True).then_inc(
                        psq_ready.sem, 1)

                def ffn_turn(l, f, sb):
                    pe.wait_ge(psq_read.sem, psq_read.freed(use(l, sb, "xh")))
                    pe.wait_ge(xh_ready.sem, xh_ready.seen(f))
                    for k in range(HB):
                        last = nc.tensor.transpose(bank_of(sb, "xh")[:, k * S:(k + 1) * S], xh[:, k, :], ident[:, :])
                    last.then_inc(psq_ready.sem, 1)

                def ffn_up(l, b, f, sb):
                    pe.wait_ge(wf_in, (l + 1) * 80)
                    pe.wait_ge(psq_read.sem, psq_read.seen(use(l, sb, "xh")))
                    if there(sb, 0):
                        pe.wait_ge(y_ready.sem, y_ready.seen((l * B + b) * NG))
                    for c in range(3):
                        what = f"gate{c}"
                        pe.wait_ge(psq_read.sem, psq_read.freed(use(l, sb, what)))
                        nc.tensor.matmul(bank_of(sb, what)[0:FCH[c], :], w1[:, DI + c * P:DI + c * P + FCH[c]],
                                         xnT[:, :], start=True, stop=True).then_inc(psq_ready.sem, 1)
                        pe.wait_ge(h_ready.sem, h_ready.prior(3 * f + c))
                        nc.tensor.matmul(psO[0:FCH[c], :], w1[:, c * P:c * P + FCH[c]],
                                         xnT[:, :], start=True, stop=True).then_inc(up_ready.sem, 1)

                def ffn_down(l, b, f, sb):
                    pe.wait_ge(h_ready.sem, h_ready.seen(3 * f + 2))
                    if there(sb, 0):
                        pe.wait_ge(y_ready.sem, y_ready.seen((l * B + b) * NG + 1))
                    for k in range(HB):
                        for c in range(3):
                            last = nc.tensor.matmul(psO[:, k * D:(k + 1) * D], hT[0:FCH[c], c, k * P:(k + 1) * P],
                                                    w2[0:FCH[c], c, :], start=(c == 0), stop=(c == 2))
                    last.then_inc(down_ready.sem, 1)

                def slots(l, b, p, sb):
                    half = ffn_half(b)
                    f = None if half is None else 2 * l + half
                    for g in range(NG):
                        off, k = lag(g, 1)
                        if there(sb, off):
                            turn_p(l * B + b + off, k)
                        off, k = piece_at(g)
                        if there(sb, off):
                            project(l, b, sb, off, f"qk{k}", (p + off) % 2, k)
                        off, k = lag(g, -1)
                        if there(sb, off):
                            scores(l * B + b + off, (p + off) % 2, k)
                        off, k = piece_at(g, 2)
                        if there(sb, off):
                            turn_qk(l * B + b + off, k)
                        off, k = lag(g, 2)
                        if there(sb, off):
                            values(l, b, l * B + b + off, (p + off) % 2, k, sb)
                        if g == 0 and there(sb, 1):
                            project(l, b, sb, 1, "v0", (p + 1) % 2, C4)
                        if g == 0 and half is not None:
                            ffn_shift(l, f, sb, half)
                        if g == 0 and there(sb, 2):
                            shifted(l * B + b + 2, sb[1] is not FILL)
                        if g == 1 and there(sb, -1):
                            turn_y(l, b, sb, 0)
                        if g == 1 and half is not None:
                            ffn_turn(l, f, sb)
                        if g == 2:
                            if there(sb, -1):
                                turn_y(l, b, sb, 1)
                            if there(sb, 1):
                                project(l, b, sb, 1, "v1", (p + 1) % 2, C4 + 1)
                            if half is not None:
                                ffn_up(l, b, f, sb)
                        if g == 3:
                            if there(sb, -1):
                                output(l, b - 1, sb)
                            if half is not None:
                                ffn_down(l, b, f, sb)

                pipeline(pe, slots)

            @block.scalar
            def _(act):
                def store_x(t, p):
                    act.wait_ge(psx_ready.sem, psx_ready.seen(t))
                    nc.scalar.copy(xsT[p][:, :], psX[:, 0:S]).then_inc(xsT_ready.sem, 1)

                def store_raw(l, t, sb, k):
                    n = t * C4 + k
                    what = f"qk{k}"
                    act.wait_ge(psq_ready.sem, psq_ready.seen(use(l, sb, what)))
                    act.wait_ge(ssq_ready.sem, ssq_ready.freed(n))
                    nc.scalar.square(sq[k % 2][:, :, :], bank_of(sb, what)[:, :]).then_inc(sq_ready.sem, 1)
                    act.wait_ge(rotab_ready.sem, rotab_ready.freed(n))
                    nc.scalar.copy(raw[k % 2][:, :, :], bank_of(sb, what)[:, :]).then_inc(psq_read.sem, 1)

                def store_v(l, sb, p, i):
                    u = use(l, sb, f"v{i}")
                    act.wait_ge(psq_ready.sem, psq_ready.seen(u))
                    nc.scalar.copy(v3[p][:, i * HP:(i + 1) * HP, 0:HD_F],
                                   bank_of(sb, f"v{i}")[:, :].rearrange("p (h e) -> p h e", h=HP)).then_inc(
                        psq_read.sem, 1)

                def store_qk(t, p, k):
                    n = t * C4 + k
                    c = k % 2 * 4
                    act.wait_ge(qk_transposed.sem, qk_transposed.seen(n))
                    if k < 2:
                        nc.scalar.copy(qT[p][:, c:c + 4, :], psTQ[:, :]).then_inc(qk_stored.sem, 1)
                    else:
                        nc.scalar.copy(kT[p][0:HD_F, 0, c:c + 4, :], psTQ[0:HD_F, :])
                        nc.scalar.copy(kT[p][HD_F:P, 1, c:c + 4, :], psTQ[HD_F:P, :]).then_inc(qk_stored.sem, 1)

                def exponent(t, g):
                    n = t * NG + g
                    act.wait_ge(dif_ready.sem, dif_ready.seen(n))
                    act.wait_ge(p_transposed.sem, p_transposed.freed(n))
                    nc.scalar.activation(prob[g % 2][:, :], dif[g % 2][:, :], ACT.Exp).then_inc(exp_ready.sem, 1)

                def store_p(t, g):
                    n = t * NG + g
                    act.wait_ge(p_transposed.sem, p_transposed.seen(n))
                    act.wait_ge(out_ready.sem, out_ready.freed(n))
                    nc.scalar.copy(probT[g % 2][:, :], psTP[:, :]).then_inc(p_stored.sem, 1)

                def store_y(l, sb, i):
                    act.wait_ge(psq_ready.sem, psq_ready.seen(use(l, sb, f"y{i}")))
                    nc.scalar.copy(yT[:, i * BANK:(i + 1) * BANK], bank_of(sb, f"y{i}")[:, :]).then_inc(
                        psq_read.sem, 1)

                def ffn_store_shift(l, sb):
                    act.wait_ge(psq_ready.sem, psq_ready.seen(use(l, sb, "shift")))
                    nc.scalar.copy(xs[:, :, DH:D], bank_of(sb, "shift")[:, 0:HB * DH].rearrange(
                        "p (b e) -> p b e", b=HB)).then_inc(psq_read.sem, 1)

                def ffn_store_xn(l, sb):
                    act.wait_ge(wf_in, (l + 1) * 80)
                    act.wait_ge(psq_ready.sem, psq_ready.seen(use(l, sb, "xh")))
                    nc.scalar.activation(xnT[:, :], bank_of(sb, "xh")[:, :], ACT.Identity,
                                         bias=lng[:, 1:2], scale=lng[:, 0:1]).then_inc(psq_read.sem, 1)

                def ffn_gelu(l, sb):
                    for c in range(3):
                        what = f"gate{c}"
                        act.wait_ge(psq_ready.sem, psq_ready.seen(use(l, sb, what)))
                        nc.scalar.activation(gl[0:FCH[c], c, :], bank_of(sb, what)[0:FCH[c], :], ACT.Gelu,
                                             bias=b1[0:FCH[c], 1, c:c + 1]).then_inc(psq_read.sem, 1)

                act.wait_ge(zeros_ready, 2)

                def slots(l, b, p, sb):
                    half = ffn_half(b)
                    for g in range(NG):
                        off, k = piece_at(g)
                        if there(sb, off):
                            store_raw(l, l * B + b + off, sb, k)
                        off, k = lag(g, 1)
                        if there(sb, off):
                            store_p(l * B + b + off, k)
                        off, k = lag(g, 0)
                        if there(sb, off):
                            exponent(l * B + b + off, k)
                        off, k = piece_at(g, 2)
                        if there(sb, off):
                            store_qk(l * B + b + off, (p + off) % 2, k)
                        if g == 0 and there(sb, 1):
                            store_v(l, sb, (p + 1) % 2, 0)
                        if g == 0 and half is not None:
                            ffn_store_shift(l, sb)
                        if g == 0 and there(sb, 2):
                            store_x(l * B + b + 2, p)
                        if g == 1 and there(sb, -1):
                            store_y(l, sb, 0)
                        if g == 1 and half is not None:
                            ffn_store_xn(l, sb)
                        if g == 2:
                            if there(sb, -1):
                                store_y(l, sb, 1)
                            if there(sb, 1):
                                store_v(l, sb, (p + 1) % 2, 1)
                            if half is not None:
                                ffn_gelu(l, sb)

                pipeline(act, slots)

            @block.vector
            def _(dve):
                def rotation(l):
                    dve.wait_ge(qks_in, (l + 1) * 16)
                    nc.vector.tensor_tensor(rot[:, :, :], rotc[:, :, :], qks[:, :, :], ALU.mult).then_inc(
                        rot_ready.sem, 1)
                    dve.wait_ge(rot_ready.sem, rot_ready.seen(l))

                def guard(t, k):
                    n = t * C4 + k
                    i = k % 2
                    dve.wait_ge(ssq_ready.sem, ssq_ready.seen(n))
                    dve.wait_ge(rn_ready.sem, rn_ready.freed(n))
                    nc.vector.tensor_scalar(ssc[i][:, :], ssq[i][:, :], 1e-24, None, ALU.max).then_inc(
                        ssc_ready.sem, 1)

                def rotate(l, t, sb, k):
                    n = t * C4 + k
                    i, kind = k % 2, k // 2
                    cos, sin = rot[:, kind, 0:HD_F], rot[:, kind, HD_F:]
                    dve.wait_ge(psq_read.sem, psq_read.seen(use(l, sb, f"qk{k}")))
                    dve.wait_ge(sum_ready.sem, sum_ready.freed(n))
                    nc.vector.tensor_tensor(t1[i][:, :, :], raw[i][:, :, :], over(cos, HP), ALU.mult)
                    guard(t, k)
                    nc.vector.tensor_tensor(t2[i][:, :, 0:HALF], raw[i][:, :, HALF:], over(sin[:, 0:HALF], HP),
                                            ALU.mult)
                    nc.vector.tensor_tensor(t2[i][:, :, HALF:], raw[i][:, :, 0:HALF], over(sin[:, HALF:], HP),
                                            ALU.mult).then_inc(rotab_ready.sem, 1)

                def norms(t, k):
                    n = t * C4 + k
                    i = k % 2
                    dve.wait_ge(sq_ready.sem, sq_ready.seen(n))
                    nc.vector.tensor_reduce(ssq[i][:, :], sq[i][:, :, :], AX, ALU.add).then_inc(ssq_ready.sem, 1)

                def scale_qk(t, k):
                    n = t * C4 + k
                    i = k % 2
                    dve.wait_ge(sum_ready.sem, sum_ready.seen(n))
                    dve.wait_ge(rn_ready.sem, rn_ready.seen(n))
                    dve.wait_ge(qk_transposed.sem, qk_transposed.freed(n))
                    nc.vector.tensor_tensor(qn[i][:, :, :], sm[i][:, :, :], along(rn[i][:, :], HD_F),
                                            ALU.mult).then_inc(qn_ready.sem, 1)

                def maxima(t, g):
                    n = t * NG + g
                    i = g % 2
                    s3 = psS[i][:, :].rearrange("p (h m) -> p h m", h=G)
                    dve.wait_ge(scores_ready.sem, scores_ready.seen(n))
                    nc.vector.tensor_reduce(mx[i][:, :], s3, AX, ALU.max).then_inc(max_ready.sem, 1)

                def less_max(t, g):
                    n = t * NG + g
                    i = g % 2
                    s3 = psS[i][:, :].rearrange("p (h m) -> p h m", h=G)
                    dve.wait_ge(exp_ready.sem, exp_ready.freed(n))
                    dve.wait_ge(max_ready.sem, max_ready.seen(n))
                    nc.vector.tensor_tensor(dif[i][:, :].rearrange("p (h m) -> p h m", h=G), s3,
                                            along(mx[i][:, :], S), ALU.subtract).then_inc(dif_ready.sem, 1)

                def row_sums(t, g):
                    n = t * NG + g
                    o3 = psO[:, :].rearrange("p (h e) -> p h e", h=G)
                    dve.wait_ge(out_ready.sem, out_ready.seen(n))
                    nc.vector.reciprocal(rz[:, :], o3[:, :, HD_F]).then_inc(rz_ready.sem, 1)

                def normalise(l, t, g, sb):
                    n = t * NG + g
                    o3 = psO[:, :].rearrange("p (h e) -> p h e", h=G)
                    dve.wait_ge(rz_ready.sem, rz_ready.seen(n))
                    if g == 0 and there(sb, -1):
                        dve.wait_ge(psq_ready.sem, psq_ready.seen(use(l, sb, "y0")))
                    if g == 2 and there(sb, -2):
                        at = before(sb)
                        dve.wait_ge(psq_ready.sem, psq_ready.seen(use(l, at, last_use(at))))
                    nc.vector.tensor_tensor(
                        y[:, g * G * HD_F:(g + 1) * G * HD_F].rearrange("p (h e) -> p h e", h=G),
                        o3[:, :, 0:HD_F], along(rz[:, :], HD_F), ALU.mult).then_inc(y_ready.sem, 1)

                def ffn_stats(l, f, sb):
                    dve.wait_ge(xs0_ready.sem, xs0_ready.seen(f))
                    dve.wait_ge(psq_read.sem, psq_read.seen(use(l, sb, "shift")))
                    for k in range(HB):
                        nc.vector.bn_stats(stats[:, k, :], xs[:, k, :]).then_inc(stats_ready.sem, 1)

                def ffn_moments(f):
                    for k in range(HB):
                        nc.vector.bn_aggr(mv[:, k, :], stats[:, k, :]).then_inc(mv_ready.sem, 1)
                    dve.wait_ge(mv_ready.sem, mv_ready.seen(f * HB + HB - 1))
                    nc.vector.tensor_scalar(ve[:, 0:HB], mv[:, 0:HB, 1], LN_EPS, None,
                                            ALU.add).then_inc(ve_ready.sem, 1)

                def ffn_norm(f):
                    dve.wait_ge(rstd_ready.sem, rstd_ready.seen(f))
                    for k in range(HB):
                        last = nc.vector.tensor_scalar(xh[:, k, :], xs[:, k, :], mv[:, k, 0:1], rstd[:, k:k + 1],
                                                       ALU.subtract, ALU.mult)
                    last.then_inc(xh_ready.sem, 1)

                def ffn_hidden(l, f, sb):
                    dve.wait_ge(wf_in, (l + 1) * 80)
                    for c in range(3):
                        dve.wait_ge(up_ready.sem, up_ready.seen(3 * f + c))
                        dve.wait_ge(psq_read.sem, psq_read.seen(use(l, sb, f"gate{c}")))
                        nc.vector.scalar_tensor_tensor(
                            hT[0:FCH[c], c, :], psO[0:FCH[c], :], b1[0:FCH[c], 0, c:c + 1],
                            gl[0:FCH[c], c, :], ALU.add, ALU.mult).then_inc(h_ready.sem, 1)

                def ffn_add(f, half):
                    dve.wait_ge(b2_added.sem, b2_added.seen(f))
                    dve.wait_ge(down_ready.sem, down_ready.seen(f))
                    xh4 = x[:, half * HB:(half + 1) * HB, :]
                    nc.vector.tensor_tensor(xh4, xh4, psO[:, :].rearrange("p (b e) -> p b e", b=HB),
                                            ALU.add).then_inc(f_added.sem, 1)

                def slots(l, b, p, sb):
                    half = ffn_half(b)
                    f = None if half is None else 2 * l + half
                    for g in range(NG):
                        score_off, sk = lag(g, 0)
                        piece_off, pk = piece_at(g)
                        if g == 1 and half is not None:
                            dve.wait_ge(stats_ready.sem, stats_ready.seen(f * HB + HB - 1))
                        if there(sb, score_off):
                            maxima(l * B + b + score_off, sk)
                        if g == 1 and half is not None:
                            ffn_moments(f)
                        if there(sb, score_off):
                            less_max(l * B + b + score_off, sk)
                        if there(sb, piece_off):
                            if (b + piece_off) % B == 0 and pk == 0:
                                rotation(l + (b + piece_off) // B)
                            norms(l * B + b + piece_off, pk)
                            rotate(l, l * B + b + piece_off, sb, pk)
                        off, k = lag(g, 2)
                        if there(sb, off):
                            row_sums(l * B + b + off, k)
                            normalise(l, l * B + b + off, k, sb)
                        off, k = piece_at(g, 1)
                        if there(sb, off):
                            scale_qk(l * B + b + off, k)
                        if half is not None:
                            if g == 0:
                                ffn_stats(l, f, sb)
                            if g == 1:
                                ffn_norm(f)
                            if g == 2:
                                ffn_hidden(l, f, sb)
                    if there(sb, -1):
                        t = l * B + b - 1
                        dve.wait_ge(o_ready.sem, o_ready.seen(t))
                        xb = x[:, (b - 1) % B, :]
                        nc.vector.tensor_tensor(xb, xb, psY[:, 0:D], ALU.add).then_inc(added.sem, 1)
                    if half is not None:
                        ffn_add(f, half)

                pipeline(dve, slots)

        with nc.Block() as block:
            @block.vector
            def _(dve):
                nc.vector.tensor_tensor(x[:, :, :], x[:, :, :], x0[:, :, :], ALU.add)


def store_stage(nc, glob, out):
    st = Stage(nc, "store")
    with st.ctx:
        stored = st.sem("out_stored")
        with nc.Block() as block:
            @block.sync
            def _(sp):
                sp.dma_start(out.rearrange("b p d -> p b d"), glob["x"][:, :, :]).then_inc(stored, 16)
                sp.wait_ge(stored, 16)


STAGES = [taylor_stage, diff_stage, expert_stage, rope_stage, cross_stage, local_stage]


def decoder(nc, dram, out):
    st = Stage(nc, "all")
    with st.ctx:
        glob = {"x": st.sb("x", [P, B, D]), "ident": st.sb("ident", [P, P]),
                "ctxT": st.sb("ctxT", [P, B, S]), "mhalf": st.sb("mhalf", [P, BANK // 4])}
        load_stage(nc, glob, dram)
        for stage in STAGES:
            stage(nc, glob, dram)
        store_stage(nc, glob, out)


def _pad_heads(w, hd):
    out = np.zeros((w.shape[0], NC, HC, PAD), w.dtype)
    out[..., :hd] = w.reshape(w.shape[0], HC, NC, hd).transpose(0, 2, 1, 3)
    return out.reshape(w.shape[0], H * PAD)


def _tables():
    t = {}
    t["c_ident"] = np.eye(P, dtype=np.float32)
    n = np.arange(P)
    t["c_experts"] = np.arange(E_EXP, dtype=np.float32)
    inv = 1.0 / 10000.0 ** (np.arange(0, HD_S, 2, dtype=np.float32) / np.float32(HD_S))
    f = n[:, None].astype(np.float32) * inv[None, :].astype(np.float32)
    t["c_rope8_cos"] = np.concatenate([np.cos(f)] * 2, 1).astype(np.float32)
    t["c_rope8_sin"] = np.concatenate([-np.sin(f), np.sin(f)], 1).astype(np.float32)
    half = np.arange(0, HD_F, 2, dtype=np.float64)
    f = n[:, None] * (1.0 / 10000.0 ** (half / HD_F))[None, :]
    power = (n - P // 2) / (WINDOW // 2)
    scale = ((half + 0.4 * HD_F) / (1.4 * HD_F))[None, :] ** power[:, None]
    rot = np.concatenate([np.cos(f), np.cos(f), -np.sin(f), np.sin(f)], 1)
    scale = np.concatenate([scale] * 4, 1)
    t["c_rot"] = np.stack([rot * scale * QK_SCALE, rot / scale], 1).astype(np.float32)
    t["c_shift"] = np.eye(P, k=1, dtype=np.float32)
    seen = (n[None, :] <= n[:, None]) & (n[None, :] >= n[:, None] - WINDOW)
    t["c_band"] = np.where(seen, 0.0, MASKED).astype(np.float32)
    t["c_own_rows8"] = (n[:, None] // HD_S == np.arange(H)[None, :]).astype(np.float32)
    t["c_causalT"] = (n[:, None] <= n[None, :]).astype(np.float32)
    return t


def _arrays(inputs):
    a = {k: np.ascontiguousarray(v) for k, v in inputs.items()}
    a["L0_attn_Wq"] = _pad_heads(a["L0_attn_Wq"], HD_A)
    a["L0_attn_Wk"] = _pad_heads(a["L0_attn_Wk"], HD_A)
    for n in ("wq1", "wk1", "wq2", "wk2", "wv"):
        full = np.zeros((H, HD_S, H, HD_S), np.float32)
        w = a["L0_xattn_" + n]
        for h in range(H):
            full[h, :, h, :] = w[h].T
        full = full.reshape(D, D)
        a["L0_xattn_" + n] = full
    for n in ("L0_xattn_wo", "L1_attn_w_qkv", "L1_attn_w_out", *("L1_xattn_" + m for m in (
            "Wq_c", "Wk_s", "Wv_s", "Wq_s", "Wk_c", "Wv_c", "Wg"))):
        a[n] = a[n].T
    w = a["L1_ffn_Wqkv"].reshape(DEPTH, D, 3, 2, 8, HD_F).copy()
    qk = w[:, :, 0:2].transpose(0, 1, 2, 4, 3, 5).reshape(DEPTH, D, 2 * INNER)
    a["L1_ffn_Wqkv"] = np.concatenate([qk, w[:, :, 2].reshape(DEPTH, D, INNER)], 2)
    a["qk_scale"] = np.concatenate([a[f"L1_ffn_{n}_scale"].reshape(DEPTH, 2, 32)[:, o, :].reshape(DEPTH, HD_F)
                                    for n in "qk" for o in ([0, 1], [1, 0])], 1)
    del a["L1_ffn_q_scale"], a["L1_ffn_k_scale"]
    a["ln_gb"] = np.stack([a.pop("L1_ffn_ln_g"), a.pop("L1_ffn_ln_b")], 2)
    rows = 3 * P - DI
    a["L1_ffn_W2"] = np.pad(a["L1_ffn_W2"], ((0, 0), (0, rows), (0, 0)))
    a["L1_ffn_b1"] = np.pad(a["L1_ffn_b1"].reshape(DEPTH, 2, DI), ((0, 0), (0, 0), (0, rows))).reshape(
        DEPTH, 6, P).transpose(0, 2, 1)
    a.update(_tables())
    a.pop("L0_ffn_scores")
    return {k: np.ascontiguousarray(v if v.ndim else v.reshape(1)) for k, v in a.items()}


def kernel(**inputs):
    import concourse.bacc as _bacc
    from concourse.bass_utils import run_bass_kernel_spmd as _run

    nc = _bacc.Bacc("TRN2", target_bir_lowering=False, num_devices=1)
    arrays = {f"in_{k}": v for k, v in _arrays(inputs).items()}
    dram = {k[3:]: nc.dram_tensor(k, v.shape, mybir.dt.from_np(v.dtype), kind="ExternalInput").ap()
            for k, v in arrays.items()}
    out = nc.dram_tensor("out_x", (B, S, D), F32, kind="ExternalOutput").ap()
    decoder(nc, dram, out)
    return _run(nc, [arrays], core_ids=[0]).results[0]["out_x"]
```

```python
from contextlib import ExitStack

import numpy as np

import concourse.bass as bass
from concourse import mybir

P = 128
B, S, D = 8, 128, 128
H = 16
G = 4
BANK = 512
WIN = 96
HD_A, VD_A = 16, 64
HD_S = 8
E_EXP, FF, TOPK = 8, 512, 2
MOE_T = 512
HD_F, WINDOW, DEPTH, INNER, DI = 64, 32, 6, 1024, 341
QK_SCALE, MASKED = 8.0, -1e30
LN_EPS = 1e-5

F32 = mybir.dt.float32
BF16 = mybir.dt.bfloat16
I32 = mybir.dt.int32
ALU = mybir.AluOpType
ACT = mybir.ActivationFunctionType
AX = mybir.AxisListType.X


class Stage:

    def __init__(self, nc, name):
        self.nc, self.name, self.ctx, self.sems = nc, name, ExitStack(), []
        self.ctx.callback(self.clear)

    def clear(self):
        if self.sems:
            self.nc.clear_and_free_semaphores(self.sems)
            self.nc.all_engine_barrier()

    def sb(self, name, shape, dt=F32):
        return self.ctx.enter_context(self.nc.sbuf_tensor(f"{self.name}_{name}", shape, dt))

    def ps(self, name, cols=BANK):
        return self.ctx.enter_context(self.nc.psum_tensor(f"{self.name}_{name}", [P, cols], F32))

    def sem(self, name):
        self.sems.append(self.nc.alloc_semaphore(f"{self.name}_{name}"))
        return self.sems[-1]


def over(ap, n):
    return ap.unsqueeze(1).to_broadcast([ap.shape[0], n, ap.shape[1]])


def along(ap, n):
    return ap.unsqueeze(2).to_broadcast([ap.shape[0], ap.shape[1], n])


class LayerNorm:

    def __init__(self, nc, st, glob, count=B):
        self.nc, self.x, self.g, self.n = nc, glob["x"], glob, count
        self.stats = st.sb("ln_stats", [P, B, 6])
        self.mv = st.sb("ln_mv", [P, B, 2])
        self.ve = st.sb("ln_var_eps", [P, B])
        self.rstd = st.sb("ln_rstd", [P, B])
        self.xh = st.sb("x_hat", [P, D])
        self.xT = st.sb("x_hat_T", [P, S])
        self.psX = st.ps("ps_x")
        self.stats_done = st.sem("ln_stats_done")
        self.mv_done = st.sem("ln_mv_done")
        self.ve_done = st.sem("ln_ve_done")
        self.rstd_done = st.sem("ln_rstd_done")
        self.xh_ready = st.sem("xh_ready")
        self.psx_ready = st.sem("psx_ready")
        self.xT_ready = st.sem("xT_ready")

    def dve_stats(self, dve):
        nc, n = self.nc, self.n
        for b in range(n):
            nc.vector.bn_stats(self.stats[:, b, :], self.x[:, b, :]).then_inc(self.stats_done, 1)
        for b in range(n):
            dve.wait_ge(self.stats_done, b + 1)
            nc.vector.bn_aggr(self.mv[:, b, :], self.stats[:, b, :]).then_inc(self.mv_done, 1)
        dve.wait_ge(self.mv_done, n)
        nc.vector.tensor_scalar(self.ve[:, 0:n], self.mv[:, 0:n, 1], LN_EPS, None,
                                ALU.add).then_inc(self.ve_done, 1)

    def pool_rstd(self, pool):
        pool.wait_ge(self.ve_done, 1)
        self.nc.gpsimd.tensor_tensor(self.rstd[:, 0:self.n], self.ve[:, 0:self.n],
                                     self.g["mhalf"][:, 0:self.n], ALU.pow).then_inc(self.rstd_done, 1)

    def dve_normalise(self, dve, b):
        dve.wait_ge(self.rstd_done, 1)
        self.nc.vector.tensor_scalar(self.xh[:, :], self.x[:, bass.ds(b, 1), :],
                                     self.mv[:, bass.ds(b, 1), 0], self.rstd[:, bass.ds(b, 1)],
                                     ALU.subtract, ALU.mult).then_inc(self.xh_ready, 1)

    def pe_transpose(self, pe, b):
        pe.wait_ge(self.xh_ready, b + 1)
        self.nc.tensor.transpose(self.psX[:, 0:S], self.xh[:, :],
                                 self.g["ident"][:, :]).then_inc(self.psx_ready, 1)

    def act_store(self, act, b):
        act.wait_ge(self.psx_ready, b + 1)
        self.nc.scalar.copy(self.xT[:, :], self.psX[:, 0:S]).then_inc(self.xT_ready, 1)


class Pipeline:

    FIRST, LAST = -2, B
    LOOP = (1, 5)

    @classmethod
    def run(cls, eng, slots):
        for b in range(cls.FIRST, cls.LOOP[0]):
            slots(b, b % 2, b)
        with eng.Fori(0, (cls.LOOP[1] - cls.LOOP[0]) // 2) as n:
            for i in range(2):
                slots(2 * n + (cls.LOOP[0] + i), (cls.LOOP[0] + i) % 2, cls.LOOP[0] + i)
        for b in range(cls.LOOP[1], cls.LAST + 1):
            slots(b, b % 2, b)

    @staticmethod
    def there(sb, off):
        return 0 <= sb + off < B


def ago(g, n, groups):
    return (g - n) // groups, (g - n) % groups


class SoftmaxHeads:

    RING = 2

    def __init__(self, nc, st, glob, groups, scale):
        self.nc, self.groups, self.scale, self.g = nc, groups, scale, glob
        self.psS = [st.ps(f"ps_scores{i}") for i in range(2)]
        self.psT = st.ps("ps_probsT")
        self.mx = [st.sb(f"row_max{i}", [P, G]) for i in range(2)]
        self.dif = [st.sb(f"dif{i}", [P, BANK]) for i in range(2)]
        self.prob = [st.sb(f"prob{i}", [P, BANK]) for i in range(2)]
        self.probT = [st.sb(f"probT{i}", [P, BANK]) for i in range(2)]
        self.scores_ready = st.sem("scores_ready")
        self.max_done = st.sem("max_done")
        self.dif_done = st.sem("dif_done")
        self.exp_done = st.sem("exp_done")
        self.transposed = st.sem("transposed")
        self.probT_done = st.sem("probT_done")
        self.values_done = st.sem("values_done")

    def credit(self, eng, *sems):
        for s in sems:
            eng.sem_inc(s, self.RING)

    def all_heads(self, ap):
        return ap.rearrange("p (h m) -> p h m", h=G)

    def slot(self, b, sb, g, n, work, *args):
        off, k = ago(g, n, self.groups)
        if Pipeline.there(sb, off):
            work(b, off, k, *args)

    def pe_scores(self, b, off, g, pe, queries, keys):
        u = (b + off) * self.groups + g
        pe.wait_ge(self.dif_done, u + 1)
        self.nc.tensor.matmul(self.psS[g % 2][:, :], queries(b, off, g), keys(b, off, g), start=True,
                              stop=True).then_inc(self.scores_ready, 1)

    def dve_shift(self, b, off, g, dve):
        u, i = (b + off) * self.groups + g, g % 2
        dve.wait_ge(self.scores_ready, u + 1)
        self.nc.vector.tensor_reduce(self.mx[i][:, :], self.all_heads(self.psS[i][:, :]), AX,
                                     ALU.max).then_inc(self.max_done, 1)
        dve.wait_ge(self.exp_done, u + 1)
        dve.wait_ge(self.max_done, u + 1)
        self.nc.vector.tensor_tensor(self.all_heads(self.dif[i][:, :]), self.all_heads(self.psS[i][:, :]),
                                     along(self.mx[i][:, :], S),
                                     ALU.subtract).then_inc(self.dif_done, 1)

    def act_exp(self, b, off, g, act):
        u, i = (b + off) * self.groups + g, g % 2
        act.wait_ge(self.dif_done, u + 1 + self.RING)
        act.wait_ge(self.transposed, u + 1)
        self.nc.scalar.activation(self.prob[i][:, :], self.dif[i][:, :], ACT.Exp,
                                  scale=self.scale).then_inc(self.exp_done, 1)

    def pe_transpose(self, b, off, g, pe):
        u, i = (b + off) * self.groups + g, g % 2
        pe.wait_ge(self.exp_done, u + 1 + self.RING)
        pe.wait_ge(self.probT_done, u + self.RING)
        for j in range(G):
            last = self.nc.tensor.transpose(self.psT[:, j * S:(j + 1) * S],
                                            self.prob[i][:, j * S:(j + 1) * S], self.g["ident"][:, :])
        last.then_inc(self.transposed, 1)

    def act_store(self, b, off, g, act):
        u, i = (b + off) * self.groups + g, g % 2
        act.wait_ge(self.transposed, u + 1 + self.RING)
        act.wait_ge(self.values_done, u + 1)
        self.nc.scalar.copy(self.probT[i][:, :], self.psT[:, :]).then_inc(self.probT_done, 1)

    def pe_values(self, b, off, g, pe, product):
        u, i = (b + off) * self.groups + g, g % 2
        pe.wait_ge(self.probT_done, u + 1 + self.RING)
        for j in range(G):
            last = product(self.probT[i][:, j * S:(j + 1) * S], b, off, g, j)
        last.then_inc(self.values_done, 1)

    def pe_slot(self, pe, b, sb, g, queries, keys, product):
        self.slot(b, sb, g, -1, self.pe_scores, pe, queries, keys)
        self.slot(b, sb, g, 1, self.pe_transpose, pe)
        self.slot(b, sb, g, 2, self.pe_values, pe, product)

    def act_slot(self, act, b, sb, g):
        self.slot(b, sb, g, 1, self.act_store, act)
        self.slot(b, sb, g, 0, self.act_exp, act)

    def dve_slot(self, dve, b, sb, g):
        self.slot(b, sb, g, 0, self.dve_shift, dve)


def load_stage(nc, glob, dram):
    st = Stage(nc, "load")
    with st.ctx:
        ctx = st.sb("ctx", [P, B, D])
        psC = [st.ps(f"ps_ctx{i}") for i in range(2)]
        loaded, ident_in, x_in = st.sem("ctx_in"), st.sem("ident_in"), st.sem("x_in")
        transposed = st.sem("ctx_transposed")
        stored, ready = st.sem("ctx_stored"), st.sem("const_ready")
        with nc.Block() as block:
            @block.sync
            def _(sp):
                sp.dma_start(ctx[:, :, :], dram["ctx_1024"].rearrange("b p d -> p b d")).then_inc(loaded, 16)
                sp.dma_start(glob["x"][:, :, :], dram["x"].rearrange("b p d -> p b d")).then_inc(x_in, 16)
                sp.wait_ge(x_in, 16)

            @block.gpsimd
            def _(pool):
                nc.gpsimd.memset(glob["mhalf"][:, :], -0.5).then_inc(ready, 1)
                pool.dma_start(glob["ident"][:, :], dram["c_ident"]).then_inc(ident_in, 16)
                pool.wait_ge(ready, 1)

            @block.tensor
            def _(pe):
                pe.wait_ge(ident_in, 16)
                pe.wait_ge(loaded, 16)
                for b in range(B):
                    nc.tensor.transpose(psC[b // 4][:, b % 4 * S:(b % 4 + 1) * S], ctx[:, b, :],
                                        glob["ident"][:, :]).then_inc(transposed, 1)

            @block.scalar
            def _(act):
                for i in range(2):
                    act.wait_ge(transposed, 4 * i + 4)
                    nc.scalar.copy(glob["ctxT"][:, 4 * i:4 * i + 4, :], psC[i][:, :]).then_inc(stored, 1)
                act.wait_ge(stored, 2)


def taylor_stage(nc, glob, dram):
    st = Stage(nc, "tay")
    with st.ctx:
        ln = LayerNorm(nc, st, glob)
        there = Pipeline.there
        x = glob["x"]
        NG = H // G
        CH = H * HD_A // P
        HPC = H // CH
        RING = 2
        wq, wk = st.sb("wq", [P, CH * P]), st.sb("wk", [P, CH * P])
        wv = st.sb("wv", [P, H * VD_A])
        wo = st.sb("wo", [P, H * VD_A // P, D])
        mask = st.sb("mask", [P, S])
        own_rows = st.sb("own_rows", [P, HPC])
        VW = VD_A + 1
        v = [st.sb(f"v{i}", [P, H * VW + WIN]) for i in range(2)]
        v3 = [a[:, 0:H * VW].rearrange("p (h e) -> p h e", e=VW) for a in v]
        qT = st.sb("qT", [P, CH * S])
        kT = [st.sb(f"kT{i}", [P, CH * S]) for i in range(2)]
        qz = [st.sb(f"q_own{i}", [P, H, S]) for i in range(2)]
        sq = [st.sb(f"square{i}", [P, BANK]) for i in range(2)]
        at = [st.sb(f"weights{i}", [P, BANK]) for i in range(2)]
        rz = st.sb("rz", [P, 2, G])
        yn = [st.sb(f"y{i}", [P, H * VD_A]) for i in range(2)]
        yT = st.sb("yT", [P, H * VD_A])
        psQ = st.ps("ps_proj")
        psV = [st.ps(f"ps_v{i}") for i in range(2)]
        psS = [st.ps(f"ps_scores{i}") for i in range(2)]
        psO = [st.ps(f"ps_out{i}") for i in range(2)]
        psY = ln.psX
        w_in, ones_ready, tables_in = st.sem("w_in"), st.sem("ones_ready"), st.sem("tables_in")
        qk_proj, v_proj = st.sem("qk_proj"), st.sem("v_proj")
        q_stored, k_stored, qz_ready = st.sem("q_stored"), st.sem("k_stored"), st.sem("qz_ready")
        v0_stored, v1_stored = st.sem("v0_stored"), st.sem("v1_stored")
        scores_ready, squared, masked = st.sem("scores_ready"), st.sem("squared"), st.sem("masked")
        out_ready, z_ready, rz_ready = st.sem("out_ready"), st.sem("z_ready"), st.sem("rz_ready")
        y_ready, yT_ready = st.sem("y_ready"), st.sem("yT_ready")
        yT0_stored, yT1_stored = st.sem("yT0_stored"), st.sem("yT1_stored")
        o_ready, added = st.sem("o_ready"), st.sem("added")

        def slot(b, sb, g, n, work, *args):
            off, k = ago(g, n, NG)
            if there(sb, off):
                work(b, off, k, *args)

        with nc.Block() as block:
            @block.sync
            def _(sp):
                sp.dma_start(wq[:, :], dram["L0_attn_Wq"]).then_inc(w_in, 16)
                sp.dma_start(wk[:, :], dram["L0_attn_Wk"]).then_inc(w_in, 16)
                sp.dma_start(wv[:, :], dram["L0_attn_Wv"]).then_inc(w_in, 16)
                sp.dma_start(wo[:, :, :], dram["L0_attn_Wo"].rearrange("(c p) n -> p c n", p=P)).then_inc(w_in, 16)
                sp.dma_start(mask[:, :], dram["c_causalT"]).then_inc(tables_in, 16)
                sp.dma_start(own_rows[:, :], dram["c_own_rows16"]).then_inc(tables_in, 16)

            @block.gpsimd
            def _(pool):
                for i in range(2):
                    nc.gpsimd.memset(v[i][:, :], 1.0).then_inc(ones_ready, 1)
                ln.pool_rstd(pool)
                pool.wait_ge(tables_in, 32)

                def slots(b, p, sb):
                    if there(sb, 1):
                        pool.wait_ge(q_stored, b + 2)
                        if there(sb, -1):
                            pool.wait_ge(scores_ready, b * NG)
                        for c in range(CH):
                            last = nc.gpsimd.tensor_tensor(
                                qz[1 - p][:, c * HPC:(c + 1) * HPC, :], over(qT[:, c * S:(c + 1) * S], HPC),
                                along(own_rows[:, :], S), ALU.mult)
                        last.then_inc(qz_ready, 1)

                Pipeline.run(pool, slots)

            @block.tensor
            def _(pe):
                pe.sem_inc(out_ready, RING)
                pe.wait_ge(w_in, 64)
                pe.wait_ge(ones_ready, 2)

                def slots(b, p, sb):
                    def scores(b, off, g):
                        u = (b + off) * NG + g
                        if g == 0:
                            pe.wait_ge(qz_ready, b + off + 1)
                            pe.wait_ge(k_stored, b + off + 1)
                        pe.wait_ge(squared, u + 1)
                        i, c = (p + off) % 2, g * G // HPC
                        nc.tensor.matmul(psS[g % 2][:, :], kT[i][:, c * S:(c + 1) * S],
                                         qz[i][:, g * G:(g + 1) * G, :], start=True, stop=True).then_inc(
                            scores_ready, 1)

                    def values(b, off, g):
                        u = (b + off) * NG + g
                        if g == 0:
                            pe.wait_ge(v0_stored, b + off + 1)
                            pe.wait_ge(v1_stored, b + off + 1)
                        pe.wait_ge(masked, u + 1 + RING)
                        pe.wait_ge(y_ready, u + 1)
                        for j in range(G):
                            c = (g * G + j) * VW
                            last = nc.tensor.matmul(psO[g % 2][:, j * S:j * S + WIN],
                                                    at[g % 2][:, j * S:(j + 1) * S],
                                                    v[(p + off) % 2][:, c:c + WIN], start=True, stop=True)
                        last.then_inc(out_ready, 1)

                    for g in range(NG):
                        slot(b, sb, g, 1, values)
                        slot(b, sb, g, -1, scores)
                        if g == 0 and there(sb, 1):
                            if there(sb, 0):
                                pe.wait_ge(v0_stored, b + 1)
                                pe.wait_ge(v1_stored, b + 1)
                            for i in range(2):
                                nc.tensor.matmul(psV[i][:, :], ln.xT[:, :], wv[:, i * BANK:(i + 1) * BANK],
                                                 start=True, stop=True).then_inc(v_proj, 1)
                        if g == 1 and there(sb, -1):
                            pe.wait_ge(y_ready, b * NG + RING)
                            if there(sb, 1):
                                pe.wait_ge(v0_stored, b + 2)
                                pe.wait_ge(v1_stored, b + 2)
                            for c in range(8):
                                last = nc.tensor.transpose(psV[c // 4][:, c % 4 * S:(c % 4 + 1) * S],
                                                           yn[1 - p][:, c * P:(c + 1) * P], glob["ident"][:, :])
                                if c % 4 == 3:
                                    last.then_inc(yT_ready, 1)
                        if g == 1 and there(sb, 2):
                            if sb >= 0:
                                pe.wait_ge(added, b - 1 + RING)
                            ln.pe_transpose(pe, b + 2)
                        if g == 2 and there(sb, 2):
                            pe.wait_ge(ln.xT_ready, b + 3)
                            if there(sb, 1):
                                pe.wait_ge(q_stored, b + 2)
                                pe.wait_ge(k_stored, b + 2)
                            for i, w in enumerate((wq, wk)):
                                for c in range(CH):
                                    o = (i * CH + c) * S
                                    last = nc.tensor.matmul(psQ[:, o:o + S], w[:, c * P:(c + 1) * P], ln.xT[:, :],
                                                            start=True, stop=True)
                            last.then_inc(qk_proj, 1)
                        if g == 2 and there(sb, -1):
                            pe.wait_ge(yT0_stored, b)
                            pe.wait_ge(yT1_stored, b)
                            for c in range(8):
                                last = nc.tensor.matmul(psY[:, 0:D], yT[:, c * P:(c + 1) * P], wo[:, c, :],
                                                        start=(c == 0), stop=(c == 7))
                            last.then_inc(o_ready, 1)

                Pipeline.run(pe, slots)

            @block.scalar
            def _(act):
                act.sem_inc(squared, RING)
                act.wait_ge(ones_ready, 2)

                def square(b, off, g):
                    u = (b + off) * NG + g
                    act.wait_ge(scores_ready, u + 1)
                    act.wait_ge(masked, u + 1)
                    nc.scalar.activation(sq[g % 2][:, :], psS[g % 2][:, :], ACT.Square, bias=1.0,
                                         scale=0.25).then_inc(squared, 1)

                def slots(b, p, sb):
                    for g in range(NG):
                        slot(b, sb, g, 0, square)
                        if g == 0 and there(sb, 1):
                            act.wait_ge(v_proj, 2 * b + 3)
                            nc.scalar.copy(v3[1 - p][:, 0:8, 0:VD_A],
                                           psV[0][:, :].rearrange("p (h e) -> p h e", h=8)).then_inc(v0_stored, 1)
                        if g == 1 and there(sb, 2):
                            if there(sb, 1):
                                act.wait_ge(v_proj, 2 * b + 4)
                            ln.act_store(act, b + 2)
                        if g == 1 and there(sb, -1):
                            act.wait_ge(yT_ready, 2 * b - 1)
                            nc.scalar.copy(yT[:, 0:BANK], psV[0][:, :]).then_inc(yT0_stored, 1)
                        if g == 2 and there(sb, 2):
                            act.wait_ge(qk_proj, b + 3)
                            if there(sb, 1):
                                act.wait_ge(qz_ready, b + 2)
                            nc.scalar.copy(qT[:, :], psQ[:, 0:CH * S]).then_inc(q_stored, 1)
                            nc.scalar.copy(kT[p][:, :], psQ[:, CH * S:]).then_inc(k_stored, 1)

                Pipeline.run(act, slots)

            @block.vector
            def _(dve):
                for s in (masked, y_ready, added):
                    dve.sem_inc(s, RING)
                ln.dve_stats(dve)
                dve.wait_ge(tables_in, 32)
                dve.wait_ge(ones_ready, 2)

                def weights(b, off, g):
                    u = (b + off) * NG + g
                    dve.wait_ge(squared, u + 1 + RING)
                    dve.wait_ge(out_ready, u + 1)
                    nc.vector.scalar_tensor_tensor(
                        at[g % 2][:, :].rearrange("p (h m) -> p h m", h=G),
                        sq[g % 2][:, :].rearrange("p (h m) -> p h m", h=G), 1.0,
                        over(mask[:, :], G), ALU.add, ALU.mult).then_inc(masked, 1)

                def normalise(b, off, g, p):
                    u = (b + off) * NG + g
                    o3 = psO[g % 2][:, :].rearrange("p (h e) -> p h e", h=G)
                    dve.wait_ge(out_ready, u + 1 + RING)
                    nc.vector.tensor_scalar(rz[:, 0, :], o3[:, :, VD_A], 2e-12, None, ALU.add).then_inc(z_ready, 1)
                    dve.wait_ge(z_ready, u + 1)
                    nc.vector.reciprocal(rz[:, 1, :], rz[:, 0, :]).then_inc(rz_ready, 1)
                    dve.wait_ge(rz_ready, u + 1)
                    nc.vector.tensor_tensor(
                        yn[(p + off) % 2][:, g * G * VD_A:(g + 1) * G * VD_A].rearrange("p (h e) -> p h e", h=G),
                        o3[:, :, 0:VD_A], along(rz[:, 1, :], VD_A), ALU.mult).then_inc(y_ready, 1)

                def slots(b, p, sb):
                    for g in range(NG):
                        slot(b, sb, g, 0, weights)
                        if g == 0 and there(sb, 2):
                            if there(sb, 1):
                                dve.wait_ge(ln.psx_ready, b + 2)
                            ln.dve_normalise(dve, b + 2)
                        slot(b, sb, g, 1, normalise, p)
                        if g == 0 and there(sb, 1):
                            dve.wait_ge(v_proj, 2 * b + 4)
                            nc.vector.tensor_copy(v3[1 - p][:, 8:16, 0:VD_A],
                                                  psV[1][:, :].rearrange("p (h e) -> p h e", h=8)).then_inc(
                                v1_stored, 1)
                        if g == 1 and there(sb, -1):
                            dve.wait_ge(yT_ready, 2 * b)
                            nc.vector.tensor_copy(yT[:, BANK:], psV[1][:, :]).then_inc(yT1_stored, 1)
                        if g == 3 and there(sb, -1):
                            dve.wait_ge(o_ready, b)
                            xb = x[:, bass.ds(b - 1, 1), :]
                            nc.vector.tensor_tensor(xb, xb, psY[:, 0:D], ALU.add).then_inc(added, 1)

                Pipeline.run(dve, slots)
                dve.wait_ge(added, B + RING)


def diff_stage(nc, glob, dram):
    st = Stage(nc, "dif")
    with st.ctx:
        NM = 2
        NG = NM * H // G
        VW = HD_S + 1
        VB = H * VW
        ln = LayerNorm(nc, st, glob)
        at = SoftmaxHeads(nc, st, glob, NG, float(HD_S) ** -0.5)
        there = Pipeline.there
        x, ctxT = glob["x"], glob["ctxT"]
        w = [st.sb(n, [P, D]) for n in ("wq1", "wq2", "wk1", "wk2")]
        wv, wo, gain = st.sb("wv", [P, D]), st.sb("wo", [P, D]), st.sb("gain", [P, 1])
        own_rows = st.sb("own_rows", [P, H])
        v = st.sb("v", [P, B * VB + WIN])
        v4 = v[:, 0:B * VB].rearrange("p (b h e) -> p b h e", b=B, e=VW)
        qT = [st.sb(f"qT{i}", [P, NM, S]) for i in range(2)]
        kT = st.sb("kT", [P, NM, S])
        kz = [st.sb(f"k_own{i}", [P, NM, H, S]) for i in range(2)]
        rz = st.sb("rz", [P, NM, H])
        rzg = st.sb("rz_gain", [P, H])
        m1, m2, o = (st.sb(n, [P, H, HD_S]) for n in ("map1", "map2", "o"))
        cen, sqr, oN = (st.sb(n, [P, H, HD_S]) for n in ("centred", "squares", "o_norm"))
        red = st.sb("head_sums", [P, 4, H])
        rs = st.sb("head_rstd", [P, H])
        oT = st.sb("oT", [P, S])
        psP, psO, psY = st.ps("ps_proj"), [st.ps(f"ps_out{i}") for i in range(2)], st.ps("ps_y")
        psF = psY[:, 256:256 + S]
        w_in, const_in, ones_ready = st.sem("w_in"), st.sem("const_in"), st.sem("ones_ready")
        v_proj, v_stored = st.sem("v_proj"), st.sem("v_stored")
        qk_proj, q_stored, k_stored = st.sem("qk_proj"), st.sem("q_stored"), st.sem("k_stored")
        kz_ready = st.sem("kz_ready")
        rz_ready, rzg_ready = st.sem("rz_ready"), st.sem("rzg_ready")
        maps_ready, o_ready, sum_ready = st.sem("maps_ready"), st.sem("o_ready"), st.sem("sum_ready")
        mean_ready, cen_ready = st.sem("mean_ready"), st.sem("cen_ready")
        sqr_ready, var_ready, ve_ready = st.sem("sqr_ready"), st.sem("var_ready"), st.sem("ve_ready")
        rs_ready, oN_ready, oT_ready = st.sem("rs_ready"), st.sem("oN_ready"), st.sem("oT_ready")
        oT_stored, y_ready, added = st.sem("oT_stored"), st.sem("y_ready"), st.sem("added")

        with nc.Block() as block:
            @block.sync
            def _(sp):
                for i, n in enumerate(("wq1", "wq2", "wk1", "wk2")):
                    sp.dma_start(w[i][:, :], dram["L0_xattn_" + n]).then_inc(w_in, 16)
                sp.dma_start(wv[:, :], dram["L0_xattn_wv"]).then_inc(w_in, 16)
                sp.dma_start(wo[:, :], dram["L0_xattn_wo"]).then_inc(w_in, 16)
                sp.dma_start(own_rows[:, :], dram["c_own_rows8"]).then_inc(const_in, 16)
                sp.dma_start(gain[:, :], dram["L0_xattn_gain"].unsqueeze(0).to_broadcast([P, 1])).then_inc(const_in, 16)

            @block.gpsimd
            def _(pool):
                nc.gpsimd.memset(v[:, :], 1.0).then_inc(ones_ready, 1)
                ln.pool_rstd(pool)
                pool.wait_ge(const_in, 32)

                def own_keys(b, sb, p, m):
                    pool.wait_ge(k_stored, b + 2)
                    if there(sb, -1):
                        pool.wait_ge(at.scores_ready, b * NG)
                    nc.gpsimd.tensor_tensor(kz[p][:, m, :, :], over(kT[:, m, :], H), along(own_rows[:, :], S),
                                            ALU.mult).then_inc(kz_ready, 1)

                def slots(b, p, sb):
                    if there(sb, 1):
                        own_keys(b, sb, 1 - p, 0)
                    if there(sb, -1):
                        pool.wait_ge(ve_ready, b)
                        nc.gpsimd.tensor_tensor(rs[:, :], red[:, 3, :], glob["mhalf"][:, 0:H],
                                                ALU.pow).then_inc(rs_ready, 1)
                    if there(sb, 1):
                        own_keys(b, sb, 1 - p, 1)

                Pipeline.run(pool, slots)

            @block.tensor
            def _(pe):
                at.credit(pe, at.transposed, at.values_done)
                pe.wait_ge(w_in, 96)
                for b in range(B):
                    nc.tensor.matmul(psO[b // 4][:, b % 4 * D:(b % 4 + 1) * D], ctxT[:, b, :], wv[:, :],
                                     start=True, stop=True).then_inc(v_proj, 1)
                pe.wait_ge(v_stored, 2)

                def slots(b, p, sb):
                    def queries(b, off, g):
                        return qT[(p + off) % 2][:, g // G, :]

                    def keys(b, off, g):
                        if g % G == 0:
                            pe.wait_ge(kz_ready, NM * (b + off) + g // G + 1)
                        if g == 0:
                            pe.wait_ge(q_stored, b + off + 1)
                        h = g % G * G
                        return kz[(p + off) % 2][:, g // G, h:h + G, :]

                    def product(probT, b, off, g, j):
                        h = g % G * G + j
                        c = g // G * 256 + h * VW
                        return nc.tensor.matmul(psO[(p + off) % 2][:, c:c + WIN], probT,
                                                v[:, bass.ds((b + off) * VB + h * VW, WIN)], start=True, stop=True)

                    for g in range(NG):
                        at.pe_slot(pe, b, sb, g, queries, keys, product)
                        if g == 1 and there(sb, 2):
                            ln.pe_transpose(pe, b + 2)
                        if g == 3 and there(sb, 2):
                            pe.wait_ge(ln.xT_ready, b + 3)
                            if there(sb, 1):
                                pe.wait_ge(q_stored, b + 2)
                                pe.wait_ge(k_stored, b + 2)
                            for i in range(4):
                                rhs = ln.xT[:, :] if i < 2 else ctxT[:, bass.ds(b + 2, 1), :]
                                last = nc.tensor.matmul(psP[:, i * S:(i + 1) * S], w[i][:, :], rhs,
                                                        start=True, stop=True)
                            last.then_inc(qk_proj, 1)
                        if g == 6 and there(sb, -1):
                            pe.wait_ge(oN_ready, b)
                            nc.tensor.transpose(psF, oN[:, :, :].rearrange("p h e -> p (h e)"),
                                                glob["ident"][:, :]).then_inc(oT_ready, 1)
                        if g == 7 and there(sb, -1):
                            pe.wait_ge(oT_stored, b)
                            nc.tensor.matmul(psY[:, 0:D], oT[:, :], wo[:, :], start=True,
                                             stop=True).then_inc(y_ready, 1)

                Pipeline.run(pe, slots)

            @block.scalar
            def _(act):
                at.credit(act, at.exp_done, at.probT_done)

                def slots(b, p, sb):
                    for g in range(NG):
                        at.act_slot(act, b, sb, g)
                        if g == 1 and there(sb, 2):
                            ln.act_store(act, b + 2)
                        if g == 6 and there(sb, -1):
                            act.wait_ge(oT_ready, b)
                            nc.scalar.copy(oT[:, :], psF).then_inc(oT_stored, 1)
                        if g == 7 and there(sb, 2):
                            act.wait_ge(qk_proj, b + 3)
                            if there(sb, 0):
                                act.wait_ge(at.scores_ready, (b + 1) * NG)
                            nc.scalar.copy(qT[p][:, :, :], psP[:, 0:NM * S]).then_inc(q_stored, 1)
                            if there(sb, 1):
                                act.wait_ge(kz_ready, NM * (b + 2))
                            nc.scalar.copy(kT[:, :, :], psP[:, NM * S:]).then_inc(k_stored, 1)

                Pipeline.run(act, slots)

            @block.vector
            def _(dve):
                at.credit(dve, at.dif_done)
                ln.dve_stats(dve)
                dve.wait_ge(const_in, 32)
                dve.wait_ge(ones_ready, 1)
                for i in range(2):
                    dve.wait_ge(v_proj, 4 * i + 4)
                    for k in range(4):
                        last = nc.vector.tensor_copy(
                            v4[:, 4 * i + k, :, 0:HD_S],
                            psO[i][:, k * D:(k + 1) * D].rearrange("p (h e) -> p h e", e=HD_S))
                    last.then_inc(v_stored, 1)

                def combine(b, p):
                    o4 = psO[p][:, :].rearrange("p (m c) -> p m c", m=NM)[:, :, 0:VB].rearrange(
                        "p m (h e) -> p m h e", e=VW)
                    dve.wait_ge(at.values_done, NG * b + at.RING)
                    nc.vector.reciprocal(rz[:, :, :], o4[:, :, :, HD_S]).then_inc(rz_ready, 1)
                    dve.wait_ge(rz_ready, b)
                    nc.vector.tensor_scalar(rzg[:, :], rz[:, 1, :], gain[:, 0:1], None,
                                            ALU.mult).then_inc(rzg_ready, 1)
                    nc.vector.tensor_tensor(m1[:, :, :], o4[:, 0, :, 0:HD_S], along(rz[:, 0, :], HD_S), ALU.mult)
                    dve.wait_ge(rzg_ready, b)
                    nc.vector.tensor_tensor(m2[:, :, :], o4[:, 1, :, 0:HD_S], along(rzg[:, :], HD_S),
                                            ALU.mult).then_inc(maps_ready, 1)

                def variances(b):
                    dve.wait_ge(maps_ready, b)
                    nc.vector.tensor_tensor(o[:, :, :], m1[:, :, :], m2[:, :, :], ALU.subtract).then_inc(o_ready, 1)
                    dve.wait_ge(o_ready, b)
                    nc.vector.tensor_reduce(red[:, 0, :], o[:, :, :], AX, ALU.add).then_inc(sum_ready, 1)
                    dve.wait_ge(sum_ready, b)
                    nc.vector.tensor_scalar(red[:, 1, :], red[:, 0, :], 1.0 / HD_S, None,
                                            ALU.mult).then_inc(mean_ready, 1)
                    dve.wait_ge(mean_ready, b)
                    nc.vector.tensor_tensor(cen[:, :, :], o[:, :, :], along(red[:, 1, :], HD_S),
                                            ALU.subtract).then_inc(cen_ready, 1)
                    dve.wait_ge(cen_ready, b)
                    nc.vector.tensor_tensor(sqr[:, :, :], cen[:, :, :], cen[:, :, :], ALU.mult).then_inc(sqr_ready, 1)
                    dve.wait_ge(sqr_ready, b)
                    nc.vector.tensor_reduce(red[:, 2, :], sqr[:, :, :], AX, ALU.add).then_inc(var_ready, 1)
                    dve.wait_ge(var_ready, b)
                    nc.vector.tensor_scalar(red[:, 3, :], red[:, 2, :], 1.0 / HD_S, LN_EPS, ALU.mult,
                                            ALU.add).then_inc(ve_ready, 1)

                def slots(b, p, sb):
                    for g in range(NG):
                        at.dve_slot(dve, b, sb, g)
                        if g == 0 and there(sb, 2):
                            if there(sb, 1):
                                dve.wait_ge(ln.psx_ready, b + 2)
                            ln.dve_normalise(dve, b + 2)
                        if g == 2 and there(sb, -1):
                            combine(b, 1 - p)
                        if g == 3 and there(sb, -1):
                            variances(b)
                        if g == 5 and there(sb, -1):
                            dve.wait_ge(rs_ready, b)
                            nc.vector.tensor_tensor(oN[:, :, :], cen[:, :, :], along(rs[:, :], HD_S),
                                                    ALU.mult).then_inc(oN_ready, 1)
                        if g == 7 and there(sb, -1):
                            dve.wait_ge(y_ready, b)
                            xb = x[:, bass.ds(b - 1, 1), :]
                            nc.vector.tensor_tensor(xb, xb, psY[:, 0:D], ALU.add).then_inc(added, 1)

                Pipeline.run(dve, slots)
                dve.wait_ge(added, B)


def expert_stage(nc, glob, dram):
    st = Stage(nc, "moe")
    with st.ctx:
        NT = MOE_T // P
        FC = FF // P
        ln = LayerNorm(nc, st, glob, NT)
        x = glob["x"]
        xT = st.sb("x_hat_T4", [P, MOE_T])
        xh = st.sb("x_hat4", [P, NT, D])
        w1 = [st.sb(f"w1_{i}", [P, FF]) for i in range(2)]
        w2 = [st.sb(f"w2_{i}", [P, FC, D]) for i in range(2)]
        hT = [st.sb(f"hT{i}", [P, FC, MOE_T]) for i in range(2)]
        idx = st.sb("idx", [P, NT, TOPK], I32)
        wts = st.sb("wts", [P, NT, TOPK])
        eid = st.sb("expert_ids", [P, E_EXP])
        hit = st.sb("hit", [P, NT, E_EXP, TOPK])
        share = st.sb("share", [P, NT, E_EXP, TOPK])
        gate = st.sb("gate", [P, NT, E_EXP])
        bias = st.sb("bias", [P, D])
        psH = [st.ps(f"ps_h{i}") for i in range(2)]
        psY = [st.ps(f"ps_y{i}") for i in range(2)]
        psX = st.ps("ps_x4")
        w1_in = [st.sem(f"w1_{i}_in") for i in range(2)]
        w2_in = [st.sem(f"w2_{i}_in") for i in range(2)]
        route_in, id_in, bias_in = st.sem("route_in"), st.sem("id_in"), st.sem("bias_in")
        hit_ready, share_ready, gate_ready = st.sem("hit_ready"), st.sem("share_ready"), st.sem("gate_ready")
        xh_ready, x_transposed, xT_ready = st.sem("xh4_ready"), st.sem("x_transposed"), st.sem("xT4_ready")
        h_ready, h_stored, y_ready, y_added = (st.sem("h_ready"), st.sem("h_stored"), st.sem("y_ready"),
                                               st.sem("y_added"))
        biased = st.sem("biased")

        with nc.Block() as block:
            @block.sync
            def _(sp):
                idx_v = dram["L0_ffn_expert_indices"].rearrange("(j p) k -> p j k", p=P)
                wts_v = dram["L0_ffn_expert_weights"].rearrange("(j p) k -> p j k", p=P)

                def load_w1(e, i):
                    sp.dma_start(w1[i][:, :], dram["L0_ffn_w1"][bass.ds(e, 1), :, :].rearrange(
                        "a p n -> p (a n)")).then_inc(w1_in[i], 16)

                def load_w2(e, i):
                    sp.dma_start(w2[i][:, :, :], dram["L0_ffn_w2"][bass.ds(e, 1), :, :].rearrange(
                        "a (c p) n -> p (a c) n", p=P)).then_inc(w2_in[i], 16)

                sp.dma_start(idx[:, :, :], idx_v).then_inc(route_in, 16)
                sp.dma_start(wts[:, :, :], wts_v).then_inc(route_in, 16)
                sp.dma_start(eid[:, :], dram["c_experts"].unsqueeze(0).to_broadcast([P, E_EXP])).then_inc(id_in, 16)
                sp.dma_start(bias[:, :], dram["L0_ffn_bias"].unsqueeze(0).to_broadcast([P, D])).then_inc(bias_in, 16)
                for i in range(2):
                    load_w1(i, i)
                    load_w2(i, i)
                with sp.Fori(1, E_EXP // 2) as n:
                    for i in range(2):
                        sp.wait_ge(h_ready, FC * (2 * n + i - 1))
                        load_w1(2 * n + i, i)
                        sp.wait_ge(y_ready, 2 * n + i - 1)
                        load_w2(2 * n + i, i)

            @block.gpsimd
            def _(pool):
                ln.pool_rstd(pool)

            @block.tensor
            def _(pe):
                pe.wait_ge(xh_ready, NT)
                for j in range(NT):
                    last = nc.tensor.transpose(psX[:, j * S:(j + 1) * S], xh[:, j, :], glob["ident"][:, :])
                last.then_inc(x_transposed, 1)
                pe.wait_ge(xT_ready, 1)

                def up(e, i, n):
                    pe.wait_ge(w1_in[i], (n + 1) * 16)
                    for c in range(FC):
                        pe.wait_ge(h_stored, FC * e + c + 1)
                        nc.tensor.matmul(psH[c % 2][:, :], w1[i][:, c * P:(c + 1) * P], xT[:, :],
                                         start=True, stop=True).then_inc(h_ready, 1)

                def down(e, i, n):
                    pe.wait_ge(w2_in[i], (n + 1) * 16)
                    pe.wait_ge(h_stored, FC * e + FC + 2)
                    pe.wait_ge(y_added, e + 1)
                    for j in range(NT):
                        for c in range(FC):
                            last = nc.tensor.matmul(psY[i][:, j * D:(j + 1) * D], hT[i][:, c, j * P:(j + 1) * P],
                                                    w2[i][:, c, :], start=(c == 0), stop=(c == FC - 1))
                    last.then_inc(y_ready, 1)

                up(0, 0, 0)
                with pe.Fori(0, E_EXP // 2 - 1) as n:
                    up(2 * n + 1, 1, n)
                    down(2 * n, 0, n)
                    up(2 * n + 2, 0, n + 1)
                    down(2 * n + 1, 1, n)
                n = E_EXP // 2 - 1
                up(2 * n + 1, 1, n)
                down(2 * n, 0, n)
                down(2 * n + 1, 1, n)

            @block.scalar
            def _(act):
                act.sem_inc(h_stored, 2)
                act.wait_ge(x_transposed, 1)
                nc.scalar.copy(xT[:, :], psX[:, :]).then_inc(xT_ready, 1)
                with act.Fori(0, E_EXP // 2) as n:
                    for i in range(2):
                        e = 2 * n
                        act.wait_ge(y_added, e + i + 1)
                        for c in range(FC):
                            act.wait_ge(h_ready, FC * e + FC * i + c + 1)
                            nc.scalar.activation(hT[i][:, c, :], psH[c % 2][:, :], ACT.Gelu).then_inc(h_stored, 1)

            @block.vector
            def _(dve):
                dve.sem_inc(y_added, 2)
                ln.dve_stats(dve)
                dve.wait_ge(route_in, 32)
                dve.wait_ge(id_in, 16)
                for j in range(NT):
                    nc.vector.tensor_tensor(hit[:, j, :, :], over(idx[:, j, :], E_EXP), along(eid[:, :], TOPK),
                                            ALU.is_equal).then_inc(hit_ready, 1)
                for j in range(NT):
                    dve.wait_ge(hit_ready, j + 1)
                    nc.vector.tensor_tensor(share[:, j, :, :], hit[:, j, :, :], over(wts[:, j, :], E_EXP),
                                            ALU.mult).then_inc(share_ready, 1)
                dve.wait_ge(share_ready, NT)
                nc.vector.tensor_reduce(gate[:, :, :], share[:, :, :, :], AX, ALU.add).then_inc(gate_ready, 1)
                dve.wait_ge(ln.rstd_done, 1)
                for j in range(NT):
                    nc.vector.tensor_scalar(xh[:, j, :], x[:, j, :], ln.mv[:, j, 0:1], ln.rstd[:, j:j + 1],
                                            ALU.subtract, ALU.mult).then_inc(xh_ready, 1)
                dve.wait_ge(xh_ready, NT)
                dve.wait_ge(bias_in, 16)
                nc.vector.tensor_tensor(x[:, :, :], x[:, :, :], over(bias[:, :], B), ALU.add).then_inc(biased, 1)
                dve.wait_ge(biased, 1)
                dve.wait_ge(gate_ready, 1)
                with dve.Fori(0, E_EXP // 2) as n:
                    for i in range(2):
                        e = 2 * n
                        dve.wait_ge(y_ready, e + i + 1)
                        dve.wait_ge(y_added, e + i + 2)
                        for j in range(NT):
                            last = nc.vector.scalar_tensor_tensor(
                                x[:, j, :], psY[i][:, j * D:(j + 1) * D], gate[:, j, bass.ds(e + i, 1)],
                                x[:, j, :], ALU.mult, ALU.add)
                        last.then_inc(y_added, 1)
                dve.wait_ge(y_added, E_EXP + 2)


def rope_stage(nc, glob, dram):
    st = Stage(nc, "rope")
    with st.ctx:
        NG = H // G
        VW = HD_S + 1
        VB = H * VW
        HALF = HD_S // 2
        ln = LayerNorm(nc, st, glob)
        at = SoftmaxHeads(nc, st, glob, NG, float(HD_S) ** -0.5)
        there = Pipeline.there
        x = glob["x"]
        w, wo, bo = st.sb("w_qkv", [P, 3 * D]), st.sb("w_out", [P, D]), st.sb("b_out", [P, D])
        cos, sin = st.sb("cos", [P, HD_S]), st.sb("sin", [P, HD_S])
        own_rows = st.sb("own_rows", [P, H])
        v = st.sb("v", [P, B * VB + WIN])
        v4 = v[:, 0:B * VB].rearrange("p (b h e) -> p b h e", b=B, e=VW)
        rc, rsn, rot = (st.sb(n, [P, 2 * H, HD_S]) for n in ("rot_cos", "rot_sin", "rotated"))
        qT = [st.sb(f"qT{i}", [P, S]) for i in range(2)]
        kT = st.sb("kT", [P, S])
        kz = [st.sb(f"k_own{i}", [P, H, S]) for i in range(2)]
        rz, on, oT = st.sb("rz", [P, H]), st.sb("o", [P, H, HD_S]), st.sb("oT", [P, S])
        psP, psO, psY = st.ps("ps_proj"), [st.ps(f"ps_out{i}") for i in range(2)], st.ps("ps_y")
        psF, psX = psY[:, 256:256 + S], ln.psX
        w_in, tab_in, bo_in = st.sem("w_in"), st.sem("tab_in"), st.sem("bo_in")
        ones_ready = st.sem("ones_ready")
        proj, rc_ready, rs_ready = st.sem("proj"), st.sem("rc_ready"), st.sem("rs_ready")
        v_stored, rot_ready = st.sem("v_stored"), st.sem("rot_ready")
        qk_transposed, q_stored, k_stored = st.sem("qk_transposed"), st.sem("q_stored"), st.sem("k_stored")
        kz_ready = st.sem("kz_ready")
        rz_ready, on_ready, oT_ready = st.sem("rz_ready"), st.sem("o_ready"), st.sem("oT_ready")
        oT_stored, y_ready, yb_added, added = (st.sem("oT_stored"), st.sem("y_ready"), st.sem("bias_added"),
                                               st.sem("added"))

        with nc.Block() as block:
            @block.sync
            def _(sp):
                sp.dma_start(w[:, :], dram["L1_attn_w_qkv"]).then_inc(w_in, 16)
                sp.dma_start(wo[:, :], dram["L1_attn_w_out"]).then_inc(w_in, 16)
                sp.dma_start(cos[:, :], dram["c_rope8_cos"]).then_inc(tab_in, 16)
                sp.dma_start(sin[:, :], dram["c_rope8_sin"]).then_inc(tab_in, 16)
                sp.dma_start(own_rows[:, :], dram["c_own_rows8"]).then_inc(tab_in, 16)
                sp.dma_start(bo[:, :], dram["L1_attn_b_out"].unsqueeze(0).to_broadcast([P, D])).then_inc(bo_in, 16)

            @block.gpsimd
            def _(pool):
                nc.gpsimd.memset(v[:, :], 1.0).then_inc(ones_ready, 1)
                ln.pool_rstd(pool)
                pool.wait_ge(tab_in, 48)

                def slots(b, p, sb):
                    if there(sb, 1):
                        pool.wait_ge(k_stored, b + 2)
                        if there(sb, -1):
                            pool.wait_ge(at.scores_ready, b * NG)
                        nc.gpsimd.tensor_tensor(kz[1 - p][:, :, :], over(kT[:, :], H), along(own_rows[:, :], S),
                                                ALU.mult).then_inc(kz_ready, 1)

                Pipeline.run(pool, slots)

            @block.tensor
            def _(pe):
                at.credit(pe, at.transposed, at.values_done)
                pe.wait_ge(w_in, 32)

                def slots(b, p, sb):
                    def queries(b, off, g):
                        return qT[(p + off) % 2][:, :]

                    def keys(b, off, g):
                        if g == 0:
                            pe.wait_ge(kz_ready, b + off + 1)
                            pe.wait_ge(q_stored, b + off + 1)
                        return kz[(p + off) % 2][:, g * G:(g + 1) * G, :]

                    def product(probT, b, off, g, j):
                        if g == 0 and j == 0:
                            pe.wait_ge(v_stored, b + off + 1)
                        c = (g * G + j) * VW
                        return nc.tensor.matmul(psO[(p + off) % 2][:, c:c + WIN], probT,
                                                v[:, bass.ds((b + off) * VB + c, WIN)], start=True, stop=True)

                    for g in range(NG):
                        at.pe_slot(pe, b, sb, g, queries, keys, product)
                        if g == 1 and there(sb, 2):
                            if there(sb, 1):
                                pe.wait_ge(k_stored, b + 2)
                            ln.pe_transpose(pe, b + 2)
                        if g == 2 and there(sb, 2):
                            pe.wait_ge(ln.xT_ready, b + 3)
                            nc.tensor.matmul(psP[:, 0:3 * D], ln.xT[:, :], w[:, :], start=True,
                                             stop=True).then_inc(proj, 1)
                        if g == 3 and there(sb, -1):
                            pe.wait_ge(on_ready, b)
                            nc.tensor.transpose(psF, on[:, :, :].rearrange("p h e -> p (h e)"),
                                                glob["ident"][:, :]).then_inc(oT_ready, 1)
                        if g == 3 and there(sb, 2):
                            pe.wait_ge(rot_ready, b + 3)
                            for i in range(2):
                                last = nc.tensor.transpose(
                                    psX[:, i * S:(i + 1) * S],
                                    rot[:, i * H:(i + 1) * H, :].rearrange("p h e -> p (h e)"), glob["ident"][:, :])
                            last.then_inc(qk_transposed, 1)
                        if g == 3 and there(sb, -1):
                            pe.wait_ge(oT_stored, b)
                            nc.tensor.matmul(psY[:, 0:D], oT[:, :], wo[:, :], start=True,
                                             stop=True).then_inc(y_ready, 1)

                Pipeline.run(pe, slots)

            @block.scalar
            def _(act):
                at.credit(act, at.exp_done, at.probT_done)

                def slots(b, p, sb):
                    for g in range(NG):
                        at.act_slot(act, b, sb, g)
                        if g == 1 and there(sb, 2):
                            if there(sb, 1):
                                act.wait_ge(proj, b + 2)
                            ln.act_store(act, b + 2)
                        if g == 3 and there(sb, -1):
                            act.wait_ge(oT_ready, b)
                            nc.scalar.copy(oT[:, :], psF).then_inc(oT_stored, 1)
                        if g == 3 and there(sb, 2):
                            act.wait_ge(qk_transposed, b + 3)
                            nc.scalar.copy(qT[p][:, :], psX[:, 0:S]).then_inc(q_stored, 1)
                            if there(sb, 1):
                                act.wait_ge(kz_ready, b + 2)
                            nc.scalar.copy(kT[:, :], psX[:, S:2 * S]).then_inc(k_stored, 1)

                Pipeline.run(act, slots)

            @block.vector
            def _(dve):
                at.credit(dve, at.dif_done)
                ln.dve_stats(dve)
                dve.wait_ge(tab_in, 48)
                dve.wait_ge(bo_in, 16)
                dve.wait_ge(ones_ready, 1)

                def rotate(b, sb):
                    dve.wait_ge(proj, b + 1)
                    qk3 = psP[:, 0:2 * D].rearrange("p (h e) -> p h e", e=HD_S)
                    nc.vector.tensor_tensor(rc[:, :, :], qk3, over(cos[:, :], 2 * H), ALU.mult).then_inc(rc_ready, 1)
                    nc.vector.tensor_tensor(rsn[:, :, 0:HALF], qk3[:, :, HALF:], over(sin[:, 0:HALF], 2 * H), ALU.mult)
                    nc.vector.tensor_tensor(rsn[:, :, HALF:], qk3[:, :, 0:HALF], over(sin[:, HALF:], 2 * H),
                                            ALU.mult).then_inc(rs_ready, 1)
                    nc.vector.tensor_copy(v4[:, bass.ds(b, 1), :, 0:HD_S], psP[:, 2 * D:3 * D].rearrange(
                        "p (h e) -> p h e", e=HD_S)).then_inc(v_stored, 1)
                    if there(sb, -1):
                        dve.wait_ge(qk_transposed, b)
                    dve.wait_ge(rs_ready, b + 1)
                    nc.vector.tensor_tensor(rot[:, :, :], rc[:, :, :], rsn[:, :, :], ALU.add).then_inc(rot_ready, 1)

                def finish(b, p):
                    dve.wait_ge(at.values_done, NG * b + at.RING)
                    o3 = psO[p][:, 0:VB].rearrange("p (h e) -> p h e", e=VW)
                    nc.vector.reciprocal(rz[:, :], o3[:, :, HD_S]).then_inc(rz_ready, 1)
                    dve.wait_ge(rz_ready, b)
                    nc.vector.tensor_tensor(on[:, :, :], o3[:, :, 0:HD_S], along(rz[:, :], HD_S),
                                            ALU.mult).then_inc(on_ready, 1)

                def slots(b, p, sb):
                    for g in range(NG):
                        at.dve_slot(dve, b, sb, g)
                        if g == 0 and there(sb, 2):
                            if there(sb, 1):
                                dve.wait_ge(ln.psx_ready, b + 2)
                            ln.dve_normalise(dve, b + 2)
                        if g == 2 and there(sb, -1):
                            finish(b, 1 - p)
                        if g == 2 and there(sb, 2):
                            rotate(b + 2, sb + 2)
                        if g == 3 and there(sb, -1):
                            xb = x[:, bass.ds(b - 1, 1), :]
                            nc.vector.tensor_tensor(xb, xb, over(bo[:, :], 1), ALU.add).then_inc(yb_added, 1)
                            dve.wait_ge(y_ready, b)
                            dve.wait_ge(yb_added, b)
                            nc.vector.tensor_tensor(xb, xb, psY[:, 0:D], ALU.add).then_inc(added, 1)

                Pipeline.run(dve, slots)
                dve.wait_ge(added, B)


def cross_stage(nc, glob, dram):
    st = Stage(nc, "cross")
    with st.ctx:
        ln = LayerNorm(nc, st, glob)
        x, ctxT = glob["x"], glob["ctxT"]
        SCALE = float(D) ** -0.5
        names = ("Wq_c", "Wk_s", "Wq_s", "Wk_c")
        w = [st.sb(n, [P, D]) for n in names]
        bias = [st.sb("b" + n[1:], [P, 1]) for n in names]
        wvs, wvc = st.sb("Wv_s", [P, D]), st.sb("Wv_c", [P, D])
        bv = st.sb("bv", [P, 2, D])
        wg, bg = st.sb("Wg", [P, 2, D]), st.sb("bg", [P, D])
        VW = D + 1
        vs = st.sb("v_sub", [P, B, VW])
        vc = [st.sb(f"v_char{i}", [P, VW]) for i in range(2)]
        qk = st.sb("qkT", [P, 4, S])
        mx, nmx = st.sb("row_max", [P, 2]), st.sb("minus_max", [P, 2])
        prob, probT = st.sb("prob", [P, 2, S]), st.sb("probT", [P, 2, S])
        rz = st.sb("rz", [P, 2])
        att = st.sb("attended", [P, 2, D])
        attT = st.sb("attendedT", [P, 2, D])
        zb, ez, den, gt, df, gd = (st.sb(n, [P, D]) for n in ("gate_in", "exp_gate", "den", "gate", "delta",
                                                             "gated"))
        psV = [st.ps("ps_proj0"), st.ps("ps_proj1")]
        psS, psT, psO, psG = st.ps("ps_scores"), st.ps("ps_T"), st.ps("ps_out"), st.ps("ps_gate")
        psU = st.ps("ps_attT")
        there = Pipeline.there
        sems = ["w_in", "b_in", "bv_in", "ones_ready", "vs_proj", "vs_stored", "qk_proj", "qk_stored", "vc_proj",
                "vc_stored", "scores_ready", "max_done", "nmax_done", "exp_done", "transposed", "probT_stored",
                "out_ready", "rz_ready", "att_ready", "att_transposed", "attT_stored", "gate_mm", "zb_ready",
                "ez_ready", "den_ready", "gt_ready", "df_ready", "gd_ready", "s_added", "added"]
        q = {n: st.sem(n) for n in sems}

        with nc.Block() as block:
            @block.sync
            def _(sp):
                for i, n in enumerate(names):
                    sp.dma_start(w[i][:, :], dram["L1_xattn_" + n]).then_inc(q["w_in"], 16)
                    sp.dma_start(bias[i][:, :], dram["L1_xattn_b" + n[1:]].unsqueeze(1)).then_inc(q["b_in"], 16)
                sp.dma_start(wvs[:, :], dram["L1_xattn_Wv_s"]).then_inc(q["w_in"], 16)
                sp.dma_start(wvc[:, :], dram["L1_xattn_Wv_c"]).then_inc(q["w_in"], 16)
                sp.dma_start(wg[:, :, :], dram["L1_xattn_Wg"].rearrange("(c p) n -> p c n", p=P)).then_inc(q["w_in"], 16)
                for i, n in enumerate(("bv_s", "bv_c")):
                    sp.dma_start(bv[:, i, :], dram["L1_xattn_" + n].unsqueeze(0).to_broadcast([P, D])).then_inc(
                        q["bv_in"], 16)
                sp.dma_start(bg[:, :], dram["L1_xattn_bg"].unsqueeze(0).to_broadcast([P, D])).then_inc(q["bv_in"], 16)

            @block.gpsimd
            def _(pool):
                nc.gpsimd.memset(vs[:, :, :].rearrange("p b e -> p (b e)"), 1.0).then_inc(q["ones_ready"], 1)
                for i in range(2):
                    nc.gpsimd.memset(vc[i][:, :], 1.0).then_inc(q["ones_ready"], 1)
                ln.pool_rstd(pool)

            @block.tensor
            def _(pe):
                pe.wait_ge(q["w_in"], 7 * 16)
                for b in range(B):
                    nc.tensor.matmul(psV[b // 4][:, b % 4 * D:(b % 4 + 1) * D], ctxT[:, b, :], wvs[:, :],
                                     start=True, stop=True).then_inc(q["vs_proj"], 1)
                pe.wait_ge(q["vs_stored"], 2)

                def slots(b, p, sb):
                    if there(sb, 0):
                        pe.wait_ge(q["qk_stored"], 4 * b + 4)
                        for m in range(2):
                            last = nc.tensor.matmul(psS[:, m * S:(m + 1) * S], qk[:, 2 * m, :], qk[:, 2 * m + 1, :],
                                                    start=True, stop=True)
                        last.then_inc(q["scores_ready"], 1)
                    if there(sb, 1):
                        ln.pe_transpose(pe, b + 1)
                    if there(sb, -1):
                        pe.wait_ge(q["att_ready"], 2 * b)
                        for m in range(2):
                            last = nc.tensor.transpose(psU[:, m * S:(m + 1) * S], att[:, m, :], glob["ident"][:, :])
                        last.then_inc(q["att_transposed"], 1)
                    if there(sb, 1):
                        pe.wait_ge(ln.xT_ready, b + 2)
                        if there(sb, 0):
                            pe.wait_ge(q["vc_stored"], b + 1)
                        nc.tensor.matmul(psV[1][:, 0:D], ln.xT[:, :], wvc[:, :], start=True, stop=True).then_inc(
                            q["vc_proj"], 1)
                        for i in range(4):
                            rhs = ln.xT[:, :] if i in (0, 3) else ctxT[:, bass.ds(b + 1, 1), :]
                            last = nc.tensor.matmul(psV[0][:, i * S:(i + 1) * S], w[i][:, :], rhs, start=True,
                                                    stop=True)
                        last.then_inc(q["qk_proj"], 1)
                    if there(sb, -1):
                        pe.wait_ge(q["attT_stored"], b)
                        for m in range(2):
                            last = nc.tensor.matmul(psG[:, 0:D], attT[:, m, :], wg[:, m, :], start=(m == 0),
                                                    stop=(m == 1))
                        last.then_inc(q["gate_mm"], 1)
                    if there(sb, 0):
                        pe.wait_ge(q["exp_done"], 2 * b + 2)
                        for m in range(2):
                            last = nc.tensor.transpose(psT[:, m * S:(m + 1) * S], prob[:, m, :], glob["ident"][:, :])
                        last.then_inc(q["transposed"], 1)
                        pe.wait_ge(q["probT_stored"], b + 1)
                        pe.wait_ge(q["vc_stored"], b + 1)
                        nc.tensor.matmul(psO[:, 0:VW], probT[:, 0, :], vs[:, bass.ds(b, 1), :], start=True, stop=True)
                        nc.tensor.matmul(psO[:, 256:256 + VW], probT[:, 1, :], vc[p][:, :], start=True,
                                         stop=True).then_inc(q["out_ready"], 1)

                Pipeline.run(pe, slots)

            @block.scalar
            def _(act):
                act.wait_ge(q["b_in"], 64)

                def slots(b, p, sb):
                    if there(sb, 1):
                        ln.act_store(act, b + 1)
                    if there(sb, 0):
                        act.wait_ge(q["nmax_done"], b + 1)
                        for m in range(2):
                            nc.scalar.activation(prob[:, m, :], psS[:, m * S:(m + 1) * S], ACT.Exp,
                                                 bias=nmx[:, m:m + 1], scale=SCALE).then_inc(q["exp_done"], 1)
                    if there(sb, -1):
                        act.wait_ge(q["att_transposed"], b)
                        nc.scalar.copy(attT[:, :, :], psU[:, 0:2 * S]).then_inc(q["attT_stored"], 1)
                    if there(sb, 1):
                        act.wait_ge(q["qk_proj"], b + 2)
                        for i in range(4):
                            nc.scalar.activation(qk[:, i, :], psV[0][:, i * S:(i + 1) * S], ACT.Identity,
                                                 bias=bias[i][:, 0:1]).then_inc(q["qk_stored"], 1)
                    if there(sb, 0):
                        act.wait_ge(q["transposed"], b + 1)
                        nc.scalar.copy(probT[:, :, :], psT[:, 0:2 * S]).then_inc(q["probT_stored"], 1)
                    if there(sb, -1):
                        act.wait_ge(q["zb_ready"], b)
                        nc.scalar.activation(ez[:, :], zb[:, :], ACT.Exp, scale=-1.0).then_inc(q["ez_ready"], 1)

                Pipeline.run(act, slots)

            @block.vector
            def _(dve):
                def then(ins, name, b):
                    ins.then_inc(q[name], 1)
                    dve.wait_ge(q[name], b + 1)

                ln.dve_stats(dve)
                dve.wait_ge(q["ones_ready"], 3)
                dve.wait_ge(q["bv_in"], 48)
                for i in range(2):
                    dve.wait_ge(q["vs_proj"], 4 * i + 4)
                    nc.vector.tensor_copy(vs[:, 4 * i:4 * i + 4, 0:D],
                                          psV[i][:, :].rearrange("p (b e) -> p b e", b=4)).then_inc(q["vs_stored"], 1)

                def slots(b, p, sb):
                    if there(sb, 0):
                        dve.wait_ge(q["scores_ready"], b + 1)
                        then(nc.vector.tensor_reduce(mx[:, :], psS[:, 0:2 * S].rearrange("p (m t) -> p m t", m=2),
                                                     AX, ALU.max), "max_done", b)
                        nc.vector.tensor_scalar(nmx[:, :], mx[:, :], -SCALE, None, ALU.mult).then_inc(
                            q["nmax_done"], 1)
                    if there(sb, 1):
                        dve.wait_ge(q["vc_proj"], b + 2)
                        nc.vector.tensor_copy(vc[1 - p][:, 0:D], psV[1][:, 0:D]).then_inc(q["vc_stored"], 1)
                    if there(sb, 2):
                        ln.dve_normalise(dve, b + 2)
                    if there(sb, -1):
                        dve.wait_ge(q["gate_mm"], b)
                        nc.vector.tensor_tensor(zb[:, :], psG[:, 0:D], bg[:, :], ALU.add).then_inc(q["zb_ready"], 1)
                        dve.wait_ge(q["ez_ready"], b)
                        then(nc.vector.tensor_scalar(den[:, :], ez[:, :], 1.0, None, ALU.add), "den_ready", b - 1)
                        then(nc.vector.reciprocal(gt[:, :], den[:, :]), "gt_ready", b - 1)
                        dve.wait_ge(q["df_ready"], b)
                        then(nc.vector.tensor_tensor(gd[:, :], gt[:, :], df[:, :], ALU.mult), "gd_ready", b - 1)
                        dve.wait_ge(q["s_added"], b)
                        xb = x[:, bass.ds(b - 1, 1), :]
                        nc.vector.tensor_tensor(xb, xb, over(gd[:, :], 1), ALU.add).then_inc(q["added"], 1)
                    if there(sb, 0):
                        dve.wait_ge(q["out_ready"], b + 1)
                        o3 = psO[:, :].rearrange("p (m c) -> p m c", m=2)
                        then(nc.vector.reciprocal(rz[:, :], o3[:, :, D]), "rz_ready", b)
                        for m in range(2):
                            nc.vector.scalar_tensor_tensor(att[:, m, :], o3[:, m, 0:D], rz[:, m:m + 1], bv[:, m, :],
                                                           ALU.mult, ALU.add).then_inc(q["att_ready"], 1)
                        dve.wait_ge(q["att_ready"], 2 * b + 2)
                        nc.vector.tensor_tensor(df[:, :], att[:, 0, :], att[:, 1, :], ALU.subtract).then_inc(
                            q["df_ready"], 1)
                        xb = x[:, bass.ds(b, 1), :]
                        nc.vector.tensor_tensor(xb, xb, over(att[:, 1, :], 1), ALU.add).then_inc(q["s_added"], 1)

                Pipeline.run(dve, slots)
                dve.wait_ge(q["added"], B)


class Signal:

    CREDIT = 2

    def __init__(self, st, name, eng, by_engine):
        self.sem = st.sem(name)
        by_engine.setdefault(eng, []).append(self)

    def seen(self, n):
        return n + 1 + self.CREDIT

    def prior(self, n):
        return n + self.CREDIT

    def freed(self, n):
        return n - 1 + self.CREDIT


def local_stage(nc, glob, dram):
    st = Stage(nc, "loc")
    with st.ctx:
        x, ident = glob["x"], glob["ident"]
        C4 = 2 * INNER // BANK
        VC = INNER // BANK
        HP = BANK // HD_F
        QC = INNER // P
        NG = H // G
        VW = HD_F + 1
        HALF = HD_F // 2
        DH = D // 2
        FFN = "feed-forward"
        FCH = [P, P, DI - 2 * P]
        wqkv, wo = st.sb("w_qkv", [P, 3 * INNER]), st.sb("w_o", [P, QC, D])
        w1, w2 = st.sb("w1", [P, 2 * DI]), st.sb("w2", [P, 3, D])
        b1, lng, b2 = st.sb("b1", [P, 2, 3]), st.sb("ln_gb", [P, 2]), st.sb("b2", [P, D])
        shift = st.sb("shift", [P, P])
        band = st.sb("band", [P, S])
        identb, maskb = st.sb("ident_bf", [P, P], BF16), st.sb("mask_bf", [P, BANK], BF16)
        rotc, qks, rot = (st.sb(n, [P, 2, 2 * HD_F]) for n in ("rot_const", "qk_scale", "rot"))
        xin = st.sb("x_in", [P, D])
        xsT = [st.sb(f"xsT{i}", [P, S]) for i in range(2)]
        raw, sq, t1, t2, sm, qn = ([st.sb(f"{n}{i}", [P, HP, HD_F]) for i in range(2)]
                                   for n in ("raw", "squares", "rot_a", "rot_b", "rotated", "qk_norm"))
        ssq, ssc, rn = ([st.sb(f"{n}{i}", [P, HP]) for i in range(2)] for n in ("ssq", "ssq_max", "r_norm"))
        qT = [st.sb(f"qT{i}", [P, QC, S]) for i in range(2)]
        kT = [st.sb(f"kT{i}", [P, 2, QC, S]) for i in range(2)]
        v = [st.sb(f"v{i}", [P, H * VW + WIN]) for i in range(2)]
        v3 = [a[:, 0:H * VW].rearrange("p (h e) -> p h e", e=VW) for a in v]
        mx = [st.sb(f"row_max{i}", [P, G]) for i in range(2)]
        dif, prob, probT = ([st.sb(f"{n}{i}", [P, BANK]) for i in range(2)] for n in ("dif", "prob", "probT"))
        rz = st.sb("rz", [P, G])
        y, yT = st.sb("y", [P, INNER]), st.sb("yT", [P, INNER])
        HB = B // 2
        xs, xh = st.sb("xs", [P, HB, D]), st.sb("x_hat", [P, HB, D])
        stats, mv = st.sb("stats", [P, B, 6]), st.sb("mv", [P, B, 2])
        ve, rstd = st.sb("var_eps", [P, B]), st.sb("rstd", [P, B])
        ones = st.sb("ones", [P, HB * DH])
        xnT = st.sb("xnT", [P, BANK])
        gl = st.sb("gelu", [P, 3, BANK])
        hT = st.sb("hT", [P, 3, BANK])
        bank = [st.ps(f"bank{i}") for i in range(8)]
        psX, psQ, psS, psTP, psTQ, psO = bank[0], bank[1:3], bank[3:5], bank[5], bank[6], bank[7]
        psY = psX

        x0 = st.sb("x_before", [P, B, D])
        in_stats, in_mv, in_ve, in_rstd = (st.sem(n) for n in ("in_stats", "in_mv", "in_var_eps", "in_rstd"))
        x0_kept = st.sem("x0_kept")
        own = {}

        def sig(name, eng):
            return Signal(st, name, eng, own)

        const_in, wo_in, wf_in = st.sem("const_in"), st.sem("w_o_in"), st.sem("w_ffn_in")
        qks_in, piece_in = st.sem("qk_scale_in"), [st.sem(f"w_piece{k}_in") for k in range(C4 + VC)]
        band_in, bf_ready = st.sem("band_in"), st.sem("bf_ready")
        ones_ready, zeros_ready = st.sem("ones_ready"), st.sem("zeros_ready")
        rot_ready = sig("rot_ready", "dve")
        xin_ready = sig("xin_ready", "pool")
        psx_ready, xsT_ready = sig("psx_ready", "pe"), sig("xsT_ready", "act")
        psq_ready, psq_read = sig("psq_ready", "pe"), sig("psq_read", "act")
        sq_ready, rotab_ready = sig("sq_ready", "act"), sig("rotab_ready", "dve")
        ssq_ready, ssc_ready = sig("ssq_ready", "dve"), sig("ssc_ready", "dve")
        sum_ready, rn_ready, qn_ready = sig("sum_ready", "pool"), sig("rn_ready", "pool"), sig("qn_ready", "dve")
        qk_transposed, qk_stored = sig("qk_transposed", "pe"), sig("qk_stored", "act")
        scores_ready, max_ready, dif_ready = sig("scores_ready", "pe"), sig("max_ready", "dve"), sig("dif_ready", "dve")
        exp_ready, p_transposed, p_stored = sig("exp_ready", "act"), sig("p_transposed", "pe"), sig("p_stored", "act")
        out_ready, rz_ready, y_ready = sig("out_ready", "pe"), sig("rz_ready", "dve"), sig("y_ready", "dve")
        o_ready, added = sig("o_ready", "pe"), sig("added", "dve")
        xs0_ready, stats_ready = sig("xs0_ready", "pool"), sig("stats_ready", "dve")
        mv_ready, ve_ready = sig("mv_ready", "dve"), sig("ve_ready", "dve")
        rstd_ready, xh_ready, b2_added = sig("rstd_ready", "pool"), sig("xh_ready", "dve"), sig("b2_added", "pool")
        up_ready, h_ready = sig("up_ready", "pe"), sig("h_ready", "dve")
        down_ready, f_added = sig("down_ready", "pe"), sig("f_added", "dve")

        def load_piece(sp, l, k):
            sp.dma_start(wqkv[:, k * BANK:(k + 1) * BANK], dram["L1_ffn_Wqkv"][
                bass.ds(l, 1), :, k * BANK:(k + 1) * BANK].rearrange("a p n -> p (a n)")).then_inc(piece_in[k], 16)

        def load_qks(sp, l):
            sp.dma_start(qks[:, :, :], dram["qk_scale"][bass.ds(l, 1), :].to_broadcast([P, 4 * HD_F])).then_inc(
                qks_in, 16)

        def load_wo(sp, l):
            sp.dma_start(wo[:, :, :], dram["L1_ffn_Wo"][bass.ds(l, 1), :, :].rearrange(
                "a (c p) n -> p (a c) n", p=P)).then_inc(wo_in, 16)

        def load_ffn(sp, l):
            sp.dma_start(w1[:, :], dram["L1_ffn_W1"][bass.ds(l, 1), :, :].rearrange("a p n -> p (a n)")).then_inc(
                wf_in, 16)
            sp.dma_start(w2[:, :, :], dram["L1_ffn_W2"][bass.ds(l, 1), :, :].rearrange(
                "a (c p) n -> p (a c) n", p=P)).then_inc(wf_in, 16)
            sp.dma_start(b1[:, :, :], dram["L1_ffn_b1"][bass.ds(l, 1), :, :].rearrange(
                "a p n -> p (a n)")).then_inc(wf_in, 16)
            sp.dma_start(lng[:, :], dram["ln_gb"][bass.ds(l, 1), :, :].rearrange("a p n -> p (a n)")).then_inc(
                wf_in, 16)
            sp.dma_start(b2[:, :], dram["L1_ffn_b2"][bass.ds(l, 1), :].to_broadcast([P, D])).then_inc(wf_in, 16)

        with nc.Block() as block:
            @block.sync
            def _(sp):
                sp.dma_start(shift[:, :], dram["c_shift"]).then_inc(const_in, 16)
                sp.dma_start(rotc[:, :, :], dram["c_rot"]).then_inc(const_in, 16)
                for k in range(C4 + VC):
                    load_piece(sp, 0, k)
                load_qks(sp, 0)
                load_wo(sp, 0)
                load_ffn(sp, 0)
                sp.dma_start(band[:, :], dram["c_band"]).then_inc(band_in, 16)
                sp.wait_ge(const_in, 32)

            @block.gpsimd
            def _(pool):
                for i in range(2):
                    nc.gpsimd.memset(v[i][:, :], 1.0).then_inc(ones_ready, 1)
                for i in range(2):
                    nc.gpsimd.memset(kT[i][:, :, :, :].rearrange("p r c n -> p (r c n)"), 0.0).then_inc(zeros_ready, 1)
                for s in own["pool"]:
                    pool.sem_inc(s.sem, s.CREDIT)
                pool.wait_ge(in_ve, 1)
                nc.gpsimd.tensor_tensor(rstd[:, :], ve[:, :], glob["mhalf"][:, 0:B], ALU.pow).then_inc(in_rstd, 1)
                nc.gpsimd.memset(ones[:, :], 1.0).then_inc(ones_ready, 1)
                pool.wait_ge(ones_ready, 3)

            @block.tensor
            def _(pe):
                for s in own["pe"]:
                    pe.sem_inc(s.sem, s.CREDIT)

            @block.scalar
            def _(act):
                for s in own["act"]:
                    act.sem_inc(s.sem, s.CREDIT)
                nc.scalar.copy(x0[:, :, :], x[:, :, :]).then_inc(x0_kept, 1)
                nc.scalar.copy(identb[:, :], ident[:, :]).then_inc(bf_ready, 1)
                act.wait_ge(band_in, 16)
                nc.scalar.copy(maskb[:, :].rearrange("p (h m) -> p h m", h=G), over(band[:, :], G)).then_inc(
                    bf_ready, 1)

            @block.vector
            def _(dve):
                for s in own["dve"]:
                    dve.sem_inc(s.sem, s.CREDIT)
                for b in range(B):
                    nc.vector.bn_stats(stats[:, b, :], x[:, b, :]).then_inc(in_stats, 1)
                for b in range(B):
                    dve.wait_ge(in_stats, b + 1)
                    nc.vector.bn_aggr(mv[:, b, :], stats[:, b, :]).then_inc(in_mv, 1)
                dve.wait_ge(in_mv, B)
                nc.vector.tensor_scalar(ve[:, :], mv[:, :, 1], LN_EPS, None, ALU.add).then_inc(in_ve, 1)
                dve.wait_ge(in_rstd, 1)
                dve.wait_ge(x0_kept, 1)
                for b in range(B):
                    nc.vector.tensor_scalar(x[:, b, :], x[:, b, :], mv[:, b, 0:1], rstd[:, b:b + 1],
                                            ALU.subtract, ALU.mult)

        ORDER = [(1, "qk3"), (1, "v0"), (FFN, "shift"), (2, "qk0"), (-1, "y0"), (FFN, "xh"), (2, "qk1"), (-1, "y1"),
                 (1, "v1"), (FFN, "gate0"), (FFN, "gate1"), (FFN, "gate2"), (2, "qk2")]
        FILL, PASS, DRAIN = range(-2, 2), range(2, B + 2), range(2, B + 2)

        def ffn_half(b):
            return {HB + 1: 0, B + 1: 1}.get(b)

        def there(sb, off):
            b, steps = sb
            return not (steps is FILL and b + off < 0 or steps is DRAIN and b + off >= B)

        def uses(sb, kind):
            return ffn_half(sb[0]) is not None if kind is FFN else there(sb, kind)

        def first_steps(steps):
            return [(b, FILL) for b in FILL] + ([] if steps is FILL else [(b, steps) for b in steps])

        def uses_before(sb, what):
            n = 0
            for step in first_steps(sb[1]):
                for kind, name in ORDER:
                    if step == sb and name == what:
                        return n
                    n += uses(step, kind)

        PASS_USES = sum(uses((b, PASS), kind) for b in PASS for kind, _ in ORDER)

        def use(l, sb, what):
            return l * PASS_USES + uses_before(sb, what)

        def before(sb):
            steps = first_steps(sb[1])
            return steps[steps.index(sb) - 1]

        def last_use(sb):
            return "qk2" if there(sb, 2) else "v1" if there(sb, 1) else "y1"

        def bank_of(sb, what):
            return psQ[uses_before(sb, what) % 2]

        def pipeline(eng, slots):
            for b in FILL:
                slots(0, b, b % 2, (b, FILL))
            with eng.Fori(0, DEPTH - 1) as l:
                for b in PASS:
                    slots(l, b, b % 2, (b, PASS))
            for b in DRAIN:
                slots(DEPTH - 1, b, b % 2, (b, DRAIN))

        def lag(g, n):
            return (0, g - n) if 0 <= g - n < 4 else ((-1, g - n + 4) if g < n else (1, g - n - 4))

        PIECE_LEAD = 7

        def piece_at(g, behind=0):
            n = g + PIECE_LEAD - behind
            return n // 4, n % 4

        with nc.Block() as block:
            @block.sync
            def _(sp):
                with sp.Fori(0, DEPTH - 1) as l:
                    sp.wait_ge(rot_ready.sem, rot_ready.seen(l))
                    load_qks(sp, l + 1)
                    for b, what, k in ((HB + 1, "qk0", 0), (HB + 1, "qk1", 1), (HB + 1, "qk2", 2),
                                       (HB + 2, "qk3", 3), (HB + 2, "v0", 4), (HB + 2, "v1", 5)):
                        sp.wait_ge(psq_ready.sem, psq_ready.seen(use(l, (b, PASS), what)))
                        load_piece(sp, l + 1, k)
                    sp.wait_ge(o_ready.sem, o_ready.seen(l * B + B - 1))
                    load_wo(sp, l + 1)
                    sp.wait_ge(b2_added.sem, b2_added.seen(2 * l + 1))
                    sp.wait_ge(down_ready.sem, down_ready.seen(2 * l + 1))
                    load_ffn(sp, l + 1)

            @block.gpsimd
            def _(pool):
                def pool_copy(to, a):
                    one = ones[:, 0:D] if len(a.shape) == 2 else ones[:, :].rearrange("p (b e) -> p b e", b=HB)
                    return nc.gpsimd.tensor_tensor(to, a, one, ALU.mult)

                def front(t, k):
                    n = t * C4 + k
                    i = k % 2
                    pool.wait_ge(ssc_ready.sem, ssc_ready.seen(n))
                    nc.gpsimd.tensor_tensor(rn[i][:, :], ssc[i][:, :], glob["mhalf"][:, 0:HP],
                                            ALU.pow).then_inc(rn_ready.sem, 1)
                    pool.wait_ge(rotab_ready.sem, rotab_ready.seen(n))
                    pool.wait_ge(qn_ready.sem, qn_ready.freed(n))
                    nc.gpsimd.tensor_tensor(sm[i][:, :, :], t1[i][:, :, :], t2[i][:, :, :],
                                            ALU.add).then_inc(sum_ready.sem, 1)

                def slots(l, b, p, sb):
                    half = ffn_half(b)
                    for g in range(NG):
                        if g == 0 and there(sb, 2):
                            if b == HB + 2 or sb == (2, PASS) or sb == (2, DRAIN):
                                pool.wait_ge(f_added.sem, f_added.seen(2 * l + (0 if b == HB + 2 else -1)))
                            pool_copy(xin[:, :], x[:, (b + 2) % B, :]).then_inc(xin_ready.sem, 1)
                        if half is not None:
                            f, hb = 2 * l + half, slice(half * HB, (half + 1) * HB)
                            if g == 0:
                                pool.wait_ge(added.sem, added.seen(l * B + half * HB + HB - 1))
                                pool.wait_ge(xh_ready.sem, xh_ready.prior(f))
                                pool_copy(xs[:, :, 0:DH], x[:, hb, 0:DH]).then_inc(xs0_ready.sem, 1)
                            if g == 1:
                                pool.wait_ge(ve_ready.sem, ve_ready.seen(f))
                                nc.gpsimd.tensor_tensor(rstd[:, 0:HB], ve[:, 0:HB], glob["mhalf"][:, 0:HB],
                                                        ALU.pow).then_inc(rstd_ready.sem, 1)
                        off, k = piece_at(g)
                        if there(sb, off):
                            front(l * B + b + off, k)
                        if half is not None and g == 1:
                            pool.wait_ge(wf_in, (l + 1) * 80)
                            pool.wait_ge(xs0_ready.sem, xs0_ready.seen(f))
                            pool.wait_ge(psq_ready.sem, psq_ready.seen(use(l, sb, "shift")))
                            nc.gpsimd.tensor_tensor(x[:, hb, :], x[:, hb, :], over(b2[:, :], HB),
                                                    ALU.add).then_inc(b2_added.sem, 1)

                pipeline(pool, slots)

            @block.tensor
            def _(pe):
                def shifted(t, full):
                    if full:
                        pe.wait_ge(added.sem, added.seen(t - 4))
                    pe.wait_ge(xin_ready.sem, xin_ready.seen(t))
                    nc.tensor.matmul(psX[0:DH, 0:S], xin[:, 0:DH], ident[:, :], start=True, stop=True)
                    nc.tensor.matmul(psX[DH:D, 0:S], xin[:, DH:D], shift[:, :], start=True,
                                     stop=True).then_inc(psx_ready.sem, 1)

                def project(l, b, sb, off, what, p, k):
                    if what == "qk0":
                        pe.wait_ge(xsT_ready.sem, xsT_ready.seen(l * B + b + off))
                    if (b + off) % B == 0:
                        pe.wait_ge(piece_in[k], (l + 1 + (b + off) // B) * 16)
                    pe.wait_ge(psq_read.sem, psq_read.freed(use(l, sb, what)))
                    nc.tensor.matmul(bank_of(sb, what)[:, :], xsT[p][:, :], wqkv[:, k * BANK:(k + 1) * BANK],
                                     start=True, stop=True).then_inc(psq_ready.sem, 1)

                def turn_qk(t, k):
                    n = t * C4 + k
                    pe.wait_ge(qn_ready.sem, qn_ready.seen(n))
                    pe.wait_ge(qk_stored.sem, qk_stored.prior(n))
                    for c in range(4):
                        last = nc.tensor.transpose(psTQ[:, c * S:(c + 1) * S],
                                                   qn[k % 2][:, 2 * c:2 * c + 2, :].rearrange("p h e -> p (h e)"),
                                                   ident[:, :])
                    last.then_inc(qk_transposed.sem, 1)

                def scores(t, p, g):
                    n = t * NG + g
                    if g == 0:
                        pe.wait_ge(qk_stored.sem, qk_stored.seen(t * C4 + C4 - 1))
                    pe.wait_ge(dif_ready.sem, dif_ready.freed(n))
                    ps = psS[g % 2]
                    nc.tensor.matmul(ps[:, :], identb[:, :], maskb[:, :], start=True, stop=False)
                    for j in range(G):
                        c = g % 2 * G + j
                        last = nc.tensor.matmul(ps[:, j * S:(j + 1) * S], qT[p][:, c, :],
                                                kT[p][:, g // 2, c, :], start=False, stop=(j == G - 1))
                    last.then_inc(scores_ready.sem, 1)

                def turn_p(t, g):
                    n = t * NG + g
                    pe.wait_ge(exp_ready.sem, exp_ready.seen(n))
                    pe.wait_ge(p_stored.sem, p_stored.prior(n))
                    for j in range(G):
                        last = nc.tensor.transpose(psTP[:, j * S:(j + 1) * S],
                                                   prob[g % 2][:, j * S:(j + 1) * S], ident[:, :])
                    last.then_inc(p_transposed.sem, 1)

                def values(l, b, t, p, g, sb):
                    n = t * NG + g
                    pe.wait_ge(p_stored.sem, p_stored.seen(n))
                    pe.wait_ge(y_ready.sem, y_ready.prior(n))
                    if g == 0:
                        at = before(sb)
                        pe.wait_ge(psq_read.sem, psq_read.seen(use(l, at, last_use(at))))
                    if g == 1 and ffn_half(b) is not None:
                        pe.wait_ge(h_ready.sem, h_ready.seen((2 * l + ffn_half(b)) * 3 + 2))
                    if g == 2 and b == HB + 2:
                        pe.wait_ge(f_added.sem, f_added.seen(2 * l))
                    if g == 2 and sb in ((2, PASS), (2, DRAIN)):
                        pe.wait_ge(f_added.sem, f_added.seen(2 * l - 1))
                    for j in range(G):
                        c = (g * G + j) * VW
                        last = nc.tensor.matmul(psO[:, j * S:j * S + WIN], probT[g % 2][:, j * S:(j + 1) * S],
                                                v[p][:, c:c + WIN], start=True, stop=True)
                    last.then_inc(out_ready.sem, 1)

                def turn_y(l, b, sb, i):
                    what = f"y{i}"
                    pe.wait_ge(psq_read.sem, psq_read.freed(use(l, sb, what)))
                    pe.wait_ge(y_ready.sem, y_ready.seen((l * B + b - 1) * NG + 2 * i + 1))
                    for c in range(4):
                        cc = 4 * i + c
                        last = nc.tensor.transpose(bank_of(sb, what)[:, c * S:(c + 1) * S],
                                                   y[:, cc * P:(cc + 1) * P], ident[:, :])
                    last.then_inc(psq_ready.sem, 1)

                def output(l, b, sb):
                    pe.wait_ge(psq_read.sem, psq_read.seen(use(l, sb, "y1")))
                    if b % B == 0:
                        pe.wait_ge(wo_in, (l + 1 + b // B) * 16)
                    for c in range(QC):
                        last = nc.tensor.matmul(psY[:, 0:D], yT[:, c * P:(c + 1) * P], wo[:, c, :],
                                                start=(c == 0), stop=(c == QC - 1))
                    last.then_inc(o_ready.sem, 1)

                def ffn_shift(l, f, sb, half):
                    pe.wait_ge(psq_read.sem, psq_read.freed(use(l, sb, "shift")))
                    pe.wait_ge(added.sem, added.seen(l * B + half * HB + HB - 1))
                    nc.tensor.matmul(bank_of(sb, "shift")[:, 0:HB * DH], shift[:, :],
                                     x[:, half * HB:(half + 1) * HB, DH:D], start=True, stop=True).then_inc(
                        psq_ready.sem, 1)

                def ffn_turn(l, f, sb):
                    pe.wait_ge(psq_read.sem, psq_read.freed(use(l, sb, "xh")))
                    pe.wait_ge(xh_ready.sem, xh_ready.seen(f))
                    for k in range(HB):
                        last = nc.tensor.transpose(bank_of(sb, "xh")[:, k * S:(k + 1) * S], xh[:, k, :], ident[:, :])
                    last.then_inc(psq_ready.sem, 1)

                def ffn_up(l, b, f, sb):
                    pe.wait_ge(wf_in, (l + 1) * 80)
                    pe.wait_ge(psq_read.sem, psq_read.seen(use(l, sb, "xh")))
                    if there(sb, 0):
                        pe.wait_ge(y_ready.sem, y_ready.seen((l * B + b) * NG))
                    for c in range(3):
                        what = f"gate{c}"
                        pe.wait_ge(psq_read.sem, psq_read.freed(use(l, sb, what)))
                        nc.tensor.matmul(bank_of(sb, what)[0:FCH[c], :], w1[:, DI + c * P:DI + c * P + FCH[c]],
                                         xnT[:, :], start=True, stop=True).then_inc(psq_ready.sem, 1)
                        pe.wait_ge(h_ready.sem, h_ready.prior(3 * f + c))
                        nc.tensor.matmul(psO[0:FCH[c], :], w1[:, c * P:c * P + FCH[c]],
                                         xnT[:, :], start=True, stop=True).then_inc(up_ready.sem, 1)

                def ffn_down(l, b, f, sb):
                    pe.wait_ge(h_ready.sem, h_ready.seen(3 * f + 2))
                    if there(sb, 0):
                        pe.wait_ge(y_ready.sem, y_ready.seen((l * B + b) * NG + 1))
                    for k in range(HB):
                        for c in range(3):
                            last = nc.tensor.matmul(psO[:, k * D:(k + 1) * D], hT[0:FCH[c], c, k * P:(k + 1) * P],
                                                    w2[0:FCH[c], c, :], start=(c == 0), stop=(c == 2))
                    last.then_inc(down_ready.sem, 1)

                def slots(l, b, p, sb):
                    half = ffn_half(b)
                    f = None if half is None else 2 * l + half
                    for g in range(NG):
                        off, k = lag(g, 1)
                        if there(sb, off):
                            turn_p(l * B + b + off, k)
                        off, k = piece_at(g)
                        if there(sb, off):
                            project(l, b, sb, off, f"qk{k}", (p + off) % 2, k)
                        off, k = piece_at(g, 2)
                        if there(sb, off):
                            turn_qk(l * B + b + off, k)
                        off, k = lag(g, -1)
                        if there(sb, off):
                            scores(l * B + b + off, (p + off) % 2, k)
                        off, k = lag(g, 2)
                        if there(sb, off):
                            values(l, b, l * B + b + off, (p + off) % 2, k, sb)
                        if g == 0 and there(sb, 1):
                            project(l, b, sb, 1, "v0", (p + 1) % 2, C4)
                        if g == 0 and half is not None:
                            ffn_shift(l, f, sb, half)
                        if g == 0 and there(sb, 2):
                            shifted(l * B + b + 2, sb[1] is not FILL)
                        if g == 1 and there(sb, -1):
                            turn_y(l, b, sb, 0)
                        if g == 1 and half is not None:
                            ffn_turn(l, f, sb)
                        if g == 2:
                            if there(sb, -1):
                                turn_y(l, b, sb, 1)
                            if there(sb, 1):
                                project(l, b, sb, 1, "v1", (p + 1) % 2, C4 + 1)
                            if half is not None:
                                ffn_up(l, b, f, sb)
                        if g == 3:
                            if there(sb, -1):
                                output(l, b - 1, sb)
                            if half is not None:
                                ffn_down(l, b, f, sb)

                pipeline(pe, slots)

            @block.scalar
            def _(act):
                def store_x(t, p):
                    act.wait_ge(psx_ready.sem, psx_ready.seen(t))
                    nc.scalar.copy(xsT[p][:, :], psX[:, 0:S]).then_inc(xsT_ready.sem, 1)

                def store_raw(l, t, sb, k):
                    n = t * C4 + k
                    what = f"qk{k}"
                    act.wait_ge(psq_ready.sem, psq_ready.seen(use(l, sb, what)))
                    act.wait_ge(ssq_ready.sem, ssq_ready.freed(n))
                    nc.scalar.square(sq[k % 2][:, :, :], bank_of(sb, what)[:, :]).then_inc(sq_ready.sem, 1)
                    act.wait_ge(rotab_ready.sem, rotab_ready.freed(n))
                    nc.scalar.copy(raw[k % 2][:, :, :], bank_of(sb, what)[:, :]).then_inc(psq_read.sem, 1)

                def store_v(l, sb, p, i):
                    u = use(l, sb, f"v{i}")
                    act.wait_ge(psq_ready.sem, psq_ready.seen(u))
                    nc.scalar.copy(v3[p][:, i * HP:(i + 1) * HP, 0:HD_F],
                                   bank_of(sb, f"v{i}")[:, :].rearrange("p (h e) -> p h e", h=HP)).then_inc(
                        psq_read.sem, 1)

                def store_qk(t, p, k):
                    n = t * C4 + k
                    c = k % 2 * 4
                    act.wait_ge(qk_transposed.sem, qk_transposed.seen(n))
                    if k < 2:
                        nc.scalar.copy(qT[p][:, c:c + 4, :], psTQ[:, :]).then_inc(qk_stored.sem, 1)
                    else:
                        nc.scalar.copy(kT[p][0:HD_F, 0, c:c + 4, :], psTQ[0:HD_F, :])
                        nc.scalar.copy(kT[p][HD_F:P, 1, c:c + 4, :], psTQ[HD_F:P, :]).then_inc(qk_stored.sem, 1)

                def exponent(t, g):
                    n = t * NG + g
                    act.wait_ge(dif_ready.sem, dif_ready.seen(n))
                    act.wait_ge(p_transposed.sem, p_transposed.freed(n))
                    nc.scalar.activation(prob[g % 2][:, :], dif[g % 2][:, :], ACT.Exp).then_inc(exp_ready.sem, 1)

                def store_p(t, g):
                    n = t * NG + g
                    act.wait_ge(p_transposed.sem, p_transposed.seen(n))
                    act.wait_ge(out_ready.sem, out_ready.freed(n))
                    nc.scalar.copy(probT[g % 2][:, :], psTP[:, :]).then_inc(p_stored.sem, 1)

                def store_y(l, sb, i):
                    act.wait_ge(psq_ready.sem, psq_ready.seen(use(l, sb, f"y{i}")))
                    nc.scalar.copy(yT[:, i * BANK:(i + 1) * BANK], bank_of(sb, f"y{i}")[:, :]).then_inc(
                        psq_read.sem, 1)

                def ffn_store_shift(l, sb):
                    act.wait_ge(psq_ready.sem, psq_ready.seen(use(l, sb, "shift")))
                    nc.scalar.copy(xs[:, :, DH:D], bank_of(sb, "shift")[:, 0:HB * DH].rearrange(
                        "p (b e) -> p b e", b=HB)).then_inc(psq_read.sem, 1)

                def ffn_store_xn(l, sb):
                    act.wait_ge(wf_in, (l + 1) * 80)
                    act.wait_ge(psq_ready.sem, psq_ready.seen(use(l, sb, "xh")))
                    nc.scalar.activation(xnT[:, :], bank_of(sb, "xh")[:, :], ACT.Identity,
                                         bias=lng[:, 1:2], scale=lng[:, 0:1]).then_inc(psq_read.sem, 1)

                def ffn_gelu(l, sb):
                    for c in range(3):
                        what = f"gate{c}"
                        act.wait_ge(psq_ready.sem, psq_ready.seen(use(l, sb, what)))
                        nc.scalar.activation(gl[0:FCH[c], c, :], bank_of(sb, what)[0:FCH[c], :], ACT.Gelu,
                                             bias=b1[0:FCH[c], 1, c:c + 1]).then_inc(psq_read.sem, 1)

                act.wait_ge(zeros_ready, 2)

                def slots(l, b, p, sb):
                    half = ffn_half(b)
                    for g in range(NG):
                        off, k = piece_at(g)
                        if there(sb, off):
                            store_raw(l, l * B + b + off, sb, k)
                        off, k = lag(g, 1)
                        if there(sb, off):
                            store_p(l * B + b + off, k)
                        off, k = lag(g, 0)
                        if there(sb, off):
                            exponent(l * B + b + off, k)
                        off, k = piece_at(g, 2)
                        if there(sb, off):
                            store_qk(l * B + b + off, (p + off) % 2, k)
                        if g == 0 and there(sb, 1):
                            store_v(l, sb, (p + 1) % 2, 0)
                        if g == 0 and half is not None:
                            ffn_store_shift(l, sb)
                        if g == 0 and there(sb, 2):
                            store_x(l * B + b + 2, p)
                        if g == 1 and there(sb, -1):
                            store_y(l, sb, 0)
                        if g == 1 and half is not None:
                            ffn_store_xn(l, sb)
                        if g == 2:
                            if there(sb, -1):
                                store_y(l, sb, 1)
                            if there(sb, 1):
                                store_v(l, sb, (p + 1) % 2, 1)
                            if half is not None:
                                ffn_gelu(l, sb)

                pipeline(act, slots)

            @block.vector
            def _(dve):
                def rotation(l):
                    dve.wait_ge(qks_in, (l + 1) * 16)
                    nc.vector.tensor_tensor(rot[:, :, :], rotc[:, :, :], qks[:, :, :], ALU.mult).then_inc(
                        rot_ready.sem, 1)
                    dve.wait_ge(rot_ready.sem, rot_ready.seen(l))

                def guard(t, k):
                    n = t * C4 + k
                    i = k % 2
                    dve.wait_ge(ssq_ready.sem, ssq_ready.seen(n))
                    dve.wait_ge(rn_ready.sem, rn_ready.freed(n))
                    nc.vector.tensor_scalar(ssc[i][:, :], ssq[i][:, :], 1e-24, None, ALU.max).then_inc(
                        ssc_ready.sem, 1)

                def rotate(l, t, sb, k):
                    n = t * C4 + k
                    i, kind = k % 2, k // 2
                    cos, sin = rot[:, kind, 0:HD_F], rot[:, kind, HD_F:]
                    dve.wait_ge(psq_read.sem, psq_read.seen(use(l, sb, f"qk{k}")))
                    dve.wait_ge(sum_ready.sem, sum_ready.freed(n))
                    nc.vector.tensor_tensor(t1[i][:, :, :], raw[i][:, :, :], over(cos, HP), ALU.mult)
                    guard(t, k)
                    nc.vector.tensor_tensor(t2[i][:, :, 0:HALF], raw[i][:, :, HALF:], over(sin[:, 0:HALF], HP),
                                            ALU.mult)
                    nc.vector.tensor_tensor(t2[i][:, :, HALF:], raw[i][:, :, 0:HALF], over(sin[:, HALF:], HP),
                                            ALU.mult).then_inc(rotab_ready.sem, 1)

                def norms(t, k):
                    n = t * C4 + k
                    i = k % 2
                    dve.wait_ge(sq_ready.sem, sq_ready.seen(n))
                    nc.vector.tensor_reduce(ssq[i][:, :], sq[i][:, :, :], AX, ALU.add).then_inc(ssq_ready.sem, 1)

                def scale_qk(t, k):
                    n = t * C4 + k
                    i = k % 2
                    dve.wait_ge(sum_ready.sem, sum_ready.seen(n))
                    dve.wait_ge(rn_ready.sem, rn_ready.seen(n))
                    dve.wait_ge(qk_transposed.sem, qk_transposed.freed(n))
                    nc.vector.tensor_tensor(qn[i][:, :, :], sm[i][:, :, :], along(rn[i][:, :], HD_F),
                                            ALU.mult).then_inc(qn_ready.sem, 1)

                def maxima(t, g):
                    n = t * NG + g
                    i = g % 2
                    s3 = psS[i][:, :].rearrange("p (h m) -> p h m", h=G)
                    dve.wait_ge(scores_ready.sem, scores_ready.seen(n))
                    nc.vector.tensor_reduce(mx[i][:, :], s3, AX, ALU.max).then_inc(max_ready.sem, 1)

                def less_max(t, g):
                    n = t * NG + g
                    i = g % 2
                    s3 = psS[i][:, :].rearrange("p (h m) -> p h m", h=G)
                    dve.wait_ge(exp_ready.sem, exp_ready.freed(n))
                    dve.wait_ge(max_ready.sem, max_ready.seen(n))
                    nc.vector.tensor_tensor(dif[i][:, :].rearrange("p (h m) -> p h m", h=G), s3,
                                            along(mx[i][:, :], S), ALU.subtract).then_inc(dif_ready.sem, 1)

                def row_sums(t, g):
                    n = t * NG + g
                    o3 = psO[:, :].rearrange("p (h e) -> p h e", h=G)
                    dve.wait_ge(out_ready.sem, out_ready.seen(n))
                    nc.vector.reciprocal(rz[:, :], o3[:, :, HD_F]).then_inc(rz_ready.sem, 1)

                def normalise(l, t, g, sb):
                    n = t * NG + g
                    o3 = psO[:, :].rearrange("p (h e) -> p h e", h=G)
                    dve.wait_ge(rz_ready.sem, rz_ready.seen(n))
                    if g == 0 and there(sb, -1):
                        dve.wait_ge(psq_ready.sem, psq_ready.seen(use(l, sb, "y0")))
                    if g == 2 and there(sb, -2):
                        at = before(sb)
                        dve.wait_ge(psq_ready.sem, psq_ready.seen(use(l, at, last_use(at))))
                    nc.vector.tensor_tensor(
                        y[:, g * G * HD_F:(g + 1) * G * HD_F].rearrange("p (h e) -> p h e", h=G),
                        o3[:, :, 0:HD_F], along(rz[:, :], HD_F), ALU.mult).then_inc(y_ready.sem, 1)

                def ffn_stats(l, f, sb):
                    dve.wait_ge(xs0_ready.sem, xs0_ready.seen(f))
                    dve.wait_ge(psq_read.sem, psq_read.seen(use(l, sb, "shift")))
                    for k in range(HB):
                        nc.vector.bn_stats(stats[:, k, :], xs[:, k, :]).then_inc(stats_ready.sem, 1)

                def ffn_moments(f):
                    for k in range(HB):
                        nc.vector.bn_aggr(mv[:, k, :], stats[:, k, :]).then_inc(mv_ready.sem, 1)
                    dve.wait_ge(mv_ready.sem, mv_ready.seen(f * HB + HB - 1))
                    nc.vector.tensor_scalar(ve[:, 0:HB], mv[:, 0:HB, 1], LN_EPS, None,
                                            ALU.add).then_inc(ve_ready.sem, 1)

                def ffn_norm(f):
                    dve.wait_ge(rstd_ready.sem, rstd_ready.seen(f))
                    for k in range(HB):
                        last = nc.vector.tensor_scalar(xh[:, k, :], xs[:, k, :], mv[:, k, 0:1], rstd[:, k:k + 1],
                                                       ALU.subtract, ALU.mult)
                    last.then_inc(xh_ready.sem, 1)

                def ffn_hidden(l, f, sb):
                    dve.wait_ge(wf_in, (l + 1) * 80)
                    for c in range(3):
                        dve.wait_ge(up_ready.sem, up_ready.seen(3 * f + c))
                        dve.wait_ge(psq_read.sem, psq_read.seen(use(l, sb, f"gate{c}")))
                        nc.vector.scalar_tensor_tensor(
                            hT[0:FCH[c], c, :], psO[0:FCH[c], :], b1[0:FCH[c], 0, c:c + 1],
                            gl[0:FCH[c], c, :], ALU.add, ALU.mult).then_inc(h_ready.sem, 1)

                def ffn_add(f, half):
                    dve.wait_ge(b2_added.sem, b2_added.seen(f))
                    dve.wait_ge(down_ready.sem, down_ready.seen(f))
                    xh4 = x[:, half * HB:(half + 1) * HB, :]
                    nc.vector.tensor_tensor(xh4, xh4, psO[:, :].rearrange("p (b e) -> p b e", b=HB),
                                            ALU.add).then_inc(f_added.sem, 1)

                def slots(l, b, p, sb):
                    half = ffn_half(b)
                    f = None if half is None else 2 * l + half
                    for g in range(NG):
                        score_off, sk = lag(g, 0)
                        piece_off, pk = piece_at(g)
                        if g == 1 and half is not None:
                            dve.wait_ge(stats_ready.sem, stats_ready.seen(f * HB + HB - 1))
                        if there(sb, score_off):
                            maxima(l * B + b + score_off, sk)
                        if g == 1 and half is not None:
                            ffn_moments(f)
                        if there(sb, score_off):
                            less_max(l * B + b + score_off, sk)
                        if there(sb, piece_off):
                            if (b + piece_off) % B == 0 and pk == 0:
                                rotation(l + (b + piece_off) // B)
                            norms(l * B + b + piece_off, pk)
                            rotate(l, l * B + b + piece_off, sb, pk)
                        off, k = lag(g, 2)
                        if there(sb, off):
                            row_sums(l * B + b + off, k)
                            normalise(l, l * B + b + off, k, sb)
                        off, k = piece_at(g, 1)
                        if there(sb, off):
                            scale_qk(l * B + b + off, k)
                        if half is not None:
                            if g == 0:
                                ffn_stats(l, f, sb)
                            if g == 1:
                                ffn_norm(f)
                            if g == 2:
                                ffn_hidden(l, f, sb)
                    if there(sb, -1):
                        t = l * B + b - 1
                        dve.wait_ge(o_ready.sem, o_ready.seen(t))
                        xb = x[:, (b - 1) % B, :]
                        nc.vector.tensor_tensor(xb, xb, psY[:, 0:D], ALU.add).then_inc(added.sem, 1)
                    if half is not None:
                        ffn_add(f, half)

                pipeline(dve, slots)

        with nc.Block() as block:
            @block.vector
            def _(dve):
                nc.vector.tensor_tensor(x[:, :, :], x[:, :, :], x0[:, :, :], ALU.add)


def store_stage(nc, glob, out):
    st = Stage(nc, "store")
    with st.ctx:
        stored = st.sem("out_stored")
        with nc.Block() as block:
            @block.sync
            def _(sp):
                sp.dma_start(out.rearrange("b p d -> p b d"), glob["x"][:, :, :]).then_inc(stored, 16)
                sp.wait_ge(stored, 16)


STAGES = [taylor_stage, diff_stage, expert_stage, rope_stage, cross_stage, local_stage]


def decoder(nc, dram, out):
    st = Stage(nc, "all")
    with st.ctx:
        glob = {"x": st.sb("x", [P, B, D]), "ident": st.sb("ident", [P, P]),
                "ctxT": st.sb("ctxT", [P, B, S]), "mhalf": st.sb("mhalf", [P, BANK // 4])}
        load_stage(nc, glob, dram)
        for stage in STAGES:
            stage(nc, glob, dram)
        store_stage(nc, glob, out)


def _tables():
    t = {}
    t["c_ident"] = np.eye(P, dtype=np.float32)
    n = np.arange(P)
    t["c_experts"] = np.arange(E_EXP, dtype=np.float32)
    inv = 1.0 / 10000.0 ** (np.arange(0, HD_S, 2, dtype=np.float32) / np.float32(HD_S))
    f = n[:, None].astype(np.float32) * inv[None, :].astype(np.float32)
    t["c_rope8_cos"] = np.concatenate([np.cos(f)] * 2, 1).astype(np.float32)
    t["c_rope8_sin"] = np.concatenate([-np.sin(f), np.sin(f)], 1).astype(np.float32)
    half = np.arange(0, HD_F, 2, dtype=np.float64)
    f = n[:, None] * (1.0 / 10000.0 ** (half / HD_F))[None, :]
    power = (n - P // 2) / (WINDOW // 2)
    scale = ((half + 0.4 * HD_F) / (1.4 * HD_F))[None, :] ** power[:, None]
    rot = np.concatenate([np.cos(f), np.cos(f), -np.sin(f), np.sin(f)], 1)
    scale = np.concatenate([scale] * 4, 1)
    t["c_rot"] = np.stack([rot * scale * QK_SCALE, rot / scale], 1).astype(np.float32)
    t["c_shift"] = np.eye(P, k=1, dtype=np.float32)
    seen = (n[None, :] <= n[:, None]) & (n[None, :] >= n[:, None] - WINDOW)
    t["c_band"] = np.where(seen, 0.0, MASKED).astype(np.float32)
    t["c_own_rows8"] = (n[:, None] // HD_S == np.arange(H)[None, :]).astype(np.float32)
    t["c_own_rows16"] = (n[:, None] // HD_A == np.arange(P // HD_A)[None, :]).astype(np.float32)
    t["c_causalT"] = (n[:, None] <= n[None, :]).astype(np.float32)
    return t


def _arrays(inputs):
    a = {k: np.ascontiguousarray(v) for k, v in inputs.items()}
    for n in ("wq1", "wk1", "wq2", "wk2", "wv"):
        full = np.zeros((H, HD_S, H, HD_S), np.float32)
        w = a["L0_xattn_" + n]
        for h in range(H):
            full[h, :, h, :] = w[h].T
        full = full.reshape(D, D)
        a["L0_xattn_" + n] = full
    for n in ("L0_xattn_wo", "L1_attn_w_qkv", "L1_attn_w_out", *("L1_xattn_" + m for m in (
            "Wq_c", "Wk_s", "Wv_s", "Wq_s", "Wk_c", "Wv_c", "Wg"))):
        a[n] = a[n].T
    w = a["L1_ffn_Wqkv"].reshape(DEPTH, D, 3, 2, 8, HD_F).copy()
    qk = w[:, :, 0:2].transpose(0, 1, 2, 4, 3, 5).reshape(DEPTH, D, 2 * INNER)
    a["L1_ffn_Wqkv"] = np.concatenate([qk, w[:, :, 2].reshape(DEPTH, D, INNER)], 2)
    a["qk_scale"] = np.concatenate([a[f"L1_ffn_{n}_scale"].reshape(DEPTH, 2, 32)[:, o, :].reshape(DEPTH, HD_F)
                                    for n in "qk" for o in ([0, 1], [1, 0])], 1)
    del a["L1_ffn_q_scale"], a["L1_ffn_k_scale"]
    a["ln_gb"] = np.stack([a.pop("L1_ffn_ln_g"), a.pop("L1_ffn_ln_b")], 2)
    rows = 3 * P - DI
    a["L1_ffn_W2"] = np.pad(a["L1_ffn_W2"], ((0, 0), (0, rows), (0, 0)))
    a["L1_ffn_b1"] = np.pad(a["L1_ffn_b1"].reshape(DEPTH, 2, DI), ((0, 0), (0, 0), (0, rows))).reshape(
        DEPTH, 6, P).transpose(0, 2, 1)
    a.update(_tables())
    a.pop("L0_ffn_scores")
    return {k: np.ascontiguousarray(v if v.ndim else v.reshape(1)) for k, v in a.items()}


def kernel(**inputs):
    import concourse.bacc as _bacc
    from concourse.bass_utils import run_bass_kernel_spmd as _run

    nc = _bacc.Bacc("TRN2", target_bir_lowering=False, num_devices=1)
    arrays = {f"in_{k}": v for k, v in _arrays(inputs).items()}
    dram = {k[3:]: nc.dram_tensor(k, v.shape, mybir.dt.from_np(v.dtype), kind="ExternalInput").ap()
            for k, v in arrays.items()}
    out = nc.dram_tensor("out_x", (B, S, D), F32, kind="ExternalOutput").ap()
    decoder(nc, dram, out)
    return _run(nc, [arrays], core_ids=[0]).results[0]["out_x"]
```
